# Optimizing a Trainium2 kernel written in Bass

```python
import numpy as np
import jax
import jax.numpy as jnp

def _softmax(x, axis=-1):
    return jax.nn.softmax(x, axis=axis)

def _gelu(x):
    return jax.nn.gelu(x, approximate=True)

def _silu(x):
    return jax.nn.silu(x)

def _sigmoid(x):
    return jax.nn.sigmoid(x)

def _layernorm(x, axis=-1, eps=1e-05):
    m = jnp.mean(x, axis=axis, keepdims=True)
    v = jnp.var(x, axis=axis, keepdims=True)
    return (x - m) / jnp.sqrt(v + eps)

def _scatter_add(tgt, idx, src, axis=0):
    return tgt.at[idx].add(src)

def _segment_sum(src, seg, n):
    return jax.ops.segment_sum(src, seg, n)
kernel_name = 'mk_xattn_ffn_d4_seqx_r8_612d60'

def setup_inputs(seed: int=0):
    np.random.seed(seed)
    _w = jnp.asarray

    def _rec_inputs():
        import jax
        import jax.numpy as jnp
        _rk = jax.random.key(seed)
        x = -0.0002928 + 1 * jax.random.normal(jax.random.fold_in(_rk, 1), (8, 128, 128), jnp.float32)
        _lenS = 128 - jax.random.randint(jax.random.fold_in(_rk, 7), (8,), 0, max(1, 128 // 4) + 1, jnp.int32)
        _lenS2 = 128 - jax.random.randint(jax.random.fold_in(_rk, 8), (8,), 0, max(1, 128 // 4) + 1, jnp.int32)
        _ctx_1024P = jax.random.normal(jax.random.fold_in(_rk, 11), (8, 16, 128), jnp.float32)
        _ctx_1024c = jax.random.dirichlet(jax.random.fold_in(_rk, 511), 0.3 * jnp.ones((16,), jnp.float32), (8, 128))
        _ctx_1024t = jnp.einsum('bsk,bkd->bsd', _ctx_1024c, _ctx_1024P)
        _ctx_1024t = _ctx_1024t * jax.lax.rsqrt(jnp.mean(jnp.square(_ctx_1024t)) + 1e-12) * 0.953939
        ctx_1024 = -1.39393e-06 + 0.999914 * (_ctx_1024t + 0.3 * jax.random.normal(jax.random.fold_in(_rk, 611), (8, 128, 128), jnp.float32))
        return (x, ctx_1024)
    x, ctx_1024 = _rec_inputs()

    def _L0_xattn_setup():
        import jax, jax.numpy as jnp
        import numpy as np
        B, T, D, H = (2, 256, 128, 16)
        DH = D // H
        key = jax.random.key(seed)
        ks = jax.random.split(key, 11)
        s = 1.0 / np.sqrt(D)
        return {'q': jax.random.normal(ks[0], (B, T, D), jnp.float32), 'k': jax.random.normal(ks[1], (B, T, D), jnp.float32), 'v': jax.random.normal(ks[2], (B, T, D), jnp.float32), 'wq_w': jax.random.normal(ks[3], (D, D), jnp.float32) * s, 'wq_b': jnp.zeros((D,), jnp.float32), 'wk_w': jax.random.normal(ks[4], (D, D), jnp.float32) * s, 'wk_b': jnp.zeros((D,), jnp.float32), 'wv_w': jax.random.normal(ks[5], (D, D), jnp.float32) * s, 'wv_b': jnp.zeros((D,), jnp.float32), 'wo_w': jax.random.normal(ks[6], (D, D), jnp.float32) * s, 'wo_b': jnp.zeros((D,), jnp.float32)}
    _L0_xattn_all = _L0_xattn_setup()
    _L0_xattn_in = {k: v for k, v in _L0_xattn_all.items() if k in ('wq_w', 'wq_b', 'wk_w', 'wk_b', 'wv_w', 'wv_b', 'wo_w', 'wo_b')}
    del _L0_xattn_all

    def _L0_ffn_setup():
        import jax, jax.numpy as jnp
        import numpy as np
        E, K, D, F = (8, 2, 128, 512)
        EPS = 1e-06
        B, S = (2, 128)
        key = jax.random.key(seed)
        ks = jax.random.split(key, 6)
        s_in = 1.0 / np.sqrt(D)
        s_mid = 1.0 / np.sqrt(F)
        return {'x': jax.random.normal(ks[0], (B, S, D), dtype=jnp.float32), 'Wg': jax.random.normal(ks[1], (D, E), dtype=jnp.float32) * s_in, 'gamma': jnp.ones((E, D), dtype=jnp.float32), 'beta': jnp.zeros((E, D), dtype=jnp.float32), 'W1': jax.random.normal(ks[2], (E, D, F), dtype=jnp.float32) * s_in, 'b1': jnp.zeros((E, F), dtype=jnp.float32), 'W2': jax.random.normal(ks[3], (E, F, D), dtype=jnp.float32) * s_mid, 'b2': jnp.zeros((E, D), dtype=jnp.float32)}
    _L0_ffn_all = _L0_ffn_setup()
    _L0_ffn_in = {k: v for k, v in _L0_ffn_all.items() if k in ('Wg', 'gamma', 'beta', 'W1', 'b1', 'W2', 'b2')}
    del _L0_ffn_all

    def _L1_xattn_setup():
        import jax, jax.numpy as jnp
        import numpy as np
        B, M, S, P, H, F = (4, 64, 512, 128, 16, 512)

        def _layernorm(x, g, b, eps=1e-06):
            mu = jnp.mean(x, axis=-1, keepdims=True)
            var = jnp.var(x, axis=-1, keepdims=True)
            return (x - mu) / jnp.sqrt(var + eps) * g + b
        key = jax.random.key(seed)
        ks = jax.random.split(key, 12)
        w = lambda k, shape: jax.random.normal(k, shape, jnp.float32) * 0.02
        return {'state_seq': jax.random.normal(ks[0], (B, M, P), jnp.float32), 'input_seq': jax.random.normal(ks[1], (B, S, P), jnp.float32), 'Wk': w(ks[2], (P, P)), 'bk': jnp.zeros((P,), jnp.float32), 'Wv': w(ks[3], (P, P)), 'bv': jnp.zeros((P,), jnp.float32), 'Wq': w(ks[4], (H, P, P)), 'bq': jnp.zeros((H, P), jnp.float32), 'Wo': w(ks[5], (H * P, P)), 'bo': jnp.zeros((P,), jnp.float32), 'Wg': w(ks[6], (P, F)), 'bg': jnp.zeros((F,), jnp.float32), 'Wl': w(ks[7], (P, F)), 'bl': jnp.zeros((F,), jnp.float32), 'Wm': w(ks[8], (F, P)), 'bm': jnp.zeros((P,), jnp.float32), 'g1': jnp.ones((P,), jnp.float32), 'b1': jnp.zeros((P,), jnp.float32), 'g2': jnp.ones((P,), jnp.float32), 'b2': jnp.zeros((P,), jnp.float32)}
    _L1_xattn_all = _L1_xattn_setup()
    _L1_xattn_in = {k: v for k, v in _L1_xattn_all.items() if k in ('Wk', 'bk', 'Wv', 'bv', 'Wq', 'bq', 'Wo', 'bo', 'Wg', 'bg', 'Wl', 'bl', 'Wm', 'bm', 'g1', 'b1', 'g2', 'b2')}
    del _L1_xattn_all

    def _L1_ffn_setup():
        import jax, jax.numpy as jnp
        import numpy as np
        D_MODEL, EXPERT_DIM, NUM_EXPERTS, TOP_K = (128, 256, 16, 2)
        SEQ_LEN, BATCH = (256, 2)
        key = jax.random.key(seed)
        ks = jax.random.split(key, 8)
        s_d = 1.0 / np.sqrt(D_MODEL)
        s_h = 1.0 / np.sqrt(EXPERT_DIM)
        return {'x': jax.random.normal(ks[0], (SEQ_LEN, BATCH, D_MODEL), jnp.float32), 'Wg': jax.random.uniform(ks[1], (D_MODEL, NUM_EXPERTS), jnp.float32, -s_d, s_d), 'bg': jax.random.uniform(ks[2], (NUM_EXPERTS,), jnp.float32, -s_d, s_d), 'bias': jnp.zeros((NUM_EXPERTS,), jnp.float32), 'W1': jax.random.uniform(ks[3], (NUM_EXPERTS, D_MODEL, EXPERT_DIM), jnp.float32, -s_d, s_d), 'b1': jax.random.uniform(ks[4], (NUM_EXPERTS, EXPERT_DIM), jnp.float32, -s_d, s_d), 'W2': jax.random.uniform(ks[5], (NUM_EXPERTS, EXPERT_DIM, D_MODEL), jnp.float32, -s_h, s_h), 'b2': jax.random.uniform(ks[6], (NUM_EXPERTS, D_MODEL), jnp.float32, -s_h, s_h)}
    _L1_ffn_all = _L1_ffn_setup()
    _L1_ffn_in = {k: v for k, v in _L1_ffn_all.items() if k in ('Wg', 'bg', 'bias', 'W1', 'b1', 'W2', 'b2')}
    del _L1_ffn_all

    def _L2_xattn_setup():
        import jax, jax.numpy as jnp
        import numpy as np
        import math
        HEADS = 16
        D_MODEL = 128
        D_K = D_MODEL // HEADS
        PRUNE_KEEP = 0.9

        def _split_heads(x, B):
            return x.reshape(B, -1, HEADS, D_K).transpose(0, 2, 1, 3)

        def _pruned_attention(q, k, v):
            B, H, S, _ = q.shape
            scores = jnp.einsum('bhqd,bhkd->bhqk', q, k) / math.sqrt(D_K)
            scores = jax.nn.softmax(scores, axis=-1)
            keep = int(S * PRUNE_KEEP)
            col_sum = jnp.sum(scores, axis=2)
            _, idx = jax.lax.top_k(col_sum, keep)
            mask = jnp.zeros((B, H, S), scores.dtype).at[jnp.arange(B)[:, None, None], jnp.arange(H)[None, :, None], idx].set(1.0)
            pruned = scores * mask[:, :, None, :]
            return jnp.einsum('bhqk,bhkd->bhqd', pruned, v)
        key = jax.random.key(seed)
        ks = jax.random.split(key, 12)
        B, S = (2, 256)
        sc = 0.02
        return {'q': jax.random.normal(ks[0], (B, S, D_MODEL), jnp.float32), 'k': jax.random.normal(ks[1], (B, S, D_MODEL), jnp.float32), 'v': jax.random.normal(ks[2], (B, S, D_MODEL), jnp.float32), 'Wq': jax.random.normal(ks[3], (D_MODEL, D_MODEL), jnp.float32) * sc, 'bq': jnp.zeros((D_MODEL,), jnp.float32), 'Wk': jax.random.normal(ks[4], (D_MODEL, D_MODEL), jnp.float32) * sc, 'bk': jnp.zeros((D_MODEL,), jnp.float32), 'Wv': jax.random.normal(ks[5], (D_MODEL, D_MODEL), jnp.float32) * sc, 'bv': jnp.zeros((D_MODEL,), jnp.float32), 'Wo': jax.random.normal(ks[6], (D_MODEL, D_MODEL), jnp.float32) * sc, 'bo': jnp.zeros((D_MODEL,), jnp.float32)}
    _L2_xattn_all = _L2_xattn_setup()
    _L2_xattn_in = {k: v for k, v in _L2_xattn_all.items() if k in ('Wq', 'bq', 'Wk', 'bk', 'Wv', 'bv', 'Wo', 'bo')}
    del _L2_xattn_all

    def _L2_ffn_setup():
        import jax, jax.numpy as jnp
        import numpy as np
        D_MODEL = 128
        D_FF = 512
        N_EXPERTS = 8
        TOP_K = 2
        B, T = (4, 256)
        key = jax.random.key(seed)
        ks = jax.random.split(key, 5)
        x = jax.random.normal(ks[0], (B, T, D_MODEL), dtype=jnp.float32)

        def lin(k, shape, fan_in):
            return jax.random.normal(k, shape, dtype=jnp.float32) / np.float32(np.sqrt(fan_in))
        return {'x': x, 'router_w': lin(ks[1], (N_EXPERTS, D_MODEL), D_MODEL), 'w_gate': lin(ks[2], (N_EXPERTS, D_MODEL, D_FF), D_MODEL), 'w_up': lin(ks[3], (N_EXPERTS, D_MODEL, D_FF), D_MODEL), 'w_down': lin(ks[4], (N_EXPERTS, D_FF, D_MODEL), D_FF)}
    _L2_ffn_all = _L2_ffn_setup()
    _L2_ffn_in = {k: v for k, v in _L2_ffn_all.items() if k in ('router_w', 'w_gate', 'w_up', 'w_down')}
    del _L2_ffn_all

    def _L3_xattn_setup():
        import jax, jax.numpy as jnp
        import numpy as np
        B, L_ENC, L_DEC, D = (16, 64, 128, 128)
        key = jax.random.key(seed)
        k1, k2, k3, k4, k5, k6 = jax.random.split(key, 6)
        encoder_hc = jax.random.normal(k1, (B, L_ENC, D), dtype=jnp.float32)
        decoder_hq = jax.random.normal(k2, (B, L_DEC, D), dtype=jnp.float32)
        w_sim = jax.random.normal(k3, (3 * D,), dtype=jnp.float32) * 0.02
        b_sim = jax.random.normal(k4, (1,), dtype=jnp.float32) * 0.02
        W_qv = jax.random.normal(k5, (4 * D, D), dtype=jnp.float32) * 0.02
        b_qv = jax.random.normal(k6, (D,), dtype=jnp.float32) * 0.02
        return {'encoder_hc': encoder_hc, 'decoder_hq': decoder_hq, 'w_sim': w_sim, 'b_sim': b_sim, 'W_qv': W_qv, 'b_qv': b_qv}
    _L3_xattn_all = _L3_xattn_setup()
    _L3_xattn_in = {k: v for k, v in _L3_xattn_all.items() if k in ('w_sim', 'b_sim', 'W_qv', 'b_qv')}
    del _L3_xattn_all

    def _L3_ffn_setup():
        import jax, jax.numpy as jnp
        import numpy as np
        B, S, D, F, E = (2, 256, 128, 512, 8)
        LN_EPS = 1e-05

        def _xavier(key, shape, fan_in, fan_out):
            a = np.sqrt(6.0 / (fan_in + fan_out))
            return jax.random.uniform(key, shape, jnp.float32, -a, a)
        key = jax.random.key(seed)
        ks = jax.random.split(key, 8)
        tgt = jax.random.normal(ks[0], (B, S, D), jnp.float32)
        router_w = _xavier(ks[1], (E, D), D, E)
        router_b = jnp.zeros((E,), jnp.float32)
        w1 = _xavier(ks[2], (E, D, F), D, F)
        b1 = jnp.zeros((E, F), jnp.float32)
        w2 = _xavier(ks[3], (E, F, D), F, D)
        b2 = jnp.zeros((E, D), jnp.float32)
        gamma = jnp.ones((D,), jnp.float32)
        beta = jnp.zeros((D,), jnp.float32)
        return {'tgt': tgt, 'router_w': router_w, 'router_b': router_b, 'w1': w1, 'b1': b1, 'w2': w2, 'b2': b2, 'gamma': gamma, 'beta': beta}
    _L3_ffn_all = _L3_ffn_setup()
    _L3_ffn_in = {k: v for k, v in _L3_ffn_all.items() if k in ('router_w', 'router_b', 'w1', 'b1', 'w2', 'b2', 'gamma', 'beta')}
    del _L3_ffn_all
    return {'x': x, 'ctx_1024': ctx_1024, 'L0_xattn_wq_w': _L0_xattn_in['wq_w'], 'L0_xattn_wq_b': _L0_xattn_in['wq_b'], 'L0_xattn_wk_w': _L0_xattn_in['wk_w'], 'L0_xattn_wk_b': _L0_xattn_in['wk_b'], 'L0_xattn_wv_w': _L0_xattn_in['wv_w'], 'L0_xattn_wv_b': _L0_xattn_in['wv_b'], 'L0_xattn_wo_w': _L0_xattn_in['wo_w'], 'L0_xattn_wo_b': _L0_xattn_in['wo_b'], 'L0_ffn_Wg': _L0_ffn_in['Wg'], 'L0_ffn_gamma': _L0_ffn_in['gamma'], 'L0_ffn_beta': _L0_ffn_in['beta'], 'L0_ffn_W1': _L0_ffn_in['W1'], 'L0_ffn_b1': _L0_ffn_in['b1'], 'L0_ffn_W2': _L0_ffn_in['W2'], 'L0_ffn_b2': _L0_ffn_in['b2'], 'L1_xattn_Wk': _L1_xattn_in['Wk'], 'L1_xattn_bk': _L1_xattn_in['bk'], 'L1_xattn_Wv': _L1_xattn_in['Wv'], 'L1_xattn_bv': _L1_xattn_in['bv'], 'L1_xattn_Wq': _L1_xattn_in['Wq'], 'L1_xattn_bq': _L1_xattn_in['bq'], 'L1_xattn_Wo': _L1_xattn_in['Wo'], 'L1_xattn_bo': _L1_xattn_in['bo'], 'L1_xattn_Wg': _L1_xattn_in['Wg'], 'L1_xattn_bg': _L1_xattn_in['bg'], 'L1_xattn_Wl': _L1_xattn_in['Wl'], 'L1_xattn_bl': _L1_xattn_in['bl'], 'L1_xattn_Wm': _L1_xattn_in['Wm'], 'L1_xattn_bm': _L1_xattn_in['bm'], 'L1_xattn_g1': _L1_xattn_in['g1'], 'L1_xattn_b1': _L1_xattn_in['b1'], 'L1_xattn_g2': _L1_xattn_in['g2'], 'L1_xattn_b2': _L1_xattn_in['b2'], 'L1_ffn_Wg': _L1_ffn_in['Wg'], 'L1_ffn_bg': _L1_ffn_in['bg'], 'L1_ffn_bias': _L1_ffn_in['bias'], 'L1_ffn_W1': _L1_ffn_in['W1'], 'L1_ffn_b1': _L1_ffn_in['b1'], 'L1_ffn_W2': _L1_ffn_in['W2'], 'L1_ffn_b2': _L1_ffn_in['b2'], 'L2_xattn_Wq': _L2_xattn_in['Wq'], 'L2_xattn_bq': _L2_xattn_in['bq'], 'L2_xattn_Wk': _L2_xattn_in['Wk'], 'L2_xattn_bk': _L2_xattn_in['bk'], 'L2_xattn_Wv': _L2_xattn_in['Wv'], 'L2_xattn_bv': _L2_xattn_in['bv'], 'L2_xattn_Wo': _L2_xattn_in['Wo'], 'L2_xattn_bo': _L2_xattn_in['bo'], 'L2_ffn_router_w': _L2_ffn_in['router_w'], 'L2_ffn_w_gate': _L2_ffn_in['w_gate'], 'L2_ffn_w_up': _L2_ffn_in['w_up'], 'L2_ffn_w_down': _L2_ffn_in['w_down'], 'L3_xattn_w_sim': _L3_xattn_in['w_sim'], 'L3_xattn_b_sim': _L3_xattn_in['b_sim'], 'L3_xattn_W_qv': _L3_xattn_in['W_qv'], 'L3_xattn_b_qv': _L3_xattn_in['b_qv'], 'L3_ffn_router_w': _L3_ffn_in['router_w'], 'L3_ffn_router_b': _L3_ffn_in['router_b'], 'L3_ffn_w1': _L3_ffn_in['w1'], 'L3_ffn_b1': _L3_ffn_in['b1'], 'L3_ffn_w2': _L3_ffn_in['w2'], 'L3_ffn_b2': _L3_ffn_in['b2'], 'L3_ffn_gamma': _L3_ffn_in['gamma'], 'L3_ffn_beta': _L3_ffn_in['beta']}

def reference(x, ctx_1024, L0_xattn_wq_w, L0_xattn_wq_b, L0_xattn_wk_w, L0_xattn_wk_b, L0_xattn_wv_w, L0_xattn_wv_b, L0_xattn_wo_w, L0_xattn_wo_b, L0_ffn_Wg, L0_ffn_gamma, L0_ffn_beta, L0_ffn_W1, L0_ffn_b1, L0_ffn_W2, L0_ffn_b2, L1_xattn_Wk, L1_xattn_bk, L1_xattn_Wv, L1_xattn_bv, L1_xattn_Wq, L1_xattn_bq, L1_xattn_Wo, L1_xattn_bo, L1_xattn_Wg, L1_xattn_bg, L1_xattn_Wl, L1_xattn_bl, L1_xattn_Wm, L1_xattn_bm, L1_xattn_g1, L1_xattn_b1, L1_xattn_g2, L1_xattn_b2, L1_ffn_Wg, L1_ffn_bg, L1_ffn_bias, L1_ffn_W1, L1_ffn_b1, L1_ffn_W2, L1_ffn_b2, L2_xattn_Wq, L2_xattn_bq, L2_xattn_Wk, L2_xattn_bk, L2_xattn_Wv, L2_xattn_bv, L2_xattn_Wo, L2_xattn_bo, L2_ffn_router_w, L2_ffn_w_gate, L2_ffn_w_up, L2_ffn_w_down, L3_xattn_w_sim, L3_xattn_b_sim, L3_xattn_W_qv, L3_xattn_b_qv, L3_ffn_router_w, L3_ffn_router_b, L3_ffn_w1, L3_ffn_b1, L3_ffn_w2, L3_ffn_b2, L3_ffn_gamma, L3_ffn_beta):
    import jax
    import jax.numpy as jnp

    def _L0_xattn_ref(q, k, v, wq_w, wq_b, wk_w, wk_b, wv_w, wv_b, wo_w, wo_b):
        import jax, jax.numpy as jnp
        import numpy as np
        B, T, D, H = (2, 256, 128, 16)
        DH = D // H
        b, t, d = q.shape
        wq = (q @ wq_w.T + wq_b).reshape(b, t, H, DH)
        wk = (k @ wk_w.T + wk_b).reshape(b, t, H, DH)
        wv = (v @ wv_w.T + wv_b).reshape(b, t, H, DH)
        scores = jnp.einsum('bthd,bshd->bhts', wq, wk) / jnp.sqrt(jnp.float32(DH))
        probs = jax.nn.softmax(scores, axis=-1)
        attn = jnp.einsum('bhts,bshd->bthd', probs, wv)
        attn = attn.reshape(b, t, d)
        return attn @ wo_w.T + wo_b

    def _L0_ffn_ref(x, Wg, gamma, beta, W1, b1, W2, b2):
        import jax, jax.numpy as jnp
        import numpy as np
        E, K, D, F = (8, 2, 128, 512)
        EPS = 1e-06
        B, S = (2, 128)
        orig_shape = x.shape
        xf = x.reshape(-1, orig_shape[-1])
        scores = xf @ Wg
        w, idx = jax.lax.top_k(scores, K)
        w = jax.nn.softmax(w, axis=-1)
        mu = jnp.mean(xf, axis=-1, keepdims=True)
        var = jnp.var(xf, axis=-1, keepdims=True)
        xhat = (xf - mu) * jax.lax.rsqrt(var + EPS)
        normed = xhat[None, :, :] * gamma[:, None, :] + beta[:, None, :]
        h = jax.nn.relu(jnp.einsum('end,edf->enf', normed, W1) + b1[:, None, :])
        out = jnp.einsum('enf,efd->end', h, W2) + b2[:, None, :] + xf[None, :, :]
        cw = jnp.sum(w[..., None] * jax.nn.one_hot(idx, E, dtype=w.dtype), axis=1)
        y = jnp.einsum('ne,end->nd', cw, out)
        return y.reshape(orig_shape)

    def _L1_xattn_ref(state_seq, input_seq, Wk, bk, Wv, bv, Wq, bq, Wo, bo, Wg, bg, Wl, bl, Wm, bm, g1, b1, g2, b2):
        import jax, jax.numpy as jnp
        import numpy as np
        B, M, S, P, H, F = (4, 64, 512, 128, 16, 512)

        def _layernorm(x, g, b, eps=1e-06):
            mu = jnp.mean(x, axis=-1, keepdims=True)
            var = jnp.var(x, axis=-1, keepdims=True)
            return (x - mu) / jnp.sqrt(var + eps) * g + b
        b_, m_, p_ = state_seq.shape
        h_ = Wq.shape[0]
        ik = input_seq @ Wk + bk
        mk = state_seq @ Wk + bk
        iv = input_seq @ Wv + bv
        mv = state_seq @ Wv + bv
        q = jnp.einsum('bmd,hdp->bhmp', state_seq, Wq) + bq[None, :, None, :]
        inp_score = jnp.einsum('bhmp,bsp->bhms', q, ik)
        self_score = jnp.sum(q * mk[:, None], axis=-1, keepdims=True)
        score = jnp.concatenate([self_score, inp_score], axis=-1)
        score = score / jnp.sqrt(jnp.asarray(p_, jnp.float32))
        attn = jax.nn.softmax(score, axis=-1)
        v_in = jnp.einsum('bhms,bsp->bhmp', attn[..., 1:], iv)
        v_self = attn[..., 0:1] * mv[:, None]
        heads = (v_in + v_self).transpose(0, 2, 1, 3).reshape(b_, m_, h_ * p_)
        attn_out = heads @ Wo + bo
        x1 = _layernorm(attn_out + state_seq, g1, b1)
        mlp = jax.nn.relu(x1 @ Wg + bg) * (x1 @ Wl + bl) @ Wm + bm
        return _layernorm(mlp + x1, g2, b2)

    def _L1_ffn_ref(x, Wg, bg, bias, W1, b1, W2, b2):
        import jax, jax.numpy as jnp
        import numpy as np
        D_MODEL, EXPERT_DIM, NUM_EXPERTS, TOP_K = (128, 256, 16, 2)
        SEQ_LEN, BATCH = (256, 2)
        logits = jnp.einsum('sbd,de->sbe', x, Wg) + bg + bias
        vals, idx = jax.lax.top_k(logits, TOP_K)
        w = jax.nn.softmax(vals - jnp.max(vals, axis=-1, keepdims=True), axis=-1)
        cw = jnp.einsum('sbk,sbke->sbe', w, jax.nn.one_hot(idx, NUM_EXPERTS, dtype=x.dtype))
        h = jax.nn.relu(jnp.einsum('sbd,edh->esbh', x, W1) + b1[:, None, None, :])
        y = jnp.einsum('esbh,ehd->esbd', h, W2) + b2[:, None, None, :]
        out = jnp.einsum('esbd,sbe->sbd', y, cw)
        return out

    def _L2_xattn_ref(q, k, v, Wq, bq, Wk, bk, Wv, bv, Wo, bo):
        import jax, jax.numpy as jnp
        import numpy as np
        import math
        HEADS = 16
        D_MODEL = 128
        D_K = D_MODEL // HEADS
        PRUNE_KEEP = 0.9

        def _split_heads(x, B):
            return x.reshape(B, -1, HEADS, D_K).transpose(0, 2, 1, 3)

        def _pruned_attention(q, k, v):
            B, H, S, _ = q.shape
            scores = jnp.einsum('bhqd,bhkd->bhqk', q, k) / math.sqrt(D_K)
            scores = jax.nn.softmax(scores, axis=-1)
            keep = int(S * PRUNE_KEEP)
            col_sum = jnp.sum(scores, axis=2)
            _, idx = jax.lax.top_k(col_sum, keep)
            mask = jnp.zeros((B, H, S), scores.dtype).at[jnp.arange(B)[:, None, None], jnp.arange(H)[None, :, None], idx].set(1.0)
            pruned = scores * mask[:, :, None, :]
            return jnp.einsum('bhqk,bhkd->bhqd', pruned, v)
        B = q.shape[0]
        qh = _split_heads(q @ Wq.T + bq, B)
        kh = _split_heads(k @ Wk.T + bk, B)
        vh = _split_heads(v @ Wv.T + bv, B)
        out = _pruned_attention(qh, kh, vh)
        concat = out.transpose(0, 2, 1, 3).reshape(B, -1, D_MODEL)
        return concat @ Wo.T + bo

    def _L2_ffn_ref(x, router_w, w_gate, w_up, w_down):
        import jax, jax.numpy as jnp
        import numpy as np
        D_MODEL = 128
        D_FF = 512
        N_EXPERTS = 8
        TOP_K = 2
        B, T = (4, 256)
        Bx, Tx, D = x.shape
        xf = x.reshape(-1, D)
        logits = xf @ router_w.T
        scores = jax.nn.softmax(logits, axis=-1)
        topk_scores, topk_ids = jax.lax.top_k(scores, TOP_K)
        topk_scores = topk_scores / topk_scores.sum(-1, keepdims=True)
        cw = (jax.nn.one_hot(topk_ids, N_EXPERTS, dtype=xf.dtype) * topk_scores[..., None]).sum(1)

        def body(acc, inputs):
            wg, wu, wd, w = inputs
            h = jax.nn.silu(xf @ wg) * (xf @ wu)
            acc = acc + w[:, None] * (h @ wd)
            return (acc, None)
        out, _ = jax.lax.scan(body, jnp.zeros_like(xf), (w_gate, w_up, w_down, cw.T))
        return out.reshape(Bx, Tx, D)

    def _L3_xattn_ref(encoder_hc, decoder_hq, w_sim, b_sim, W_qv, b_qv):
        import jax, jax.numpy as jnp
        import numpy as np
        B, L_ENC, L_DEC, D = (16, 64, 128, 128)
        d = encoder_hc.shape[-1]
        w1, w2, w3 = (w_sim[:d], w_sim[d:2 * d], w_sim[2 * d:])
        Sim = (encoder_hc @ w1)[:, :, None] + (decoder_hq @ w2)[:, None, :] + jnp.einsum('bid,bjd->bij', encoder_hc * w3, decoder_hq) + b_sim[0]
        A = jax.nn.softmax(Sim, axis=2)
        hq_hat = jnp.einsum('bij,bjd->bid', A, decoder_hq)
        Batt = jax.nn.softmax(jnp.max(Sim, axis=2), axis=1)
        hc_bar = jnp.einsum('bi,bid->bd', Batt, encoder_hc)[:, None, :]
        hc_hat = jnp.broadcast_to(hc_bar, encoder_hc.shape)
        feats = jnp.concatenate([encoder_hc, hq_hat, encoder_hc * hq_hat, encoder_hc * hc_hat], axis=-1)
        hcq = feats @ W_qv + b_qv
        return hcq

    def _L3_ffn_ref(tgt, router_w, router_b, w1, b1, w2, b2, gamma, beta):
        import jax, jax.numpy as jnp
        import numpy as np
        B, S, D, F, E = (2, 256, 128, 512, 8)
        LN_EPS = 1e-05

        def _xavier(key, shape, fan_in, fan_out):
            a = np.sqrt(6.0 / (fan_in + fan_out))
            return jax.random.uniform(key, shape, jnp.float32, -a, a)
        logits = jnp.einsum('bsd,ed->bse', tgt, router_w) + router_b
        rw = jax.nn.softmax(logits, axis=-1)
        rw = jnp.zeros_like(rw).at[..., 0].set(1.0)
        h = jax.nn.relu(jnp.einsum('bsd,edf->besf', tgt, w1) + b1[None, :, None, :])
        eo = jnp.einsum('besf,efd->besd', h, w2) + b2[None, :, None, :]
        tgt2 = jnp.einsum('besd,bse->bsd', eo, rw)
        x = tgt + tgt2
        mean = jnp.mean(x, axis=-1, keepdims=True)
        var = jnp.mean(jnp.square(x - mean), axis=-1, keepdims=True)
        return (x - mean) * jax.lax.rsqrt(var + LN_EPS) * gamma + beta
    x = x + _L0_xattn_ref(_layernorm(x, axis=-1), ctx_1024, ctx_1024, L0_xattn_wq_w, L0_xattn_wq_b, L0_xattn_wk_w, L0_xattn_wk_b, L0_xattn_wv_w, L0_xattn_wv_b, L0_xattn_wo_w, L0_xattn_wo_b)
    x = x + _L0_ffn_ref(_layernorm(x, axis=-1), L0_ffn_Wg, L0_ffn_gamma, L0_ffn_beta, L0_ffn_W1, L0_ffn_b1, L0_ffn_W2, L0_ffn_b2)
    x = x + _L1_xattn_ref(_layernorm(x, axis=-1), ctx_1024, L1_xattn_Wk, L1_xattn_bk, L1_xattn_Wv, L1_xattn_bv, L1_xattn_Wq, L1_xattn_bq, L1_xattn_Wo, L1_xattn_bo, L1_xattn_Wg, L1_xattn_bg, L1_xattn_Wl, L1_xattn_bl, L1_xattn_Wm, L1_xattn_bm, L1_xattn_g1, L1_xattn_b1, L1_xattn_g2, L1_xattn_b2)
    x = x + _L1_ffn_ref(_layernorm(x, axis=-1), L1_ffn_Wg, L1_ffn_bg, L1_ffn_bias, L1_ffn_W1, L1_ffn_b1, L1_ffn_W2, L1_ffn_b2)
    x = x + _L2_xattn_ref(_layernorm(x, axis=-1), ctx_1024, ctx_1024, L2_xattn_Wq, L2_xattn_bq, L2_xattn_Wk, L2_xattn_bk, L2_xattn_Wv, L2_xattn_bv, L2_xattn_Wo, L2_xattn_bo)
    x = x + _L2_ffn_ref(_layernorm(x, axis=-1), L2_ffn_router_w, L2_ffn_w_gate, L2_ffn_w_up, L2_ffn_w_down)
    x = x + _L3_xattn_ref(_layernorm(x, axis=-1), ctx_1024, L3_xattn_w_sim, L3_xattn_b_sim, L3_xattn_W_qv, L3_xattn_b_qv)
    x = x + _L3_ffn_ref(_layernorm(x, axis=-1), L3_ffn_router_w, L3_ffn_router_b, L3_ffn_w1, L3_ffn_b1, L3_ffn_w2, L3_ffn_b2, L3_ffn_gamma, L3_ffn_beta)
    return x

_drawn_inputs = setup_inputs


def setup_inputs(seed=0):
    import zlib

    import numpy as np

    out = dict(_drawn_inputs(seed))
    spreads = {'L0_xattn_wq_b': (0.0, 0.1),
     'L0_xattn_wk_b': (0.0, 2.0),
     'L0_xattn_wv_b': (0.0, 0.1),
     'L0_xattn_wo_b': (0.0, 0.1),
     'L0_ffn_gamma': (1.0, 0.2),
     'L0_ffn_beta': (0.0, 0.28),
     'L0_ffn_b1': (0.0, 0.276),
     'L0_ffn_b2': (0.0, 0.1),
     'L1_xattn_bk': (0.0, 2.0),
     'L1_xattn_bv': (0.0, 0.1),
     'L1_xattn_bq': (0.0, 0.8),
     'L1_xattn_bo': (0.0, 0.1),
     'L1_xattn_bg': (0.0, 0.8),
     'L1_xattn_bl': (0.0, 0.8),
     'L1_xattn_bm': (0.0, 0.542),
     'L1_xattn_g1': (1.0, 0.2),
     'L1_xattn_b1': (0.0, 0.1),
     'L1_xattn_g2': (1.0, 0.2),
     'L1_xattn_b2': (0.0, 0.1),
     'L1_ffn_bias': (0.0, 0.306),
     'L2_xattn_bq': (0.0, 0.8),
     'L2_xattn_bk': (0.0, 2.0),
     'L2_xattn_bv': (0.0, 0.793),
     'L2_xattn_bo': (0.0, 0.1),
     'L3_ffn_router_b': (0.0, 0.1),
     'L3_ffn_b1': (0.0, 0.422),
     'L3_ffn_b2': (0.0, 0.378),
     'L3_ffn_gamma': (1.0, 0.2),
     'L3_ffn_beta': (0.0, 0.345)}
    factors = {'L1_xattn_Wk': 8.0,
     'L1_xattn_Wq': 8.0,
     'L1_xattn_Wg': 7.08,
     'L1_xattn_Wl': 5.737,
     'L1_xattn_Wm': 4.903,
     'L1_ffn_bg': 2.98,
     'L1_ffn_b1': 6.418,
     'L1_ffn_b2': 4.843,
     'L2_xattn_Wq': 8.0,
     'L2_xattn_Wk': 8.0,
     'L2_xattn_Wv': 4.813,
     'L2_xattn_Wo': 4.343,
     'L3_xattn_w_sim': 8.0,
     'L3_xattn_b_qv': 7.781}
    for name, (base, spread) in spreads.items():
        noise = np.random.default_rng([zlib.crc32(name.encode()), seed]).standard_normal(out[name].shape)
        drawn = base * np.exp(spread * noise) if base else spread * noise
        out[name] = jnp.asarray(drawn.astype(out[name].dtype))
    for name, factor in factors.items():
        out[name] = (out[name] * factor).astype(out[name].dtype)
    return out
```

```python
import concourse.bass as bass
from concourse import mybir
from contextlib import ExitStack

NB, P, D = 8, 128, 128
T = NB * P
H = 16
DH = D // H
E0, F0 = 8, 512
E1, F1 = 16, 256
E2, F2 = 8, 512
F3 = 512
FM = 512
KEEP = int(P * 0.9)
DROP = P - KEEP
assert 8 < DROP <= 16

COLS, ROWS, SQS = {}, {}, {}


def _place(table, names):
    at = 0
    for name, n in names:
        table[name] = (at, n)
        at += n
    table["end"] = at


_place(COLS, [("bq0", 1), ("bk0", 1), ("gamma0", E0), ("beta0", E0 + 1), ("b1_0", E0 * F0 // P),
              ("bk1", 1), ("bq1", H), ("bg1", FM // P), ("bl1", FM // P), ("b1_1", E1 * F1 // P),
              ("bq2", 1), ("bk2", 1), ("w1s", 1), ("w2s", 1), ("w3s", 1), ("bqv", 1), ("b1_3", F3 // P)])
_place(ROWS, [("bv0", D), ("bo0", D), ("bv1", D), ("bo1", D), ("bm1", D), ("g1", D), ("be1", D),
              ("g2", D), ("be2", D), ("bv2", D), ("bo2", D), ("b2_3", D), ("g3", D), ("be3", D),
              ("rbg", E1), ("rbias", E1), ("bsim", 1)])
_place(SQS, [("wq0", D), ("wk0", D), ("wv0", D), ("wo0", D), ("r0", E0), ("wk1", D), ("wv1", D),
             ("r1", E1), ("wq2", D), ("wk2", D), ("wv2", D), ("wo2", D), ("r2", E2), ("wqv", 4 * D)])


def stages(order, groups, current, previous):
    for step in range(groups):
        for stage, positions, lag in order:
            for back, on in ((0, current), (1, previous)):
                n = step - lag + back * groups
                if on and n in positions and 0 <= n < groups:
                    yield stage, n, back


def pipelined(eng, order, groups, iterations, close):
    for stage, n, back in stages(order, groups, True, False):
        stage(0, n)
    close()
    with eng.Fori(1, iterations) as it:
        for stage, n, back in stages(order, groups, True, True):
            stage(it - back, n)
        close()
    for stage, n, back in stages(order, groups, False, True):
        stage(iterations - 1, n)
    close()


class Steps:

    def __init__(self, eng, sem):
        self.eng, self.sem, self.n = eng, sem, 0

    def one(self):
        self.n += 1
        return 1

    def close(self):
        if self.n:
            self.eng.wait_ge(self.sem, self.n)
            self.eng.sem_inc(self.sem, -self.n)
            self.n = 0


def build(nc, x_in, ctx_in, ctxT_in, cols_in, rows_in, sq_in, w0_in, w1q_in, w1o_in, w1m_in, w1_in,
          w2_in, w3_in, b2_0_in, b2_1_in, out):
    F32 = mybir.dt.float32
    U32 = mybir.dt.uint32
    ALU = mybir.AluOpType
    ACT = mybir.ActivationFunctionType
    X_AX = mybir.AxisListType.X

    ctx = ExitStack()
    with ctx:
        def sb(name, shape, dt=F32):
            return ctx.enter_context(nc.sbuf_tensor(name, shape, dt))

        def sem(name):
            return ctx.enter_context(nc.semaphore(name))

        x = sb("x_tok", [P, NB, D])
        xn = sb("xn_tok", [P, NB, D])
        xnT = sb("xn_feat", [D, T])
        ctx_tok = sb("ctx_tok", [P, NB, D])
        ctxT = sb("ctx_feat", [D, T])
        kT = sb("keys_feat", [D, T])
        qT = sb("queries_feat", [D, T])
        iv = sb("values_ctx", [P, NB, D])
        mv = sb("values_state", [P, NB, D])
        att = sb("att_tok", [P, NB, D])
        attT = sb("att_feat", [D, T])
        prob = sb("probabilities", [P, 2, H, P])
        probT = sb("probabilities_keys", [P, 2, H, P])
        q_b = sb("queries_batch", [D, 2, P])
        k_mask = sb("keys_masked", [D, 2, 4, P])
        head_mask = sb("head_mask", [P, 4])
        slot_mask = sb("slot_mask", [P, 4, 32])
        v_wide = sb("values_wide", [P, 2, H, 32])
        v_kept = sb("values_kept", [P, 2, H, 32])
        qh = sb("queries_heads", [P, 2, 4, P])
        qmk = sb("queries_times_keys", [P, 2, 4, P])
        mva = sb("self_values_weighted", [P, 2, 4, D])
        heads = sb("heads_tok", [P, 2, 4, D])
        headsT = sb("heads_feat", [P, 2, 4, P])
        hT = sb("hidden", [P, 2, 4, 512])
        normed = sb("expert_input", [D, 2, T])
        slot = sb("expert_weights", [P, 2, 1536])
        cols = sb("cols", [P, COLS["end"]])
        rows = sb("rows", [P, ROWS["end"]])
        sq = sb("square_weights", [D, SQS["end"]])
        wq1 = sb("wq1", [D, H, D])
        wo1 = sb("wo1", [D, H, D])
        wm1 = sb("wmlp1", [P, 3 * FM])
        w3 = sb("w3", [P, 2 * F3])
        b2_0 = sb("b2_0", [E0, D])
        b2_1 = sb("b2_1", [E1, D])
        ident = sb("identity", [P, P])
        ones = sb("ones", [P, 1])
        neg_half = sb("neg_half", [P, NB])
        expert_no = sb("expert_number", [P, E1])
        stats = sb("stats", [P, NB, 6])
        mean_var = sb("mean_var", [P, NB, 2])
        var_eps = sb("var_eps", [P, NB])
        rstd = sb("rstd", [P, NB])
        neg_max = sb("neg_max", [P, 8, 4])
        row_max = sb("row_max", [P, 2, 4])
        z = sb("exp_sums", [P, 2, H])
        r = sb("inverse_sums", [P, 2, H])
        self_arg = sb("self_arg", [P, 2, 4])
        self_exp = sb("self_exp", [P, 2, 4])
        self_w = sb("self_weight", [P, 2, 4])
        col_sum = sb("column_sums", [P, 2, H])
        ranked = sb("ranked", [H, P + 8])
        top = sb("top", [H, 2, 8])
        kept = sb("kept", [H, P])
        logits = sb("logits", [P, NB, E1])
        best = sb("best", [P, NB, 8])
        best_at = sb("best_at", [P, NB, 8], U32)
        best_no = sb("best_number", [P, NB, 2])
        gap = sb("gap", [P, NB])
        gap_exp = sb("gap_exp", [P, NB])
        w_a = sb("weight_first", [P, NB])
        w_b = sb("weight_second", [P, NB])
        cw = sb("combine_weights", [P, NB, E1])
        cw_b = sb("combine_weights_second", [P, NB, E1])
        cw_sum = sb("combine_sum", [P, NB])
        cwT = sb("combine_weights_experts", [E1, T])
        m_sim = sb("row_maxima", [P, NB])
        batt = sb("row_weights_b", [NB, P])
        batt2 = sb("row_weights_b2", [NB, P])
        bstat = sb("row_weights_stats", [NB, 4])
        batt_col = sb("row_weights", [P, NB])
        hc_bar = sb("hc_bar", [D, NB])

        def col(name, i=0, n=1):
            at = COLS[name][0] + i
            return cols[:, bass.ds(at, n)] if not isinstance(at, int) else cols[:, at:at + n]

        def row(name):
            at, n = ROWS[name]
            return rows[:, at:at + n]

        def row_b(name):
            return row(name)[:, None, :].broadcast_to([P, NB, D])

        def w(name, i=0, n=None):
            at, size = SQS[name]
            return sq[:, at + i:at + i + (n or size)]

        bank = [ctx.enter_context(nc.psum_tensor(f"bank{i}", [P, 512], F32)) for i in range(8)]

        def b4(i):
            return bank[i][:, :].rearrange("p (a b) -> p a b", a=4)

        x_loaded = sem("x_loaded")
        ctx_loaded = sem("ctx_loaded")
        cols_loaded = sem("cols_loaded")
        rows_loaded = sem("rows_loaded")
        sq_loaded = sem("sq_loaded")
        w1_attn_loaded = sem("w1_attn_loaded")
        w3_loaded = sem("w3_loaded")
        b2_loaded = sem("b2_loaded")
        slot0_loaded = sem("slot0_loaded")
        slot1_loaded = sem("slot1_loaded")
        slot0_free = sem("slot0_free")
        slot1_free = sem("slot1_free")
        consts_dve = sem("consts_dve")
        consts_pe = sem("consts_pe")
        dve_steps = sem("dve_steps")
        act_steps = sem("act_steps")
        pool_steps = sem("pool_steps")
        var_ready = sem("var_ready")
        rstd_ready = sem("rstd_ready")
        norm_tok_ready = sem("norm_tok_ready")
        transposed = sem("transposed")
        feat_ready = sem("feat_ready")
        feat_ready_dve = sem("feat_ready_dve")
        projected = sem("projected")
        qkv_ready = sem("qkv_ready")
        qkv_ready_pool = sem("qkv_ready_pool")
        qk_ready = sem("qk_ready")
        qk_free = sem("qk_free")
        scores_done = sem("scores_done")
        neg_max_ready = sem("neg_max_ready")
        probs_ready = sem("probs_ready")
        probsT_done = sem("probsT_done")
        probsT_ready = sem("probsT_ready")
        out_done = sem("out_done")
        out_free = sem("out_free")
        inv_ready = sem("inv_ready")
        colsum_done = sem("colsum_done")
        colsum_ready = sem("colsum_ready")
        ranked_done = sem("ranked_done")
        kept_ready = sem("kept_ready")
        keptT_done = sem("keptT_done")
        v_kept_ready = sem("v_kept_ready")
        att_ready = sem("att_ready")
        exps_done = sem("exps_done")
        scores_free = sem("scores_free")
        inverse_ready = sem("inverse_ready")
        turn_free = sem("turn_free")
        v_free = sem("v_free")
        v_ready = sem("v_ready")
        probsT_copied = sem("probsT_copied")
        y_attn_done = sem("y_attn_done")
        heads_q_done = sem("heads_q_done")
        q_free = sem("q_free")
        qh_ready = sem("qh_ready")
        qh_ready_pool = sem("qh_ready_pool")
        qmk_ready = sem("qmk_ready")
        probs_ready_dve = sem("probs_ready_dve")
        self_w_ready = sem("self_w_ready")
        mva_ready = sem("mva_ready")
        pv_done = sem("pv_done")
        own_free = sem("own_free")
        heads_ready = sem("heads_ready")
        headsT_done = sem("headsT_done")
        headsT_ready = sem("headsT_ready")
        wo_done = sem("wo_done")
        wo_free = sem("wo_free")
        router_done = sem("router_done")
        gap_ready = sem("gap_ready")
        gap_exp_ready = sem("gap_exp_ready")
        cw_ready = sem("cw_ready")
        cwT_done = sem("cwT_done")
        cwT_ready = sem("cwT_ready")
        bias_done = sem("bias_done")
        bias_free = sem("bias_free")
        normed_ready = sem("normed_ready")
        h_done = sem("h_done")
        g_done = sem("g_done")
        h_evac = sem("h_evac")
        y_done = sem("y_done")
        y_free = sem("y_free")
        store_done = sem("store_done")
        x3_sim = sem("x3_sim")
        x3_sims = sem("x3_sims")
        x3_neg = sem("x3_neg")
        x3_exp = sem("x3_exp")
        x3_t = sem("x3_t")
        x3_te = sem("x3_te")
        x3_pv = sem("x3_pv")
        x3_hq = sem("x3_hq")
        x3_hqT = sem("x3_hqT")
        x3_m = sem("x3_m")
        x3_mT = sem("x3_mT")
        x3_arg = sem("x3_arg")
        x3_bexp = sem("x3_bexp")
        x3_b = sem("x3_b")
        x3_bT = sem("x3_bT")
        x3_bTe = sem("x3_bTe")
        x3_hc = sem("x3_hc")
        x3_feats = sem("x3_feats")
        x3_out = sem("x3_out")
        x3_oute = sem("x3_oute")
        x3_outT = sem("x3_outT")
        slot_loaded = [slot0_loaded, slot1_loaded]
        slot_free = [slot0_free, slot1_free]

        block = ctx.enter_context(nc.Block())

        SC0 = float(DH) ** -0.5
        SC1 = float(D) ** -0.5
        PAD, GONE = -1.0e30, -3.0e38

        class FFN:
            def __init__(self, experts, width, gated, first, bias, up_bias, source, weights):
                self.E, self.FC, self.gated = experts, width // P, gated
                self.first, self.bias, self.up_bias = first, bias, up_bias
                self.source, self.weights = source, weights

            def ring(self):
                return 2 if self.gated else 4

            def w1(self, sub, fc):
                return self.weights(sub)[:, fc * P:(fc + 1) * P]

            def up(self, sub, fc):
                at = self.FC * P + fc * P
                return self.weights(sub)[:, at:at + P]

            def w2(self, sub, fc):
                at = (2 if self.gated else 1) * self.FC * P + fc * D
                return self.weights(sub)[:, at:at + D]

        in_slot = lambda sub: slot[:, sub, :]
        ffn0 = FFN(E0, F0, False, ACT.Relu, "b1_0", None, lambda sub: normed[:, sub, :], in_slot)
        mlp1 = FFN(1, FM, True, ACT.Relu, "bg1", "bl1", lambda sub: xnT[:, :], lambda sub: wm1[:, :])
        ffn1 = FFN(E1, F1, False, ACT.Relu, "b1_1", None, lambda sub: xnT[:, :], in_slot)
        ffn2 = FFN(E2, F2, True, ACT.Silu, None, None, lambda sub: xnT[:, :], in_slot)
        ffn3 = FFN(1, F3, False, ACT.Relu, "b1_3", None, lambda sub: xnT[:, :], lambda sub: w3[:, :])

        @block.sync
        def _(sp):
            sp.dma_start(x[:, :, :], x_in).then_inc(x_loaded, 16)
            sp.dma_start(ctxT[:, :], ctxT_in).then_inc(ctx_loaded, 16)
            sp.dma_start(sq[:, :], sq_in).then_inc(sq_loaded, 16)
            sp.dma_start(cols[:, :], cols_in).then_inc(cols_loaded, 16)
            sp.dma_start(rows[:, :], rows_in.broadcast_to([P, ROWS["end"]])).then_inc(rows_loaded, 16)
            sp.dma_start(b2_0[:, :], b2_0_in).then_inc(b2_loaded, 16)
            sp.dma_start(b2_1[:, :], b2_1_in).then_inc(b2_loaded, 16)
            for sub in range(2):
                sp.sem_inc(slot_free[sub], 1)

            def expert_loads(source, experts, width):
                with sp.Fori(0, experts // 2) as i:
                    for sub in range(2):
                        sp.wait_ge(slot_free[sub], 1)
                        sp.sem_inc(slot_free[sub], -1)
                        sp.dma_start(slot[:, sub, 0:width], source[bass.ds(2 * i + sub, 1), :, :]
                                     .rearrange("e p n -> p (e n)")).then_inc(slot_loaded[sub], 16)

            expert_loads(w0_in, E0, 2 * F0)
            sp.dma_start(wq1[:, :, :], w1q_in).then_inc(w1_attn_loaded, 16)
            sp.dma_start(wo1[:, :, :], w1o_in).then_inc(w1_attn_loaded, 16)
            sp.dma_start(wm1[:, :], w1m_in).then_inc(w1_attn_loaded, 16)
            sp.dma_start(ctx_tok[:, :, :], ctx_in).then_inc(w3_loaded, 16)
            sp.dma_start(w3[:, :], w3_in).then_inc(w3_loaded, 16)
            expert_loads(w1_in, E1, 2 * F1)
            expert_loads(w2_in, E2, 3 * F2)
            sp.wait_ge(store_done, 1)
            sp.sem_inc(store_done, -1)
            sp.dma_start(out, x[:, :, :]).then_inc(store_done, 16)
            sp.wait_ge(store_done, 16)

        @block.gpsimd
        def _(pool):
            st = Steps(pool, pool_steps)
            pool.memset(ident[:, :], 0.0).then_inc(st.sem, st.one())
            pool.memset(head_mask[:, :], 1.0).then_inc(st.sem, st.one())
            pool.memset(neg_half[:, :], -0.5).then_inc(st.sem, st.one())
            pool.memset(ones[:, :], 1.0).then_inc(st.sem, st.one())
            pool.memset(slot_mask[:, :, :], 1.0).then_inc(st.sem, st.one())
            pool.iota(expert_no[:, :], [[1, E1]], base=0, channel_multiplier=0,
                      allow_small_or_imprecise_dtypes=True).then_inc(st.sem, st.one())
            pool.wait_ge(st.sem, st.n)
            pool.affine_select(out=ident[:, :], in_=ident[:, :], compare_op=ALU.not_equal,
                               fill=1.0, base=0, pattern=[[-1, P]], channel_multiplier=1)\
                .then_inc(st.sem, st.one())
            pool.affine_select(out=slot_mask[:, :, :], in_=slot_mask[:, :, :], compare_op=ALU.is_ge, fill=0.0,
                               base=0, pattern=[[-DH, 4], [1, 32]], channel_multiplier=0)\
                .then_inc(st.sem, st.one())
            pool.wait_ge(st.sem, st.n)
            pool.affine_select(out=slot_mask[:, :, :], in_=slot_mask[:, :, :], compare_op=ALU.is_ge, fill=0.0,
                               base=DH - 1, pattern=[[DH, 4], [-1, 32]], channel_multiplier=0)\
                .then_inc(st.sem, st.one())
            for g in range(4):
                m = head_mask[32 * g:32 * g + 32, :]
                pool.wait_ge(st.sem, st.n)
                pool.affine_select(out=m, in_=m, compare_op=ALU.is_ge, fill=0.0, base=0,
                                   pattern=[[-DH, 4]], channel_multiplier=1).then_inc(st.sem, st.one())
                pool.wait_ge(st.sem, st.n)
                pool.affine_select(out=m, in_=m, compare_op=ALU.is_ge, fill=0.0, base=DH - 1,
                                   pattern=[[DH, 4]], channel_multiplier=-1).then_inc(st.sem, st.one())
            pool.wait_ge(st.sem, st.n)
            pool.sem_inc(consts_pe, 1)
            pool.sem_inc(consts_dve, 1)
            st.close()

            def inverse_roots():
                pool.wait_ge(var_ready, 1)
                pool.sem_inc(var_ready, -1)
                pool.tensor_tensor(rstd[:, :], var_eps[:, :], neg_half[:, :], ALU.pow)\
                    .then_inc(rstd_ready, 1)

            def narrow_attention():
                pool.wait_ge(qkv_ready_pool, 1)
                pool.sem_inc(qkv_ready_pool, -1)

                def spread_queries_keys(it, n):
                    pool.wait_ge(qk_free, 1)
                    pool.sem_inc(qk_free, -1)
                    tok = bass.ds((2 * it + n // 4) * P, P)
                    pool.tensor_copy(q_b[:, n // 4, :], qT[:, tok]).then_inc(st.sem, st.one())
                    pool.tensor_tensor(k_mask[:, n // 4, :, :],
                                       kT[:, tok][:, None, :].broadcast_to([D, 4, P]),
                                       head_mask[:, :, None].broadcast_to([D, 4, P]), ALU.mult)\
                        .then_inc(st.sem, st.one())
                    pool.wait_ge(st.sem, st.n)
                    pool.sem_inc(qk_ready, 1)

                def spread_values(it, n):
                    pool.wait_ge(v_free, 1)
                    pool.sem_inc(v_free, -1)
                    four = [P, 4, 4, 32]
                    v_b = iv[:, bass.ds(2 * it + n // 4, 1), :].rearrange("p b (j c) -> p (b j) c", j=4)
                    pool.tensor_tensor(v_wide[:, n // 4, :, :].rearrange("p (j i) c -> p j i c", j=4),
                                       v_b[:, :, None, :].broadcast_to(four),
                                       slot_mask[:, None, :, :].broadcast_to(four), ALU.mult)\
                        .then_inc(v_ready, 1)

                def normalise(it, n):
                    pool.wait_ge(inverse_ready, 1)
                    pool.sem_inc(inverse_ready, -1)
                    h = slice(4 * (n % 4), 4 * (n % 4) + 4)
                    pool.tensor_tensor(prob[:, n // 4, h, :], prob[:, n // 4, h, :],
                                       r[:, n // 4, h][:, :, None].broadcast_to([P, 4, P]), ALU.mult)\
                        .then_inc(probs_ready, 1)

                for sub in range(2):
                    pool.sem_inc(qk_free, 1)
                    pool.sem_inc(v_free, 1)
                pipelined(pool, [(spread_queries_keys, (0, 4), 0), (spread_values, (0, 4), 2),
                                 (normalise, range(8), 3)], 8, NB // 2, st.close)
                pool.wait_ge(qk_free, 2)
                pool.sem_inc(qk_free, -2)
                pool.wait_ge(v_free, 2)
                pool.sem_inc(v_free, -2)

            def wide_attention():
                def self_products(it, n):
                    pool.wait_ge(qh_ready_pool, 1)
                    pool.sem_inc(qh_ready_pool, -1)
                    tok = bass.ds((2 * it + n // 4) * P, P)
                    pool.tensor_tensor(qmk[:, n % 2, :, :], qh[:, n % 2, :, :],
                                       qT[:, tok][:, None, :].broadcast_to([P, 4, P]), ALU.mult)\
                        .then_inc(qmk_ready, 1)

                def self_values(it, n):
                    pool.wait_ge(self_w_ready, 1)
                    pool.sem_inc(self_w_ready, -1)
                    pool.tensor_tensor(mva[:, n % 2, :, :],
                                       mv[:, bass.ds(2 * it + n // 4, 1), :].broadcast_to([P, 4, D]),
                                       self_w[:, n % 2, :, None].broadcast_to([P, 4, D]), ALU.mult)\
                        .then_inc(mva_ready, 1)

                pipelined(pool, [(self_values, range(8), 2), (self_products, range(8), 0)],
                          8, NB // 2, lambda: None)

            inverse_roots()
            narrow_attention()
            inverse_roots()
            inverse_roots()
            inverse_roots()
            wide_attention()
            inverse_roots()
            inverse_roots()
            inverse_roots()
            inverse_roots()
            narrow_attention()
            inverse_roots()
            inverse_roots()
            inverse_roots()
            inverse_roots()

        @block.scalar
        def _(act):
            st = Steps(act, act_steps)

            def evacuate_transposed(dst, also=()):
                for half in range(2):
                    act.wait_ge(transposed, 1)
                    act.sem_inc(transposed, -1)
                    act.activation(dst[:, half * 512:(half + 1) * 512], bank[half][:, :], ACT.Copy)\
                        .then_inc(st.sem, st.one())
                act.wait_ge(st.sem, st.n)
                act.sem_inc(feat_ready, 1)
                for token in also:
                    act.sem_inc(token, 1)
                st.close()

            def narrow_attention(prune):
                def exps(it, n):
                    act.wait_ge(neg_max_ready, 1)
                    act.sem_inc(neg_max_ready, -1)
                    for i in range(4):
                        h = 4 * (n % 4) + i
                        act.activation(prob[:, n // 4, h, :], b4(n % 2)[:, i, :], ACT.Exp,
                                       bias=neg_max[:, n, i:i + 1], accum_out=z[:, n // 4, h:h + 1])\
                            .then_inc(exps_done, 1)

                def copy_probsT(it, n):
                    act.wait_ge(probsT_done, 1)
                    act.sem_inc(probsT_done, -1)
                    h = 4 * (n % 4)
                    act.activation(probT[:, n // 4, h:h + 4, :], b4(2 + n % 2), ACT.Copy)\
                        .then_inc(st.sem, st.one())
                    act.wait_ge(st.sem, st.n)
                    act.sem_inc(probsT_ready, 1)
                    act.sem_inc(turn_free, 1)
                    act.sem_inc(probsT_copied, 1)

                if prune:
                    pipelined(act, [(exps, range(8), 0), (copy_probsT, range(8), 2)], 8, NB // 2, st.close)
                else:
                    pipelined(act, [(exps, range(8), 0)], 8, NB // 2, lambda: None)

            def wide_attention():
                def copy_probsT(it, n):
                    act.wait_ge(probsT_done, 1)
                    act.sem_inc(probsT_done, -1)
                    act.activation(probT[:, 0, 4 * (n % 2):4 * (n % 2) + 4, :], b4(3), ACT.Copy)\
                        .then_inc(probsT_ready, 1)

                def copy_headsT(it, n):
                    act.wait_ge(headsT_done, 1)
                    act.sem_inc(headsT_done, -1)
                    act.activation(headsT[:, n % 2, :, :], b4(5), ACT.Copy).then_inc(headsT_ready, 1)

                def exps(it, n):
                    act.wait_ge(neg_max_ready, 1)
                    act.sem_inc(neg_max_ready, -1)
                    for i in range(4):
                        act.activation(prob[:, 0, 4 * (n % 2) + i, :], b4(1 + n % 2)[:, i, :],
                                       ACT.Exp, bias=neg_max[:, n, i:i + 1], scale=SC1,
                                       accum_out=z[:, 0, 4 * (n % 2) + i:4 * (n % 2) + i + 1])\
                            .then_inc(st.sem, st.one())
                    act.activation(self_exp[:, n % 2, :], self_arg[:, n % 2, :], ACT.Exp)\
                        .then_inc(st.sem, st.one())
                    act.wait_ge(st.sem, st.n)
                    act.sem_inc(probs_ready, 1)
                    act.sem_inc(probs_ready_dve, 1)

                pipelined(act, [(copy_headsT, range(8), 5), (copy_probsT, range(8), 3), (exps, range(8), 1)],
                          8, NB // 2, st.close)

            def router_exp():
                act.wait_ge(gap_ready, 1)
                act.sem_inc(gap_ready, -1)
                act.activation(gap_exp[:, :], gap[:, :], ACT.Exp).then_inc(gap_exp_ready, 1)

            def ffn(f):
                def expert(e, sub):
                    for k in range(2 * f.FC):
                        half, fc = divmod(k, f.FC)
                        act.wait_ge(h_done, 1)
                        act.sem_inc(h_done, -1)
                        kw = {"bias": col(f.bias, e * f.FC + fc)} if f.bias else {}
                        act.activation(hT[:, half, fc, :], bank[k % f.ring()][:, :], f.first, **kw)\
                            .then_inc(g_done if f.gated else h_evac, 1)
                if f.E == 1:
                    expert(0, 0)
                else:
                    with act.Fori(0, f.E // 2) as i:
                        for sub in range(2):
                            expert(2 * i + sub, sub)

            act.wait_ge(cols_loaded, 16)
            evacuate_transposed(xnT)
            narrow_attention(False)
            evacuate_transposed(xnT)
            evacuate_transposed(kT, also=[feat_ready_dve])
            router_exp()
            ffn(ffn0)
            evacuate_transposed(xnT)
            wide_attention()
            evacuate_transposed(xnT)
            ffn(mlp1)
            evacuate_transposed(xnT)
            router_exp()
            ffn(ffn1)
            evacuate_transposed(xnT)
            narrow_attention(True)
            evacuate_transposed(xnT)
            router_exp()
            ffn(ffn2)
            evacuate_transposed(xnT, also=[feat_ready_dve])
            for g in range(2):
                act.wait_ge(x3_neg, 1)
                act.sem_inc(x3_neg, -1)
                for i in range(4):
                    b = 4 * g + i
                    act.activation(prob[:, 0, b, :], b4(g)[:, i, :], ACT.Exp,
                                   bias=neg_max[:, g, i:i + 1], accum_out=z[:, 0, b:b + 1])\
                        .then_inc(st.sem, st.one())
                act.wait_ge(st.sem, st.n)
                act.sem_inc(x3_exp, 1)
            act.wait_ge(x3_arg, 1)
            act.sem_inc(x3_arg, -1)
            act.activation(batt2[:, :], batt[:, :], ACT.Exp, bias=bstat[:, 0:1],
                           accum_out=bstat[:, 1:2]).then_inc(st.sem, st.one())
            act.wait_ge(st.sem, st.n)
            act.sem_inc(x3_bexp, 1)
            for half in range(2):
                act.wait_ge(x3_out, 1)
                act.sem_inc(x3_out, -1)
                act.activation(attT[:, half * 512:(half + 1) * 512], bank[half][:, :],
                               ACT.Identity, bias=col("bqv")).then_inc(st.sem, st.one())
            act.wait_ge(st.sem, st.n)
            act.sem_inc(x3_oute, 1)
            evacuate_transposed(xnT)
            ffn(ffn3)

        @block.tensor
        def _(pe):
            def mm(o, l, rh, start=True, stop=True, **kw):
                return pe.matmul(o, l, rh, start=start, stop=stop, **kw)

            def transpose_tiles(src, ready):
                pe.wait_ge(ready, 1)
                pe.sem_inc(ready, -1)
                for b in range(NB):
                    t = pe.transpose(b4(b // 4)[:, b % 4, :], src[:, b, :], ident[:, :])
                    if b % 4 == 3:
                        t.then_inc(transposed, 1)

            def project(weight, src, at):
                for half in range(2):
                    mm(bank[at + half][:, :], weight, src[:, half * 512:(half + 1) * 512])\
                        .then_inc(projected, 1)

            def project_tok(weight, src, at):
                for b in range(NB):
                    m = mm(b4(at + b // 4)[:, b % 4, :], src[:, b * P:(b + 1) * P], weight)
                    if b % 4 == 3:
                        m.then_inc(projected, 1)

            def narrow_attention(prune):
                def scores(it, n):
                    if n % 4 == 0:
                        pe.wait_ge(qk_ready, 1)
                        pe.sem_inc(qk_ready, -1)
                    pe.wait_ge(scores_free, 1)
                    pe.sem_inc(scores_free, -1)
                    p = slice(32 * (n % 4), 32 * (n % 4) + 32)
                    mm(bank[n % 2][:, :], q_b[p, n // 4, :],
                       k_mask[p, n // 4, :, :].rearrange("p a b -> p (a b)")).then_inc(scores_done, 1)

                def turn(it, n):
                    pe.wait_ge(probs_ready, 1)
                    pe.sem_inc(probs_ready, -1)
                    pe.wait_ge(turn_free, 1)
                    pe.sem_inc(turn_free, -1)
                    for i in range(4):
                        t = pe.transpose(b4(2 + n % 2)[:, i, :], prob[:, n // 4, 4 * (n % 4) + i, :],
                                         ident[:, :])
                    t.then_inc(probsT_done, 1)

                def four_heads(source, n):
                    j = n % 4
                    for i in range(4):
                        h = 4 * j + i
                        m = mm(bank[6 + n // 4][32 * j:32 * j + 32, 0:P], source[:, n // 4, h, :],
                               probT[:, n // 4, h, :], start=(i == 0), stop=(i == 3))
                    return m

                def values(it, n):
                    pe.wait_ge(probsT_ready, 1)
                    pe.sem_inc(probsT_ready, -1)
                    if n % 4 == 0:
                        pe.wait_ge(v_ready, 1)
                        pe.sem_inc(v_ready, -1)
                        pe.wait_ge(out_free, 1)
                        pe.sem_inc(out_free, -1)
                    m = four_heads(v_wide, n)
                    if n % 4 == 3:
                        m.then_inc(out_done, 1)

                def turn_sums(it, n):
                    pe.wait_ge(colsum_ready, 1)
                    pe.sem_inc(colsum_ready, -1)
                    pe.transpose(bank[5][0:H, 0:P], col_sum[:, n // 4, :], ident[:, :])\
                        .then_inc(ranked_done, 1)

                def turn_kept(it, n):
                    pe.wait_ge(kept_ready, 1)
                    pe.sem_inc(kept_ready, -1)
                    pe.transpose(bank[5][:, 256:256 + H], kept[:, :], ident[0:H, 0:H])\
                        .then_inc(keptT_done, 1)

                def values_kept(it, n):
                    pe.wait_ge(v_kept_ready, 1)
                    pe.sem_inc(v_kept_ready, -1)
                    pe.wait_ge(probsT_ready, 4)
                    pe.sem_inc(probsT_ready, -4)
                    pe.wait_ge(out_free, 1)
                    pe.sem_inc(out_free, -1)
                    for j in range(4):
                        m = four_heads(v_kept, n - 3 + j)
                    m.then_inc(out_done, 1)

                pe.sem_inc(scores_free, 2)
                pe.sem_inc(turn_free, 2)
                pe.sem_inc(out_free, 2)
                if prune:
                    pipelined(pe, [(scores, range(8), 0), (turn, range(8), 2), (turn_sums, (3, 7), 4),
                                   (turn_kept, (3, 7), 5), (values_kept, (3, 7), 6)], 8, NB // 2,
                              lambda: None)
                else:
                    pipelined(pe, [(scores, range(8), 0), (turn, range(8), 2), (values, range(8), 3)],
                              8, NB // 2, lambda: None)
                pe.wait_ge(scores_free, 2)
                pe.sem_inc(scores_free, -2)
                pe.wait_ge(turn_free, 2)
                pe.sem_inc(turn_free, -2)
                pe.wait_ge(out_free, 2)
                pe.sem_inc(out_free, -2)

            def attention_output(weight):
                pe.wait_ge(att_ready, 1)
                pe.sem_inc(att_ready, -1)
                for b in range(NB):
                    m = mm(b4(2 + b // 4)[:, b % 4, :], attT[:, b * P:(b + 1) * P], weight)
                    if b % 4 == 3:
                        m.then_inc(y_attn_done, 1)

            def wide_attention():
                def queries(it, n):
                    pe.wait_ge(q_free, 1)
                    pe.sem_inc(q_free, -1)
                    for i in range(4):
                        m = mm(b4(0)[:, i, :], wq1[:, 4 * (n % 4) + i, :],
                               xnT[:, bass.ds((2 * it + n // 4) * P, P)])
                    m.then_inc(heads_q_done, 1)

                def scores(it, n):
                    pe.wait_ge(qh_ready, 1)
                    pe.sem_inc(qh_ready, -1)
                    for i in range(4):
                        mm(b4(1 + n % 2)[:, i, :], qh[:, n % 2, i, :],
                           kT[:, bass.ds((2 * it + n // 4) * P, P)])
                    pe.wait_ge(qmk_ready, 1)
                    pe.sem_inc(qmk_ready, -1)
                    pe.wait_ge(own_free, 1)
                    pe.sem_inc(own_free, -1)
                    for i in range(4):
                        at = 4 * (n % 2) + i
                        m = mm(bank[7][:, at:at + 1], qmk[:, n % 2, i, :], ones[:, :])
                    m.then_inc(scores_done, 1)

                def turn(it, n):
                    pe.wait_ge(probs_ready, 1)
                    pe.sem_inc(probs_ready, -1)
                    for i in range(4):
                        t = pe.transpose(b4(3)[:, i, :], prob[:, 0, 4 * (n % 2) + i, :], ident[:, :])
                    t.then_inc(probsT_done, 1)

                def values(it, n):
                    pe.wait_ge(probsT_ready, 1)
                    pe.sem_inc(probsT_ready, -1)
                    for i in range(4):
                        m = mm(b4(4)[:, i, :], probT[:, 0, 4 * (n % 2) + i, :],
                               iv[:, bass.ds(2 * it + n // 4, 1), :].rearrange("p a b -> p (a b)"))
                    m.then_inc(pv_done, 1)

                def turn_heads(it, n):
                    pe.wait_ge(heads_ready, 1)
                    pe.sem_inc(heads_ready, -1)
                    for i in range(4):
                        t = pe.transpose(b4(5)[:, i, :], heads[:, n % 2, i, :], ident[:, :])
                    t.then_inc(headsT_done, 1)

                def output(it, n):
                    pe.wait_ge(headsT_ready, 1)
                    pe.sem_inc(headsT_ready, -1)
                    if n % 4 == 0:
                        pe.wait_ge(wo_free, 1)
                        pe.sem_inc(wo_free, -1)
                    for i in range(4):
                        h = 4 * (n % 4) + i
                        m = mm(bank[6][:, 0:D], headsT[:, n % 2, i, :], wo1[:, h, :],
                               start=(h == 0), stop=(h == H - 1))
                    if n % 4 == 3:
                        m.then_inc(wo_done, 1)

                pe.sem_inc(q_free, 1)
                pe.sem_inc(own_free, 1)
                pe.sem_inc(wo_free, 1)
                pipelined(pe, [(queries, range(8), 0), (scores, range(8), 1), (output, range(8), 5),
                               (turn_heads, range(8), 4), (values, range(8), 3), (turn, range(8), 2)],
                          8, NB // 2, lambda: None)
                pe.wait_ge(q_free, 1)
                pe.sem_inc(q_free, -1)
                pe.wait_ge(own_free, 1)
                pe.sem_inc(own_free, -1)
                pe.wait_ge(wo_free, 1)
                pe.sem_inc(wo_free, -1)

            def route(weight, experts, src):
                for b in range(NB):
                    m = mm(bank[4][:, b * experts:(b + 1) * experts], src[:, b * P:(b + 1) * P], weight)
                m.then_inc(router_done, 1)

            def expert_biases(b2, experts):
                pe.wait_ge(cw_ready, 1)
                pe.sem_inc(cw_ready, -1)
                for b in range(NB):
                    t = pe.transpose(b4(2 + b // 4)[0:experts, b % 4, :], cw[:, b, 0:experts], ident[:, :])
                t.then_inc(cwT_done, 1)
                pe.wait_ge(cwT_ready, 1)
                pe.sem_inc(cwT_ready, -1)
                for b in range(NB):
                    m = mm(b4(6 + b // 4)[:, b % 4, :], cwT[0:experts, b * P:(b + 1) * P], b2[0:experts, :])
                m.then_inc(bias_done, 1)
                pe.wait_ge(bias_free, 1)
                pe.sem_inc(bias_free, -1)

            def ffn(f):
                def expert(sub):
                    if f.E > 1:
                        pe.wait_ge(slot_loaded[sub], 16)
                        pe.sem_inc(slot_loaded[sub], -16)
                    if f is ffn0:
                        pe.wait_ge(normed_ready, 1)
                        pe.sem_inc(normed_ready, -1)
                    src, ring = f.source(sub), f.ring()
                    for k in range(2 * f.FC):
                        half, fc = divmod(k, f.FC)
                        if k >= ring:
                            pe.wait_ge(h_evac, k - ring + 1)
                        m = mm(bank[k % ring][:, :], f.w1(sub, fc), src[:, half * 512:(half + 1) * 512])
                        if f.gated:
                            m = mm(bank[2 + k % ring][:, :], f.up(sub, fc),
                                   src[:, half * 512:(half + 1) * 512])
                        m.then_inc(h_done, 1)
                    for half in range(2):
                        pe.wait_ge(h_evac, f.FC * (half + 1))
                        pe.wait_ge(y_free, 1)
                        pe.sem_inc(y_free, -1)
                        for t in range(4):
                            for fc in range(f.FC):
                                m = mm(b4(4 + 2 * sub + half)[:, t, :],
                                       hT[:, half, fc, t * P:(t + 1) * P], f.w2(sub, fc),
                                       start=(fc == 0), stop=(fc == f.FC - 1))
                        m.then_inc(y_done, 1)
                    pe.sem_inc(h_evac, -2 * f.FC)

                for _ in range(4):
                    pe.sem_inc(y_free, 1)
                if f.E == 1:
                    expert(0)
                else:
                    with pe.Fori(0, f.E // 2):
                        for sub in range(2):
                            expert(sub)
                pe.wait_ge(y_free, 4)
                pe.sem_inc(y_free, -4)

            pe.wait_ge(consts_pe, 1)
            pe.sem_inc(consts_pe, -1)
            pe.wait_ge(sq_loaded, 16)
            pe.wait_ge(ctx_loaded, 16)

            project(w("wk0"), ctxT, 2)
            project_tok(w("wv0"), ctxT, 4)
            transpose_tiles(xn, norm_tok_ready)
            pe.wait_ge(feat_ready, 1)
            pe.sem_inc(feat_ready, -1)
            project(w("wq0"), xnT, 6)
            pe.wait_ge(qkv_ready, 1)
            pe.sem_inc(qkv_ready, -1)
            narrow_attention(False)
            attention_output(w("wo0"))
            transpose_tiles(xn, norm_tok_ready)
            pe.wait_ge(feat_ready, 1)
            pe.sem_inc(feat_ready, -1)
            route(w("r0"), E0, xnT)
            transpose_tiles(att, norm_tok_ready)
            pe.wait_ge(feat_ready, 1)
            pe.sem_inc(feat_ready, -1)
            pe.wait_ge(b2_loaded, 32)
            expert_biases(b2_0, E0)
            ffn(ffn0)

            project(w("wk1"), ctxT, 2)
            project_tok(w("wv1"), ctxT, 4)
            transpose_tiles(xn, norm_tok_ready)
            pe.wait_ge(feat_ready, 1)
            pe.sem_inc(feat_ready, -1)
            pe.wait_ge(qkv_ready, 1)
            pe.sem_inc(qkv_ready, -1)
            project(w("wk1"), xnT, 2)
            project_tok(w("wv1"), xnT, 4)
            pe.wait_ge(qkv_ready, 1)
            pe.sem_inc(qkv_ready, -1)
            pe.wait_ge(w1_attn_loaded, 48)
            wide_attention()
            transpose_tiles(iv, norm_tok_ready)
            pe.wait_ge(feat_ready, 1)
            pe.sem_inc(feat_ready, -1)
            ffn(mlp1)
            transpose_tiles(xn, norm_tok_ready)
            pe.wait_ge(feat_ready, 1)
            pe.sem_inc(feat_ready, -1)
            route(w("r1"), E1, xnT)
            expert_biases(b2_1, E1)
            ffn(ffn1)

            project(w("wk2"), ctxT, 2)
            project_tok(w("wv2"), ctxT, 4)
            transpose_tiles(xn, norm_tok_ready)
            pe.wait_ge(feat_ready, 1)
            pe.sem_inc(feat_ready, -1)
            project(w("wq2"), xnT, 6)
            pe.wait_ge(qkv_ready, 1)
            pe.sem_inc(qkv_ready, -1)
            narrow_attention(True)
            attention_output(w("wo2"))
            transpose_tiles(xn, norm_tok_ready)
            pe.wait_ge(feat_ready, 1)
            pe.sem_inc(feat_ready, -1)
            route(w("r2"), E2, xnT)
            pe.wait_ge(cw_ready, 1)
            pe.sem_inc(cw_ready, -1)
            ffn(ffn2)

            transpose_tiles(xn, norm_tok_ready)
            pe.wait_ge(feat_ready, 1)
            pe.sem_inc(feat_ready, -1)
            for b in range(NB):
                m = mm(bank[2][:, b:b + 1], xnT[:, b * P:(b + 1) * P], col("w1s"))
            pe.wait_ge(x3_sim, 1)
            pe.sem_inc(x3_sim, -1)
            for b in range(NB):
                m = mm(b4(b // 4)[:, b % 4, :], qT[:, b * P:(b + 1) * P], ctxT[:, b * P:(b + 1) * P])
                if b % 4 == 3:
                    m.then_inc(x3_sims, 1)
            pe.wait_ge(w3_loaded, 32)
            pe.wait_ge(x3_m, 1)
            pe.sem_inc(x3_m, -1)
            pe.transpose(bank[3][0:NB, 0:P], m_sim[:, :], ident[:, :]).then_inc(x3_mT, 1)
            for g in range(2):
                pe.wait_ge(x3_exp, 1)
                pe.sem_inc(x3_exp, -1)
                for i in range(4):
                    t = pe.transpose(b4(4 + g)[:, i, :], prob[:, 0, 4 * g + i, :], ident[:, :])
                t.then_inc(x3_t, 1)
            for g in range(2):
                pe.wait_ge(x3_te, 1)
                pe.sem_inc(x3_te, -1)
                for i in range(4):
                    m = mm(b4(6 + g)[:, i, :], probT[:, 0, 4 * g + i, :], ctx_tok[:, 4 * g + i, :])
                m.then_inc(x3_pv, 1)
            pe.wait_ge(x3_b, 1)
            pe.sem_inc(x3_b, -1)
            pe.transpose(bank[3][:, 256:256 + NB], batt[:, :], ident[0:NB, 0:NB]).then_inc(x3_bT, 1)
            for g in range(2):
                pe.wait_ge(x3_hq, 1)
                pe.sem_inc(x3_hq, -1)
                for i in range(4):
                    t = pe.transpose(b4(4 + g)[:, i, :], iv[:, 4 * g + i, :], ident[:, :])
                t.then_inc(x3_hqT, 1)
            pe.wait_ge(x3_bTe, 1)
            pe.sem_inc(x3_bTe, -1)
            for b in range(NB):
                m = mm(bank[2][:, 16 + b:17 + b], xn[:, b, :], batt_col[:, b:b + 1])
            m.then_inc(x3_hc, 1)
            pe.wait_ge(x3_feats, 1)
            pe.sem_inc(x3_feats, -1)
            for half in range(2):
                t = slice(half * 512, (half + 1) * 512)
                for i, src in enumerate((xnT[:, t], kT[:, t], normed[:, 0, t], normed[:, 1, t])):
                    m = mm(bank[half][:, :], w("wqv", i * D, D), src, start=(i == 0), stop=(i == 3))
                m.then_inc(x3_out, 1)
            pe.wait_ge(x3_oute, 1)
            pe.sem_inc(x3_oute, -1)
            for b in range(NB):
                t = pe.transpose(b4(2 + b // 4)[:, b % 4, :], attT[:, b * P:(b + 1) * P], ident[:, :])
            t.then_inc(x3_outT, 1)

            transpose_tiles(xn, norm_tok_ready)
            pe.wait_ge(feat_ready, 1)
            pe.sem_inc(feat_ready, -1)
            ffn(ffn3)

        @block.vector
        def _(dve):
            st = Steps(dve, dve_steps)

            def layer_norm(src, dst, eps, gamma=None, beta=None, give=()):
                dve.wait_ge(st.sem, st.n)
                for b in range(NB):
                    dve.bn_stats(stats[:, b, :], src[:, b, :]).then_inc(st.sem, st.one())
                dve.wait_ge(st.sem, st.n)
                for b in range(NB):
                    dve.bn_aggr(mean_var[:, b, :], stats[:, b, :]).then_inc(st.sem, st.one())
                dve.wait_ge(st.sem, st.n)
                dve.tensor_scalar(var_eps[:, :], mean_var[:, :, 1], eps, None, ALU.add)\
                    .then_inc(st.sem, st.one())
                dve.wait_ge(st.sem, st.n)
                dve.sem_inc(var_ready, 1)
                dve.wait_ge(rstd_ready, 1)
                dve.sem_inc(rstd_ready, -1)
                for b in range(NB):
                    dve.tensor_scalar(dst[:, b, :], src[:, b, :], mean_var[:, b, 0:1],
                                      rstd[:, b:b + 1], ALU.subtract, ALU.mult).then_inc(st.sem, st.one())
                if gamma:
                    dve.wait_ge(st.sem, st.n)
                    dve.tensor_tensor(dst[:, :, :], dst[:, :, :], row_b(gamma), ALU.mult)\
                        .then_inc(st.sem, st.one())
                    dve.wait_ge(st.sem, st.n)
                    dve.tensor_tensor(dst[:, :, :], dst[:, :, :], row_b(beta), ALU.add)\
                        .then_inc(st.sem, st.one())
                dve.wait_ge(st.sem, st.n)
                for token in give:
                    dve.sem_inc(token, 1)
                st.close()

            def add_to_x(what):
                dve.wait_ge(st.sem, st.n)
                dve.tensor_tensor(x[:, :, :], x[:, :, :], what, ALU.add).then_inc(st.sem, st.one())
                dve.wait_ge(st.sem, st.n)

            def copy_projected(dst, at, bias, scale):
                for half in range(2):
                    dve.wait_ge(projected, 1)
                    dve.sem_inc(projected, -1)
                    dve.tensor_scalar(dst[:, half * 512:(half + 1) * 512], bank[at + half][:, :],
                                      col(bias), scale, ALU.add, ALU.mult).then_inc(st.sem, st.one())

            def copy_values(dst, at, bias):
                for half in range(2):
                    dve.wait_ge(projected, 1)
                    dve.sem_inc(projected, -1)
                    dve.tensor_tensor(dst[:, 4 * half:4 * half + 4, :], b4(at + half),
                                      row(bias)[:, None, :].broadcast_to([P, 4, D]), ALU.add)\
                        .then_inc(st.sem, st.one())

            def narrow_attention(prune):
                def maxima(it, n):
                    dve.wait_ge(scores_done, 1)
                    dve.sem_inc(scores_done, -1)
                    if n % 4 == 3:
                        dve.sem_inc(qk_free, 1)
                    dve.tensor_reduce(neg_max[:, n, :], b4(n % 2), X_AX, ALU.max, negate=True)\
                        .then_inc(neg_max_ready, 1)

                def inverse_sums(it, n):
                    dve.wait_ge(exps_done, 4)
                    dve.sem_inc(exps_done, -4)
                    h = slice(4 * (n % 4), 4 * (n % 4) + 4)
                    dve.reciprocal(r[:, n // 4, h], z[:, n // 4, h]).then_inc(st.sem, st.one())
                    dve.wait_ge(st.sem, st.n)
                    dve.sem_inc(inverse_ready, 1)
                    dve.sem_inc(scores_free, 1)

                def copy_probsT(it, n):
                    dve.wait_ge(probsT_done, 1)
                    dve.sem_inc(probsT_done, -1)
                    h = 4 * (n % 4)
                    dve.tensor_copy(probT[:, n // 4, h:h + 4, :], b4(2 + n % 2)).then_inc(st.sem, st.one())
                    dve.wait_ge(st.sem, st.n)
                    dve.sem_inc(probsT_ready, 1)
                    dve.sem_inc(turn_free, 1)

                def copy_out(it, n):
                    dve.wait_ge(out_done, 1)
                    dve.sem_inc(out_done, -1)
                    if not prune:
                        dve.sem_inc(v_free, 1)
                    dve.tensor_copy(attT[:, bass.ds((2 * it + n // 4) * P, P)], bank[6 + n // 4][:, 0:P])\
                        .then_inc(st.sem, st.one())
                    dve.wait_ge(st.sem, st.n)
                    dve.sem_inc(out_free, 1)

                def column_sums(it, n):
                    dve.wait_ge(probsT_copied, 1)
                    dve.sem_inc(probsT_copied, -1)
                    h = slice(4 * (n % 4), 4 * (n % 4) + 4)
                    dve.tensor_reduce(col_sum[:, n // 4, h], probT[:, n // 4, h, :], X_AX, ALU.add)\
                        .then_inc(st.sem, st.one())
                    if n % 4 == 3:
                        dve.wait_ge(st.sem, st.n)
                        dve.sem_inc(colsum_ready, 1)

                def rank(it, n):
                    dve.wait_ge(ranked_done, 1)
                    dve.sem_inc(ranked_done, -1)
                    dve.tensor_scalar(ranked[:, 0:P], bank[5][0:H, P - 1::-1][:, 0:P], -1.0, None,
                                      ALU.mult).then_inc(st.sem, st.one())
                    dve.memset(ranked[:, P:P + 8], PAD).then_inc(st.sem, st.one())
                    dve.wait_ge(st.sem, st.n)
                    dve.max(top[:, 0, :], ranked[:, :]).then_inc(st.sem, st.one())
                    dve.wait_ge(st.sem, st.n)
                    dve.match_replace(ranked[:, :], top[:, 0, :], ranked[:, :], GONE)\
                        .then_inc(st.sem, st.one())
                    dve.wait_ge(st.sem, st.n)
                    dve.max(top[:, 1, :], ranked[:, :]).then_inc(st.sem, st.one())
                    dve.wait_ge(st.sem, st.n)
                    dve.memset(top[:, 1, DROP - 8:8], PAD).then_inc(st.sem, st.one())
                    dve.wait_ge(st.sem, st.n)
                    dve.match_replace(ranked[:, :], top[:, 1, :], ranked[:, :], GONE)\
                        .then_inc(st.sem, st.one())
                    dve.wait_ge(st.sem, st.n)
                    dve.tensor_scalar(kept[:, :], ranked[:, P - 1::-1][:, 0:P], PAD, None, ALU.is_gt)\
                        .then_inc(st.sem, st.one())
                    dve.wait_ge(st.sem, st.n)
                    dve.sem_inc(kept_ready, 1)

                def keep_values(it, n):
                    dve.wait_ge(keptT_done, 1)
                    dve.sem_inc(keptT_done, -1)
                    dve.wait_ge(v_ready, 1)
                    dve.sem_inc(v_ready, -1)
                    dve.tensor_tensor(v_kept[:, n // 4, :, :], v_wide[:, n // 4, :, :],
                                      bank[5][:, 256:256 + H][:, :, None].broadcast_to([P, H, 32]), ALU.mult)\
                        .then_inc(st.sem, st.one())
                    dve.wait_ge(st.sem, st.n)
                    dve.sem_inc(v_kept_ready, 1)
                    dve.sem_inc(v_free, 1)

                if prune:
                    order = [(maxima, range(8), 0), (inverse_sums, range(8), 1), (rank, (3, 7), 5),
                             (keep_values, (3, 7), 6), (copy_out, (3, 7), 7), (column_sums, range(8), 3)]
                else:
                    order = [(maxima, range(8), 0), (inverse_sums, range(8), 1), (copy_out, (3, 7), 4),
                             (copy_probsT, range(8), 2)]
                st.close()
                pipelined(dve, order, 8, NB // 2, st.close)
                dve.sem_inc(att_ready, 1)

            def attention_output(bias):
                dve.tensor_tensor(x[:, :, :], x[:, :, :], row_b(bias), ALU.add).then_inc(st.sem, st.one())
                dve.wait_ge(st.sem, st.n)
                for half in range(2):
                    dve.wait_ge(y_attn_done, 1)
                    dve.sem_inc(y_attn_done, -1)
                    part = x[:, 4 * half:4 * half + 4, :]
                    dve.tensor_tensor(part, part, b4(2 + half), ALU.add).then_inc(st.sem, st.one())
                dve.wait_ge(st.sem, st.n)

            def wide_attention():
                def queries(it, n):
                    dve.wait_ge(heads_q_done, 1)
                    dve.sem_inc(heads_q_done, -1)
                    at = COLS["bq1"][0] + 4 * (n % 4)
                    dve.tensor_tensor(qh[:, n % 2, :, :], b4(0),
                                      cols[:, at:at + 4][:, :, None].broadcast_to([P, 4, P]), ALU.add)\
                        .then_inc(st.sem, st.one())
                    dve.wait_ge(st.sem, st.n)
                    dve.sem_inc(qh_ready, 1)
                    dve.sem_inc(qh_ready_pool, 1)
                    dve.sem_inc(q_free, 1)

                def maxima(it, n):
                    dve.wait_ge(scores_done, 1)
                    dve.sem_inc(scores_done, -1)
                    own = bank[7][:, 4 * (n % 2):4 * (n % 2) + 4]
                    m = row_max[:, n % 2, :]
                    dve.tensor_reduce(m, b4(1 + n % 2), X_AX, ALU.max).then_inc(st.sem, st.one())
                    dve.wait_ge(st.sem, st.n)
                    dve.tensor_tensor(m, m, own, ALU.max).then_inc(st.sem, st.one())
                    dve.wait_ge(st.sem, st.n)
                    dve.tensor_scalar(neg_max[:, n, :], m, -SC1, None, ALU.mult).then_inc(st.sem, st.one())
                    dve.wait_ge(st.sem, st.n)
                    dve.scalar_tensor_tensor(self_arg[:, n % 2, :], own, SC1, neg_max[:, n, :],
                                             ALU.mult, ALU.add).then_inc(st.sem, st.one())
                    dve.wait_ge(st.sem, st.n)
                    dve.sem_inc(neg_max_ready, 1)
                    dve.sem_inc(own_free, 1)

                def weights(it, n):
                    dve.wait_ge(probs_ready_dve, 1)
                    dve.sem_inc(probs_ready_dve, -1)
                    four = slice(4 * (n % 2), 4 * (n % 2) + 4)
                    total, inv = z[:, 1, four], r[:, 0, 4 * (n % 4):4 * (n % 4) + 4]
                    dve.tensor_tensor(total, z[:, 0, four], self_exp[:, n % 2, :], ALU.add)\
                        .then_inc(st.sem, st.one())
                    dve.wait_ge(st.sem, st.n)
                    dve.reciprocal(inv, total).then_inc(st.sem, st.one())
                    dve.wait_ge(st.sem, st.n)
                    dve.tensor_tensor(self_w[:, n % 2, :], self_exp[:, n % 2, :], inv, ALU.mult)\
                        .then_inc(st.sem, st.one())
                    dve.wait_ge(st.sem, st.n)
                    dve.sem_inc(self_w_ready, 1)

                def heads_out(it, n):
                    dve.wait_ge(pv_done, 1)
                    dve.sem_inc(pv_done, -1)
                    dve.wait_ge(mva_ready, 1)
                    dve.sem_inc(mva_ready, -1)
                    for i in range(4):
                        dve.scalar_tensor_tensor(heads[:, n % 2, i, :], b4(4)[:, i, :],
                                                 r[:, 0, 4 * (n % 4) + i:4 * (n % 4) + i + 1],
                                                 mva[:, n % 2, i, :], ALU.mult, ALU.add)\
                            .then_inc(st.sem, st.one())
                    dve.wait_ge(st.sem, st.n)
                    dve.sem_inc(heads_ready, 1)

                def residual(it, n):
                    dve.wait_ge(wo_done, 1)
                    dve.sem_inc(wo_done, -1)
                    b = bass.ds(2 * it + n // 4, 1)
                    dve.tensor_tensor(att[:, b, :], xn[:, b, :], bank[6][:, 0:D][:, None, :], ALU.add)\
                        .then_inc(st.sem, st.one())
                    dve.wait_ge(st.sem, st.n)
                    dve.sem_inc(wo_free, 1)

                st.close()
                pipelined(dve, [(residual, (3, 7), 6), (heads_out, range(8), 4), (weights, range(8), 2),
                                (queries, range(8), 0), (maxima, range(8), 1)], 8, NB // 2, st.close)

            def route(experts, biases, out_weights_sum=False):
                dve.wait_ge(router_done, 1)
                dve.sem_inc(router_done, -1)
                lg = logits[:, :, 0:experts]
                dve.tensor_copy(lg, bank[4][:, 0:NB * experts].rearrange("p (b e) -> p b e", b=NB))\
                    .then_inc(st.sem, st.one())
                for bias in biases:
                    dve.wait_ge(st.sem, st.n)
                    dve.tensor_tensor(lg, lg, row(bias)[:, None, :].broadcast_to([P, NB, experts]), ALU.add)\
                        .then_inc(st.sem, st.one())
                dve.wait_ge(st.sem, st.n)
                for b in range(NB):
                    dve.max(best[:, b, :], logits[:, b, 0:experts]).then_inc(st.sem, st.one())
                dve.wait_ge(st.sem, st.n)
                dve.tensor_tensor(gap[:, :], best[:, :, 1], best[:, :, 0], ALU.subtract)\
                    .then_inc(st.sem, st.one())
                dve.wait_ge(st.sem, st.n)
                dve.sem_inc(gap_ready, 1)
                for b in range(NB):
                    dve.max_index(best_at[:, b, :], best[:, b, :], logits[:, b, 0:experts])\
                        .then_inc(st.sem, st.one())
                dve.wait_ge(st.sem, st.n)
                dve.tensor_copy(best_no[:, :, :], best_at[:, :, 0:2]).then_inc(st.sem, st.one())
                dve.wait_ge(gap_exp_ready, 1)
                dve.sem_inc(gap_exp_ready, -1)
                dve.tensor_scalar(w_a[:, :], gap_exp[:, :], 1.0, None, ALU.add).then_inc(st.sem, st.one())
                dve.wait_ge(st.sem, st.n)
                dve.reciprocal(w_a[:, :], w_a[:, :]).then_inc(st.sem, st.one())
                dve.wait_ge(st.sem, st.n)
                dve.tensor_tensor(w_b[:, :], w_a[:, :], gap_exp[:, :], ALU.mult).then_inc(st.sem, st.one())
                full = [P, NB, experts]
                number = expert_no[:, 0:experts][:, None, :].broadcast_to(full)
                for o, i, weight in ((cw, 0, w_a), (cw_b, 1, w_b)):
                    dve.wait_ge(st.sem, st.n)
                    dve.tensor_tensor(o[:, :, 0:experts], number,
                                      best_no[:, :, i:i + 1].broadcast_to(full), ALU.is_equal)\
                        .then_inc(st.sem, st.one())
                    dve.wait_ge(st.sem, st.n)
                    dve.tensor_tensor(o[:, :, 0:experts], o[:, :, 0:experts],
                                      weight[:, :, None].broadcast_to(full), ALU.mult)\
                        .then_inc(st.sem, st.one())
                dve.wait_ge(st.sem, st.n)
                dve.tensor_tensor(cw[:, :, 0:experts], cw[:, :, 0:experts], cw_b[:, :, 0:experts], ALU.add)\
                    .then_inc(st.sem, st.one())
                dve.wait_ge(st.sem, st.n)
                dve.sem_inc(cw_ready, 1)

            def expert_biases(experts):
                dve.wait_ge(cwT_done, 1)
                dve.sem_inc(cwT_done, -1)
                for half in range(2):
                    dve.tensor_copy(cwT[0:experts, half * 512:(half + 1) * 512],
                                    bank[2 + half][0:experts, :]).then_inc(st.sem, st.one())
                dve.wait_ge(st.sem, st.n)
                dve.sem_inc(cwT_ready, 1)
                dve.wait_ge(bias_done, 1)
                dve.sem_inc(bias_done, -1)
                for half in range(2):
                    part = x[:, 4 * half:4 * half + 4, :]
                    dve.tensor_tensor(part, part, b4(6 + half), ALU.add).then_inc(st.sem, st.one())
                dve.wait_ge(st.sem, st.n)
                dve.sem_inc(bias_free, 1)

            def scaled_input(e, sub):
                dve.tensor_scalar(normed[:, sub, :], kT[:, :], col("gamma0", e), col("beta0", e),
                                  ALU.mult, ALU.add).then_inc(st.sem, st.one())
                dve.wait_ge(st.sem, st.n)
                dve.sem_inc(normed_ready, 1)

            def ffn(f, finish):
                def expert(e, sub):
                    if f is ffn0:
                        scaled_input(e + 1, 1 - sub)
                    if f.gated:
                        for k in range(2 * f.FC):
                            half, fc = divmod(k, f.FC)
                            h = hT[:, half, fc, :]
                            dve.wait_ge(g_done, 1)
                            dve.sem_inc(g_done, -1)
                            if f.up_bias:
                                dve.scalar_tensor_tensor(h, bank[2 + k % 2][:, :], col(f.up_bias, fc), h,
                                                         ALU.add, ALU.mult).then_inc(h_evac, 1)
                            else:
                                dve.tensor_tensor(h, bank[2 + k % 2][:, :], h, ALU.mult)\
                                    .then_inc(h_evac, 1)
                    for half in range(2):
                        dve.wait_ge(y_done, 1)
                        dve.sem_inc(y_done, -1)
                        if half == 1 and f.E > 1:
                            dve.sem_inc(slot_free[sub], 1)
                        finish(e, sub, half)
                        dve.wait_ge(st.sem, st.n)
                        dve.sem_inc(y_free, 1)

                st.close()
                if f.E == 1:
                    expert(0, 0)
                else:
                    with dve.Fori(0, f.E // 2) as i:
                        for sub in range(2):
                            expert(2 * i + sub, sub)
                        st.close()

            def combine(e, sub, half):
                for t in range(4):
                    b = 4 * half + t
                    dve.scalar_tensor_tensor(x[:, b, :], b4(4 + 2 * sub + half)[:, t, :],
                                             cw[:, b, bass.ds(e, 1)], x[:, b, :], ALU.mult, ALU.add)\
                        .then_inc(st.sem, st.one())

            def residual_into(dst):
                def finish(e, sub, half):
                    part = dst[:, 4 * half:4 * half + 4, :]
                    dve.tensor_tensor(part, part, b4(4 + half), ALU.add).then_inc(st.sem, st.one())
                return finish

            dve.wait_ge(x_loaded, 16)
            dve.wait_ge(consts_dve, 1)
            dve.sem_inc(consts_dve, -1)
            dve.wait_ge(cols_loaded, 16)
            dve.wait_ge(rows_loaded, 16)

            copy_projected(kT, 2, "bk0", 1.0)
            copy_values(iv, 4, "bv0")
            layer_norm(x, xn, 1e-5, give=[norm_tok_ready])
            copy_projected(qT, 6, "bq0", SC0)
            dve.wait_ge(st.sem, st.n)
            dve.sem_inc(qkv_ready, 1)
            dve.sem_inc(qkv_ready_pool, 1)
            narrow_attention(False)
            attention_output("bo0")
            layer_norm(x, xn, 1e-5, give=[norm_tok_ready])
            layer_norm(xn, att, 1e-6, give=[norm_tok_ready])
            route(E0, [])
            dve.wait_ge(feat_ready_dve, 1)
            dve.sem_inc(feat_ready_dve, -1)
            scaled_input(0, 0)
            expert_biases(E0)
            dve.tensor_tensor(cw_sum[:, :], w_a[:, :], w_b[:, :], ALU.add).then_inc(st.sem, st.one())
            dve.wait_ge(st.sem, st.n)
            for b in range(NB):
                dve.scalar_tensor_tensor(x[:, b, :], xn[:, b, :], cw_sum[:, b:b + 1], x[:, b, :],
                                         ALU.mult, ALU.add).then_inc(st.sem, st.one())
            ffn(ffn0, combine)
            dve.wait_ge(normed_ready, 1)
            dve.sem_inc(normed_ready, -1)

            copy_projected(kT, 2, "bk1", 1.0)
            copy_values(iv, 4, "bv1")
            layer_norm(x, xn, 1e-5, give=[norm_tok_ready, qkv_ready])
            copy_projected(qT, 2, "bk1", 1.0)
            copy_values(mv, 4, "bv1")
            dve.wait_ge(st.sem, st.n)
            dve.tensor_tensor(xn[:, :, :], xn[:, :, :], row_b("bo1"), ALU.add).then_inc(st.sem, st.one())
            dve.wait_ge(st.sem, st.n)
            dve.sem_inc(qkv_ready, 1)
            wide_attention()
            layer_norm(att, iv, 1e-6, "g1", "be1", give=[norm_tok_ready])
            dve.tensor_tensor(mv[:, :, :], iv[:, :, :], row_b("bm1"), ALU.add).then_inc(st.sem, st.one())
            dve.wait_ge(st.sem, st.n)
            ffn(mlp1, residual_into(mv))
            layer_norm(mv, att, 1e-6, "g2", "be2")
            add_to_x(att[:, :, :])
            layer_norm(x, xn, 1e-5, give=[norm_tok_ready])
            route(E1, ["rbg", "rbias"])
            expert_biases(E1)
            ffn(ffn1, combine)

            copy_projected(kT, 2, "bk2", 1.0)
            copy_values(iv, 4, "bv2")
            layer_norm(x, xn, 1e-5, give=[norm_tok_ready])
            copy_projected(qT, 6, "bq2", SC0)
            dve.wait_ge(st.sem, st.n)
            dve.sem_inc(qkv_ready, 1)
            dve.sem_inc(qkv_ready_pool, 1)
            narrow_attention(True)
            attention_output("bo2")
            layer_norm(x, xn, 1e-5, give=[norm_tok_ready])
            route(E2, [])
            ffn(ffn2, combine)

            layer_norm(x, xn, 1e-5, give=[norm_tok_ready])
            dve.wait_ge(feat_ready_dve, 1)
            dve.sem_inc(feat_ready_dve, -1)
            dve.tensor_scalar(qT[:, :], xnT[:, :], col("w3s"), col("w2s"), ALU.mult, ALU.add)\
                .then_inc(st.sem, st.one())
            dve.wait_ge(st.sem, st.n)
            dve.sem_inc(x3_sim, 1)
            for g in range(2):
                dve.wait_ge(x3_sims, 1)
                dve.sem_inc(x3_sims, -1)
                four = slice(4 * g, 4 * g + 4)
                dve.tensor_reduce(m_sim[:, four], b4(g), X_AX, ALU.max).then_inc(st.sem, st.one())
                dve.wait_ge(st.sem, st.n)
                dve.tensor_scalar(neg_max[:, g, :], m_sim[:, four], -1.0, None, ALU.mult)\
                    .then_inc(st.sem, st.one())
                dve.wait_ge(st.sem, st.n)
                dve.sem_inc(x3_neg, 1)
            dve.tensor_tensor(m_sim[:, :], m_sim[:, :], bank[2][:, 0:NB], ALU.add)\
                .then_inc(st.sem, st.one())
            dve.wait_ge(st.sem, st.n)
            dve.tensor_scalar(m_sim[:, :], m_sim[:, :], row("bsim"), None, ALU.add)\
                .then_inc(st.sem, st.one())
            dve.wait_ge(st.sem, st.n)
            dve.sem_inc(x3_m, 1)
            dve.wait_ge(x3_mT, 1)
            dve.sem_inc(x3_mT, -1)
            dve.tensor_copy(batt[:, :], bank[3][0:NB, 0:P]).then_inc(st.sem, st.one())
            dve.wait_ge(st.sem, st.n)
            dve.tensor_reduce(bstat[:, 0:1], batt[:, :], X_AX, ALU.max, negate=True)\
                .then_inc(st.sem, st.one())
            dve.wait_ge(st.sem, st.n)
            dve.sem_inc(x3_arg, 1)
            for g in range(2):
                dve.wait_ge(x3_t, 1)
                dve.sem_inc(x3_t, -1)
                dve.tensor_copy(probT[:, 0, 4 * g:4 * g + 4, :], b4(4 + g)).then_inc(st.sem, st.one())
                dve.wait_ge(st.sem, st.n)
                dve.sem_inc(x3_te, 1)
            dve.wait_ge(x3_bexp, 1)
            dve.sem_inc(x3_bexp, -1)
            dve.reciprocal(bstat[:, 2:3], bstat[:, 1:2]).then_inc(st.sem, st.one())
            dve.wait_ge(st.sem, st.n)
            dve.tensor_scalar(batt[:, :], batt2[:, :], bstat[:, 2:3], None, ALU.mult)\
                .then_inc(st.sem, st.one())
            dve.reciprocal(r[:, 0, 0:NB], z[:, 0, 0:NB]).then_inc(st.sem, st.one())
            dve.wait_ge(st.sem, st.n)
            dve.sem_inc(x3_b, 1)
            for g in range(2):
                dve.wait_ge(x3_pv, 1)
                dve.sem_inc(x3_pv, -1)
                four = slice(4 * g, 4 * g + 4)
                dve.tensor_tensor(iv[:, four, :], b4(6 + g),
                                  r[:, 0, four][:, :, None].broadcast_to([P, 4, D]), ALU.mult)\
                    .then_inc(st.sem, st.one())
                dve.wait_ge(st.sem, st.n)
                dve.sem_inc(x3_hq, 1)
            dve.wait_ge(x3_bT, 1)
            dve.sem_inc(x3_bT, -1)
            dve.tensor_copy(batt_col[:, :], bank[3][:, 256:256 + NB]).then_inc(st.sem, st.one())
            dve.wait_ge(st.sem, st.n)
            dve.sem_inc(x3_bTe, 1)
            for g in range(2):
                dve.wait_ge(x3_hqT, 1)
                dve.sem_inc(x3_hqT, -1)
                dve.tensor_copy(kT[:, g * 512:(g + 1) * 512], bank[4 + g][:, :]).then_inc(st.sem, st.one())
            dve.wait_ge(x3_hc, 1)
            dve.sem_inc(x3_hc, -1)
            dve.tensor_copy(hc_bar[:, :], bank[2][:, 16:16 + NB]).then_inc(st.sem, st.one())
            dve.wait_ge(st.sem, st.n)
            dve.tensor_tensor(normed[:, 0, :], xnT[:, :], kT[:, :], ALU.mult).then_inc(st.sem, st.one())
            dve.tensor_tensor(normed[:, 1, :].rearrange("p (b t) -> p b t", b=NB),
                              xnT[:, :].rearrange("p (b t) -> p b t", b=NB),
                              hc_bar[:, :, None].broadcast_to([D, NB, P]), ALU.mult)\
                .then_inc(st.sem, st.one())
            dve.wait_ge(st.sem, st.n)
            dve.sem_inc(x3_feats, 1)
            dve.wait_ge(x3_outT, 1)
            dve.sem_inc(x3_outT, -1)
            for half in range(2):
                part = x[:, 4 * half:4 * half + 4, :]
                dve.tensor_tensor(part, part, b4(2 + half), ALU.add).then_inc(st.sem, st.one())

            layer_norm(x, xn, 1e-5, give=[norm_tok_ready])
            dve.tensor_tensor(mv[:, :, :], xn[:, :, :], row_b("b2_3"), ALU.add).then_inc(st.sem, st.one())
            dve.wait_ge(st.sem, st.n)
            ffn(ffn3, residual_into(mv))
            layer_norm(mv, att, 1e-5, "g3", "be3")
            add_to_x(att[:, :, :])
            dve.sem_inc(store_done, 1)


def kernel(**inputs):
    import numpy as np
    import concourse.bacc as _bacc
    from concourse import mybir as _mybir
    from concourse.bass_utils import run_bass_kernel_spmd as _run

    g = {k: np.asarray(v) for k, v in inputs.items()}
    lay = np.ascontiguousarray

    def chunks(a):
        return a.reshape(-1, P).T

    def weights(a):
        e, k, m = a.shape
        return a.reshape(e, k // P, P, m).transpose(0, 2, 1, 3).reshape(e, P, -1)

    ws = g["L3_xattn_w_sim"]
    beta0 = g["L0_ffn_beta"]
    cols = np.concatenate([
        chunks(g["L0_xattn_wq_b"]), chunks(g["L0_xattn_wk_b"]), chunks(g["L0_ffn_gamma"]),
        chunks(beta0), chunks(beta0[0]), chunks(g["L0_ffn_b1"]), chunks(g["L1_xattn_bk"]),
        chunks(g["L1_xattn_bq"]), chunks(g["L1_xattn_bg"]), chunks(g["L1_xattn_bl"]), chunks(g["L1_ffn_b1"]),
        chunks(g["L2_xattn_bq"]), chunks(g["L2_xattn_bk"]), chunks(ws[:D]), chunks(ws[D:2 * D]),
        chunks(ws[2 * D:]), chunks(g["L3_xattn_b_qv"]), chunks(g["L3_ffn_b1"][0])], axis=1)
    rows = np.concatenate([g[n].reshape(-1) for n in (
        "L0_xattn_wv_b", "L0_xattn_wo_b", "L1_xattn_bv", "L1_xattn_bo", "L1_xattn_bm", "L1_xattn_g1",
        "L1_xattn_b1", "L1_xattn_g2", "L1_xattn_b2", "L2_xattn_bv", "L2_xattn_bo")] + [
        g["L3_ffn_b2"][0], g["L3_ffn_gamma"], g["L3_ffn_beta"], g["L1_ffn_bg"], g["L1_ffn_bias"],
        g["L3_xattn_b_sim"]]).reshape(1, -1)
    sq = np.concatenate([
        g["L0_xattn_wq_w"].T, g["L0_xattn_wk_w"].T, g["L0_xattn_wv_w"].T, g["L0_xattn_wo_w"].T,
        g["L0_ffn_Wg"], g["L1_xattn_Wk"], g["L1_xattn_Wv"], g["L1_ffn_Wg"], g["L2_xattn_Wq"].T,
        g["L2_xattn_Wk"].T, g["L2_xattn_Wv"].T, g["L2_xattn_Wo"].T, g["L2_ffn_router_w"].T,
        weights(g["L3_xattn_W_qv"][None])[0]], axis=1)
    arrays = {
        "x_in": g["x"].transpose(1, 0, 2),
        "ctx_in": g["ctx_1024"].transpose(1, 0, 2),
        "ctxT_in": g["ctx_1024"].reshape(T, D).T,
        "cols_in": cols, "rows_in": rows, "sq_in": sq,
        "w0_in": np.concatenate([g["L0_ffn_W1"], weights(g["L0_ffn_W2"])], axis=2),
        "w1q_in": g["L1_xattn_Wq"].transpose(1, 0, 2),
        "w1o_in": g["L1_xattn_Wo"].reshape(H, D, D).transpose(1, 0, 2),
        "w1m_in": np.concatenate([g["L1_xattn_Wg"], g["L1_xattn_Wl"], weights(g["L1_xattn_Wm"][None])[0]], axis=1),
        "w1_in": np.concatenate([g["L1_ffn_W1"], weights(g["L1_ffn_W2"])], axis=2),
        "w2_in": np.concatenate([g["L2_ffn_w_gate"], g["L2_ffn_w_up"], weights(g["L2_ffn_w_down"])], axis=2),
        "w3_in": np.concatenate([g["L3_ffn_w1"][0], weights(g["L3_ffn_w2"][0:1])[0]], axis=1),
        "b2_0_in": g["L0_ffn_b2"], "b2_1_in": g["L1_ffn_b2"],
    }
    arrays = {k: lay(v) for k, v in arrays.items()}
    nc = _bacc.Bacc("TRN2", target_bir_lowering=False, num_devices=1)
    args = [nc.dram_tensor(k, v.shape, _mybir.dt.from_np(v.dtype), kind="ExternalInput").ap()
            for k, v in arrays.items()]
    out = nc.dram_tensor("out_dram", (P, NB, D), _mybir.dt.float32, kind="ExternalOutput").ap()
    build(nc, *args, out)
    result = _run(nc, [arrays], core_ids=[0])
    return result.results[0]["out_dram"].transpose(1, 0, 2)
```

```python
import concourse.bass as bass
from concourse import mybir
from contextlib import ExitStack

NB, P, D = 8, 128, 128
T = NB * P
H = 16
DH = D // H
E0, F0 = 8, 512
E1, F1 = 16, 256
E2, F2 = 8, 512
F3 = 512
FM = 512
KEEP = int(P * 0.9)
DROP = P - KEEP
assert 8 < DROP <= 16

COLS, ROWS, SQS = {}, {}, {}


def _place(table, names):
    at = 0
    for name, n in names:
        table[name] = (at, n)
        at += n
    table["end"] = at


_place(COLS, [("bq0", 1), ("bk0", 1), ("gamma0", E0), ("beta0", E0 + 1), ("b1_0", E0 * F0 // P),
              ("bk1", 1), ("bq1", H), ("bg1", FM // P), ("bl1", FM // P), ("b1_1", E1 * F1 // P),
              ("bq2", 1), ("bk2", 1), ("w1s", 1), ("w2s", 1), ("w3s", 1), ("bqv", 1), ("b1_3", F3 // P)])
_place(ROWS, [("bv0", D), ("bo0", D), ("bv1", D), ("bo1", D), ("bm1", D), ("g1", D), ("be1", D),
              ("g2", D), ("be2", D), ("bv2", D), ("bo2", D), ("b2_3", D), ("g3", D), ("be3", D),
              ("rbg", E1), ("rbias", E1), ("bsim", 1)])
_place(SQS, [("wq0", D), ("wk0", D), ("wv0", D), ("wo0", D), ("r0", E0), ("wk1", D), ("wv1", D),
             ("r1", E1), ("wq2", D), ("wk2", D), ("wv2", D), ("wo2", D), ("r2", E2), ("wqv", 4 * D)])


def stages(order, groups, current, previous):
    for step in range(groups):
        for stage, positions, lag in order:
            for back, on in ((0, current), (1, previous)):
                n = step - lag + back * groups
                if on and n in positions and 0 <= n < groups:
                    yield stage, n, back


def pipelined(eng, order, groups, iterations, close):
    for stage, n, back in stages(order, groups, True, False):
        stage(0, n)
    close()
    with eng.Fori(1, iterations) as it:
        for stage, n, back in stages(order, groups, True, True):
            stage(it - back, n)
        close()
    for stage, n, back in stages(order, groups, False, True):
        stage(iterations - 1, n)
    close()


class Steps:

    def __init__(self, eng, sem):
        self.eng, self.sem, self.n = eng, sem, 0

    def one(self):
        self.n += 1
        return 1

    def close(self):
        if self.n:
            self.eng.wait_ge(self.sem, self.n)
            self.eng.sem_inc(self.sem, -self.n)
            self.n = 0


def build(nc, x_in, ctx_in, ctxT_in, cols_in, rows_in, sq_in, w0_in, w1q_in, w1o_in, w1m_in, w1_in,
          w2_in, w3_in, b2_0_in, b2_1_in, out):
    F32 = mybir.dt.float32
    F32R = mybir.dt.float32r
    U32 = mybir.dt.uint32
    ALU = mybir.AluOpType
    ACT = mybir.ActivationFunctionType
    X_AX = mybir.AxisListType.X

    ctx = ExitStack()
    with ctx:
        def sb(name, shape, dt=F32):
            return ctx.enter_context(nc.sbuf_tensor(name, shape, dt))

        def sem(name):
            return ctx.enter_context(nc.semaphore(name))

        x = sb("x_tok", [P, NB, D])
        xn = sb("xn_tok", [P, NB, D])
        xnT = sb("xn_feat", [D, T])
        ctxT = sb("ctx_feat", [D, T])
        kT = sb("keys_feat", [D, T])
        qT = sb("queries_feat", [D, T])
        iv = sb("values_ctx", [P, NB, D])
        mv = sb("values_state", [P, NB, D])
        ctx_tok = mv
        att = sb("att_tok", [P, NB, D])
        attT = sb("att_feat", [D, T])
        prob = sb("probabilities", [P, 2, H, P])
        probT = sb("probabilities_keys", [P, 2, H, P])
        scratch = sb("scratch", [P, 10, 512])

        def part(at, **sizes):
            return scratch[:, at:at + 2, :].rearrange("p a (h t) -> p a h t", **sizes)

        q_b = scratch[:, 6, 0:2 * P].rearrange("p (a t) -> p a t", a=2)
        k_mask = part(0, t=P)
        head_mask = sb("head_mask", [P, 4])
        slot_mask = sb("slot_mask", [P, 4, 32])
        v_wide = part(2, t=32)
        v_kept = part(4, t=32)
        qh = part(0, t=P)
        qmk = part(2, t=P)
        mva = part(4, t=D)
        heads = part(6, t=D)
        headsT = part(8, t=P)
        hT = sb("hidden", [P, 2, 4, 512])
        normed = sb("expert_input", [D, 2, T])
        w_in = sb("weights_in", [P, 1024])
        w_hi = sb("weights_in_hi", [P, 2, 1024], F32R)
        w_lo = sb("weights_in_lo", [P, 2, 1024], F32R)
        w_out = sb("weights_out", [P, 2, 512])
        in_hi = sb("input_hi", [D, 2, T], F32R)
        in_lo = sb("input_lo", [D, 2, T], F32R)
        cols = sb("cols", [P, COLS["end"]])
        rows = sb("rows", [P, ROWS["end"]])
        sq = sb("square_weights", [D, SQS["end"]])
        wq1 = sb("wq1", [D, H, D])
        wo1 = sb("wo1", [D, H, D])
        b2_0 = sb("b2_0", [E0, D])
        b2_1 = sb("b2_1", [E1, D])
        ident = sb("identity", [P, P])
        ones = sb("ones", [P, 1])
        neg_half = sb("neg_half", [P, NB])
        expert_no = sb("expert_number", [P, E1])
        stats = sb("stats", [P, NB, 6])
        mean_var = sb("mean_var", [P, NB, 2])
        var_eps = sb("var_eps", [P, NB])
        rstd = sb("rstd", [P, NB])
        neg_max = sb("neg_max", [P, 8, 4])
        row_max = sb("row_max", [P, 2, 4])
        z = sb("exp_sums", [P, 2, H])
        r = sb("inverse_sums", [P, 2, H])
        self_arg = sb("self_arg", [P, 2, 4])
        self_exp = sb("self_exp", [P, 2, 4])
        self_w = sb("self_weight", [P, 2, 4])
        col_sum = sb("column_sums", [P, 2, H])
        ranked = sb("ranked", [H, P + 8])
        top = sb("top", [H, 2, 8])
        kept = sb("kept", [H, P])
        logits = sb("logits", [P, NB, E1])
        best = sb("best", [P, NB, 8])
        best_at = sb("best_at", [P, NB, 8], U32)
        best_no = sb("best_number", [P, NB, 2])
        gap = sb("gap", [P, NB])
        gap_exp = sb("gap_exp", [P, NB])
        w_a = sb("weight_first", [P, NB])
        w_b = sb("weight_second", [P, NB])
        cw = sb("combine_weights", [P, NB, E1])
        cw_b = sb("combine_weights_second", [P, NB, E1])
        cw_sum = sb("combine_sum", [P, NB])
        cwT = kT[0:E1, :]
        m_sim = sb("row_maxima", [P, NB])
        batt = probT[0:NB, 1, 8, :]
        batt2 = probT[0:NB, 1, 9, :]
        bstat = sb("row_weights_stats", [NB, 4])
        batt_col = sb("row_weights", [P, NB])
        hc_bar = sb("hc_bar", [D, NB])

        def col(name, i=0, n=1):
            at = COLS[name][0] + i
            return cols[:, bass.ds(at, n)] if not isinstance(at, int) else cols[:, at:at + n]

        def row(name):
            at, n = ROWS[name]
            return rows[:, at:at + n]

        def row_b(name):
            return row(name)[:, None, :].broadcast_to([P, NB, D])

        def w(name, i=0, n=None):
            at, size = SQS[name]
            return sq[:, at + i:at + i + (n or size)]

        bank = [ctx.enter_context(nc.psum_tensor(f"bank{i}", [P, 512], F32)) for i in range(8)]

        def b4(i):
            return bank[i][:, :].rearrange("p (a b) -> p a b", a=4)

        x_loaded = sem("x_loaded")
        ctx_loaded = sem("ctx_loaded")
        cols_loaded = sem("cols_loaded")
        rows_loaded = sem("rows_loaded")
        sq_loaded = sem("sq_loaded")
        w1_attn_loaded = sem("w1_attn_loaded")
        ctx_tok_loaded = sem("ctx_tok_loaded")
        b2_loaded = sem("b2_loaded")
        w_in_loaded = sem("w_in_loaded")
        w_loaded_free = sem("w_loaded_free")
        w_out_loaded = [sem("w_out_loaded0"), sem("w_out_loaded1")]
        consts_dve = sem("consts_dve")
        consts_pe = sem("consts_pe")
        dve_steps = sem("dve_steps")
        act_steps = sem("act_steps")
        pool_steps = sem("pool_steps")
        var_ready = sem("var_ready")
        rstd_ready = sem("rstd_ready")
        norm_tok_ready = sem("norm_tok_ready")
        transposed = sem("transposed")
        feat_ready = sem("feat_ready")
        feat_ready_dve = sem("feat_ready_dve")
        projected = sem("projected")
        qkv_ready = sem("qkv_ready")
        qkv_ready_pool = sem("qkv_ready_pool")
        qk_ready = sem("qk_ready")
        qk_free = sem("qk_free")
        scores_done = sem("scores_done")
        neg_max_ready = sem("neg_max_ready")
        probs_ready = sem("probs_ready")
        probsT_done = sem("probsT_done")
        probsT_ready = sem("probsT_ready")
        out_done = sem("out_done")
        out_free = sem("out_free")
        inv_ready = sem("inv_ready")
        colsum_done = sem("colsum_done")
        colsum_ready = sem("colsum_ready")
        ranked_done = sem("ranked_done")
        kept_ready = sem("kept_ready")
        keptT_done = sem("keptT_done")
        v_kept_ready = sem("v_kept_ready")
        att_ready = sem("att_ready")
        exps_done = sem("exps_done")
        scores_free = sem("scores_free")
        inverse_ready = sem("inverse_ready")
        turn_free = sem("turn_free")
        v_free = sem("v_free")
        v_ready = sem("v_ready")
        probsT_copied = sem("probsT_copied")
        y_attn_done = sem("y_attn_done")
        heads_q_done = sem("heads_q_done")
        q_free = sem("q_free")
        qh_ready = sem("qh_ready")
        qh_ready_pool = sem("qh_ready_pool")
        qmk_ready = sem("qmk_ready")
        probs_ready_dve = sem("probs_ready_dve")
        self_w_ready = sem("self_w_ready")
        mva_ready = sem("mva_ready")
        pv_done = sem("pv_done")
        own_free = sem("own_free")
        heads_ready = sem("heads_ready")
        headsT_done = sem("headsT_done")
        headsT_ready = sem("headsT_ready")
        wo_done = sem("wo_done")
        wo_free = sem("wo_free")
        router_done = sem("router_done")
        gap_ready = sem("gap_ready")
        gap_exp_ready = sem("gap_exp_ready")
        cw_ready = sem("cw_ready")
        cwT_done = sem("cwT_done")
        cwT_ready = sem("cwT_ready")
        bias_done = sem("bias_done")
        bias_free = sem("bias_free")
        input_ready = sem("input_ready")
        h_done = sem("h_done")
        g_done = sem("g_done")
        h_ready = sem("h_ready")
        input_hi_ready = sem("input_hi_ready")
        w_in_ready = [sem("w_in_ready0"), sem("w_in_ready1")]
        w_in_free = [sem("w_in_free0"), sem("w_in_free1")]
        w_out_free = [sem("w_out_free0"), sem("w_out_free1")]
        y_done = sem("y_done")
        y_free = sem("y_free")
        store_done = sem("store_done")
        x3_sim = sem("x3_sim")
        x3_sims = sem("x3_sims")
        x3_neg = sem("x3_neg")
        x3_exp = sem("x3_exp")
        x3_t = sem("x3_t")
        x3_te = sem("x3_te")
        x3_pv = sem("x3_pv")
        x3_hq = sem("x3_hq")
        x3_hqT = sem("x3_hqT")
        x3_m = sem("x3_m")
        x3_mT = sem("x3_mT")
        x3_arg = sem("x3_arg")
        x3_bexp = sem("x3_bexp")
        x3_b = sem("x3_b")
        x3_bT = sem("x3_bT")
        x3_bTe = sem("x3_bTe")
        x3_hc = sem("x3_hc")
        x3_feats = sem("x3_feats")
        x3_out = sem("x3_out")
        x3_oute = sem("x3_oute")
        x3_outT = sem("x3_outT")

        block = ctx.enter_context(nc.Block())

        SC0 = float(DH) ** -0.5
        SC1 = float(D) ** -0.5
        PAD, GONE = -1.0e30, -3.0e38

        LOW, HIGH = 0, 1

        class FFN:
            def __init__(self, experts, width, gated, first, bias, up_bias):
                self.E, self.FC, self.gated = experts, width // P, gated
                self.first, self.bias, self.up_bias = first, bias, up_bias

            def w1(self, part, sub, fc):
                return part[:, sub, fc * P:(fc + 1) * P]

            def up(self, part, sub, fc):
                at = self.FC * P + fc * P
                return part[:, sub, at:at + P]

            def w2(self, sub, fc):
                return w_out[:, sub, fc * D:(fc + 1) * D]

            def in_columns(self):
                return (2 if self.gated else 1) * self.FC * P

            def columns(self):
                return self.in_columns() + self.FC * D

            def hidden_bank(self, n, k):
                return k % 3 if self.gated else (self.FC * n + k) % 4

            def output_bank(self, n):
                return 6 + n % 2 if self.gated else 4 + n

        ffn0 = FFN(E0, F0, False, ACT.Relu, "b1_0", None)
        mlp1 = FFN(1, FM, True, ACT.Relu, "bg1", "bl1")
        ffn1 = FFN(E1, F1, False, ACT.Relu, "b1_1", None)
        ffn2 = FFN(E2, F2, True, ACT.Silu, None, None)
        ffn3 = FFN(1, F3, False, ACT.Relu, "b1_3", None)

        def halves(eng, order, f, close, between=None, between_at=0):
            groups, iterations = (2, 1) if f.E == 1 else (4, f.E // 2)
            last = order[-1][0]
            for stage, n, back in stages(order, groups, True, False):
                if between and stage is last and n == between_at:
                    between()
                stage(0, n)
            close()
            if iterations > 1:
                with eng.Fori(1, iterations) as i:
                    for stage, n, back in stages(order, groups, True, True):
                        stage(i - back, n)
                    close()
            for stage, n, back in stages(order, groups, False, True):
                stage(iterations - 1, n)
            close()

        @block.sync
        def _(sp):
            sp.dma_start(x[:, :, :], x_in).then_inc(x_loaded, 16)
            sp.dma_start(ctxT[:, :], ctxT_in).then_inc(ctx_loaded, 16)
            sp.dma_start(sq[:, :], sq_in).then_inc(sq_loaded, 16)
            sp.dma_start(cols[:, :], cols_in).then_inc(cols_loaded, 16)
            sp.dma_start(rows[:, :], rows_in.broadcast_to([P, ROWS["end"]])).then_inc(rows_loaded, 16)
            sp.dma_start(b2_0[:, :], b2_0_in).then_inc(b2_loaded, 16)
            sp.dma_start(b2_1[:, :], b2_1_in).then_inc(b2_loaded, 16)
            sp.sem_inc(w_loaded_free, 1)
            for sub in range(2):
                sp.sem_inc(w_out_free[sub], 1)

            def load_weights(source, f, sub):
                cut, end = f.in_columns(), f.columns()
                sp.wait_ge(w_loaded_free, 1)
                sp.sem_inc(w_loaded_free, -1)
                sp.dma_start(w_in[:, 0:cut], source[:, 0:cut]).then_inc(w_in_loaded, 16)
                sp.wait_ge(w_out_free[sub], 1)
                sp.sem_inc(w_out_free[sub], -1)
                sp.dma_start(w_out[:, sub, 0:end - cut], source[:, cut:end]).then_inc(w_out_loaded[sub], 16)

            def load_experts(source, f):
                with sp.Fori(0, f.E // 2) as i:
                    for sub in range(2):
                        load_weights(source[bass.ds(2 * i + sub, 1), :, :]
                                     .rearrange("e p n -> p (e n)"), f, sub)

            load_experts(w0_in, ffn0)
            sp.dma_start(wq1[:, :, :], w1q_in).then_inc(w1_attn_loaded, 16)
            sp.dma_start(wo1[:, :, :], w1o_in).then_inc(w1_attn_loaded, 16)
            load_weights(w1m_in, mlp1, 0)
            load_experts(w1_in, ffn1)
            sp.dma_start(ctx_tok[:, :, :], ctx_in).then_inc(ctx_tok_loaded, 16)
            load_experts(w2_in, ffn2)
            load_weights(w3_in, ffn3, 0)
            sp.wait_ge(store_done, 1)
            sp.sem_inc(store_done, -1)
            sp.dma_start(out, x[:, :, :]).then_inc(store_done, 16)
            sp.wait_ge(store_done, 16)

        @block.gpsimd
        def _(pool):
            st = Steps(pool, pool_steps)
            pool.memset(ident[:, :], 0.0).then_inc(st.sem, st.one())
            pool.memset(head_mask[:, :], 1.0).then_inc(st.sem, st.one())
            pool.memset(neg_half[:, :], -0.5).then_inc(st.sem, st.one())
            pool.memset(ones[:, :], 1.0).then_inc(st.sem, st.one())
            pool.memset(slot_mask[:, :, :], 1.0).then_inc(st.sem, st.one())
            pool.iota(expert_no[:, :], [[1, E1]], base=0, channel_multiplier=0,
                      allow_small_or_imprecise_dtypes=True).then_inc(st.sem, st.one())
            pool.wait_ge(st.sem, st.n)
            pool.affine_select(out=ident[:, :], in_=ident[:, :], compare_op=ALU.not_equal,
                               fill=1.0, base=0, pattern=[[-1, P]], channel_multiplier=1)\
                .then_inc(st.sem, st.one())
            pool.affine_select(out=slot_mask[:, :, :], in_=slot_mask[:, :, :], compare_op=ALU.is_ge, fill=0.0,
                               base=0, pattern=[[-DH, 4], [1, 32]], channel_multiplier=0)\
                .then_inc(st.sem, st.one())
            pool.wait_ge(st.sem, st.n)
            pool.affine_select(out=slot_mask[:, :, :], in_=slot_mask[:, :, :], compare_op=ALU.is_ge, fill=0.0,
                               base=DH - 1, pattern=[[DH, 4], [-1, 32]], channel_multiplier=0)\
                .then_inc(st.sem, st.one())
            for g in range(4):
                m = head_mask[32 * g:32 * g + 32, :]
                pool.wait_ge(st.sem, st.n)
                pool.affine_select(out=m, in_=m, compare_op=ALU.is_ge, fill=0.0, base=0,
                                   pattern=[[-DH, 4]], channel_multiplier=1).then_inc(st.sem, st.one())
                pool.wait_ge(st.sem, st.n)
                pool.affine_select(out=m, in_=m, compare_op=ALU.is_ge, fill=0.0, base=DH - 1,
                                   pattern=[[DH, 4]], channel_multiplier=-1).then_inc(st.sem, st.one())
            pool.wait_ge(st.sem, st.n)
            pool.sem_inc(consts_pe, 1)
            pool.sem_inc(consts_dve, 1)
            st.close()

            def inverse_roots():
                pool.wait_ge(var_ready, 1)
                pool.sem_inc(var_ready, -1)
                pool.tensor_tensor(rstd[:, :], var_eps[:, :], neg_half[:, :], ALU.pow)\
                    .then_inc(rstd_ready, 1)

            def narrow_attention():
                pool.wait_ge(qkv_ready_pool, 1)
                pool.sem_inc(qkv_ready_pool, -1)

                def spread_queries_keys(it, n):
                    pool.wait_ge(qk_free, 1)
                    pool.sem_inc(qk_free, -1)
                    tok = bass.ds((2 * it + n // 4) * P, P)
                    pool.tensor_copy(q_b[:, n // 4, :], qT[:, tok]).then_inc(st.sem, st.one())
                    pool.tensor_tensor(k_mask[:, n // 4, :, :],
                                       kT[:, tok][:, None, :].broadcast_to([D, 4, P]),
                                       head_mask[:, :, None].broadcast_to([D, 4, P]), ALU.mult)\
                        .then_inc(st.sem, st.one())
                    pool.wait_ge(st.sem, st.n)
                    pool.sem_inc(qk_ready, 1)

                def spread_values(it, n):
                    pool.wait_ge(v_free, 1)
                    pool.sem_inc(v_free, -1)
                    four = [P, 4, 4, 32]
                    v_b = iv[:, bass.ds(2 * it + n // 4, 1), :].rearrange("p b (j c) -> p (b j) c", j=4)
                    pool.tensor_tensor(v_wide[:, n // 4, :, :].rearrange("p (j i) c -> p j i c", j=4),
                                       v_b[:, :, None, :].broadcast_to(four),
                                       slot_mask[:, None, :, :].broadcast_to(four), ALU.mult)\
                        .then_inc(v_ready, 1)

                def normalise(it, n):
                    pool.wait_ge(inverse_ready, 1)
                    pool.sem_inc(inverse_ready, -1)
                    h = slice(4 * (n % 4), 4 * (n % 4) + 4)
                    pool.tensor_tensor(prob[:, n // 4, h, :], prob[:, n // 4, h, :],
                                       r[:, n // 4, h][:, :, None].broadcast_to([P, 4, P]), ALU.mult)\
                        .then_inc(probs_ready, 1)

                for sub in range(2):
                    pool.sem_inc(qk_free, 1)
                    pool.sem_inc(v_free, 1)
                pipelined(pool, [(spread_queries_keys, (0, 4), 0), (spread_values, (0, 4), 2),
                                 (normalise, range(8), 3)], 8, NB // 2, st.close)
                pool.wait_ge(qk_free, 2)
                pool.sem_inc(qk_free, -2)
                pool.wait_ge(v_free, 2)
                pool.sem_inc(v_free, -2)

            def split_weights(f, sub):
                n = slice(0, f.in_columns())
                pool.wait_ge(w_in_loaded, 16)
                pool.sem_inc(w_in_loaded, -16)
                pool.wait_ge(w_in_free[sub], 1)
                pool.sem_inc(w_in_free[sub], -1)
                pool.tensor_scalar(w_hi[:, sub, n], w_in[:, n], 1.0, None, ALU.mult)\
                    .then_inc(st.sem, st.one())
                pool.wait_ge(st.sem, st.n)
                pool.tensor_tensor(w_lo[:, sub, n], w_in[:, n], w_hi[:, sub, n], ALU.subtract)\
                    .then_inc(st.sem, st.one())
                pool.wait_ge(st.sem, st.n)
                pool.sem_inc(w_in_ready[sub], 1)
                pool.sem_inc(w_loaded_free, 1)
                st.close()

            def split_other_experts(f):
                split_weights(f, 1)
                with pool.Fori(1, f.E // 2):
                    for sub in range(2):
                        split_weights(f, sub)

            def wide_attention():
                def self_products(it, n):
                    pool.wait_ge(qh_ready_pool, 1)
                    pool.sem_inc(qh_ready_pool, -1)
                    tok = bass.ds((2 * it + n // 4) * P, P)
                    pool.tensor_tensor(qmk[:, n % 2, :, :], qh[:, n % 2, :, :],
                                       qT[:, tok][:, None, :].broadcast_to([P, 4, P]), ALU.mult)\
                        .then_inc(qmk_ready, 1)

                def self_values(it, n):
                    pool.wait_ge(self_w_ready, 1)
                    pool.sem_inc(self_w_ready, -1)
                    pool.tensor_tensor(mva[:, n % 2, :, :],
                                       mv[:, bass.ds(2 * it + n // 4, 1), :].broadcast_to([P, 4, D]),
                                       self_w[:, n % 2, :, None].broadcast_to([P, 4, D]), ALU.mult)\
                        .then_inc(mva_ready, 1)

                pipelined(pool, [(self_values, range(8), 2), (self_products, range(8), 0)],
                          8, NB // 2, lambda: None)

            for sub in range(2):
                pool.sem_inc(w_in_free[sub], 1)
            inverse_roots()
            narrow_attention()
            split_weights(ffn0, 0)
            inverse_roots()
            inverse_roots()
            split_other_experts(ffn0)
            inverse_roots()
            split_weights(mlp1, 0)
            wide_attention()
            inverse_roots()
            inverse_roots()
            inverse_roots()
            split_weights(ffn1, 0)
            split_other_experts(ffn1)
            inverse_roots()
            narrow_attention()
            split_weights(ffn2, 0)
            inverse_roots()
            split_other_experts(ffn2)
            inverse_roots()
            split_weights(ffn3, 0)
            inverse_roots()
            inverse_roots()

        @block.scalar
        def _(act):
            st = Steps(act, act_steps)

            def evacuate_transposed(dst, also=(), split=False):
                for half in range(2):
                    act.wait_ge(transposed, 1)
                    act.sem_inc(transposed, -1)
                    act.activation(dst[:, half * 512:(half + 1) * 512], bank[half][:, :], ACT.Copy)\
                        .then_inc(st.sem, st.one())
                act.wait_ge(st.sem, st.n)
                act.sem_inc(feat_ready, 1)
                if split:
                    act.activation(in_hi[:, 0, :], dst[:, :], ACT.Copy).then_inc(input_hi_ready, 1)
                for token in also:
                    act.sem_inc(token, 1)
                st.close()

            def narrow_attention(prune):
                def exps(it, n):
                    act.wait_ge(neg_max_ready, 1)
                    act.sem_inc(neg_max_ready, -1)
                    for i in range(4):
                        h = 4 * (n % 4) + i
                        act.activation(prob[:, n // 4, h, :], b4(n % 2)[:, i, :], ACT.Exp,
                                       bias=neg_max[:, n, i:i + 1], accum_out=z[:, n // 4, h:h + 1])\
                            .then_inc(exps_done, 1)

                def copy_probsT(it, n):
                    act.wait_ge(probsT_done, 1)
                    act.sem_inc(probsT_done, -1)
                    h = 4 * (n % 4)
                    act.activation(probT[:, n // 4, h:h + 4, :], b4(2 + n % 2), ACT.Copy)\
                        .then_inc(st.sem, st.one())
                    act.wait_ge(st.sem, st.n)
                    act.sem_inc(probsT_ready, 1)
                    act.sem_inc(turn_free, 1)
                    act.sem_inc(probsT_copied, 1)

                if prune:
                    pipelined(act, [(exps, range(8), 0), (copy_probsT, range(8), 2)], 8, NB // 2, st.close)
                else:
                    pipelined(act, [(exps, range(8), 0)], 8, NB // 2, lambda: None)

            def wide_attention():
                def copy_probsT(it, n):
                    act.wait_ge(probsT_done, 1)
                    act.sem_inc(probsT_done, -1)
                    act.activation(probT[:, 0, 4 * (n % 2):4 * (n % 2) + 4, :], b4(3), ACT.Copy)\
                        .then_inc(probsT_ready, 1)

                def copy_headsT(it, n):
                    act.wait_ge(headsT_done, 1)
                    act.sem_inc(headsT_done, -1)
                    act.activation(headsT[:, n % 2, :, :], b4(5), ACT.Copy).then_inc(headsT_ready, 1)

                def exps(it, n):
                    act.wait_ge(neg_max_ready, 1)
                    act.sem_inc(neg_max_ready, -1)
                    for i in range(4):
                        act.activation(prob[:, 0, 4 * (n % 2) + i, :], b4(1 + n % 2)[:, i, :],
                                       ACT.Exp, bias=neg_max[:, n, i:i + 1], scale=SC1,
                                       accum_out=z[:, 0, 4 * (n % 2) + i:4 * (n % 2) + i + 1])\
                            .then_inc(st.sem, st.one())
                    act.activation(self_exp[:, n % 2, :], self_arg[:, n % 2, :], ACT.Exp)\
                        .then_inc(st.sem, st.one())
                    act.wait_ge(st.sem, st.n)
                    act.sem_inc(probs_ready, 1)
                    act.sem_inc(probs_ready_dve, 1)

                pipelined(act, [(copy_headsT, range(8), 5), (copy_probsT, range(8), 3), (exps, range(8), 1)],
                          8, NB // 2, st.close)

            def router_exp():
                act.wait_ge(gap_ready, 1)
                act.sem_inc(gap_ready, -1)
                act.activation(gap_exp[:, :], gap[:, :], ACT.Exp).then_inc(gap_exp_ready, 1)

            def ffn(f):
                def hidden(i, n):
                    half, e = n % 2, 2 * i + n // 2
                    for fc in range(f.FC):
                        act.wait_ge(h_done, 1)
                        act.sem_inc(h_done, -1)
                        kw = {"bias": col(f.bias, e * f.FC + fc)} if f.bias else {}
                        act.activation(hT[:, half, fc, :], bank[f.hidden_bank(n, fc)][:, :], f.first, **kw)\
                            .then_inc(g_done if f.gated else h_ready, 1)
                    if half == 1:
                        act.sem_inc(w_in_free[n // 2], 1)

                order = [(hidden, range(4), 0)]
                halves(act, order, f, st.close, router_exp if f.E > 1 else None, 2)

            act.wait_ge(cols_loaded, 16)
            evacuate_transposed(xnT)
            narrow_attention(False)
            evacuate_transposed(xnT)
            evacuate_transposed(kT, also=[feat_ready_dve])
            ffn(ffn0)
            evacuate_transposed(xnT)
            wide_attention()
            evacuate_transposed(xnT, split=True)
            ffn(mlp1)
            evacuate_transposed(xnT, split=True)
            ffn(ffn1)
            evacuate_transposed(xnT)
            narrow_attention(True)
            evacuate_transposed(xnT, split=True)
            ffn(ffn2)
            evacuate_transposed(xnT, also=[feat_ready_dve])
            for g in range(2):
                act.wait_ge(x3_neg, 1)
                act.sem_inc(x3_neg, -1)
                for i in range(4):
                    b = 4 * g + i
                    act.activation(prob[:, 0, b, :], b4(g)[:, i, :], ACT.Exp,
                                   bias=neg_max[:, g, i:i + 1], accum_out=z[:, 0, b:b + 1])\
                        .then_inc(st.sem, st.one())
                act.wait_ge(st.sem, st.n)
                act.sem_inc(x3_exp, 1)
            act.wait_ge(x3_arg, 1)
            act.sem_inc(x3_arg, -1)
            act.activation(batt2[:, :], batt[:, :], ACT.Exp, bias=bstat[:, 0:1],
                           accum_out=bstat[:, 1:2]).then_inc(st.sem, st.one())
            act.wait_ge(st.sem, st.n)
            act.sem_inc(x3_bexp, 1)
            for half in range(2):
                act.wait_ge(x3_out, 1)
                act.sem_inc(x3_out, -1)
                act.activation(attT[:, half * 512:(half + 1) * 512], bank[half][:, :],
                               ACT.Identity, bias=col("bqv")).then_inc(st.sem, st.one())
            act.wait_ge(st.sem, st.n)
            act.sem_inc(x3_oute, 1)
            evacuate_transposed(xnT, split=True)
            ffn(ffn3)

        @block.tensor
        def _(pe):
            def mm(o, l, rh, start=True, stop=True, **kw):
                return pe.matmul(o, l, rh, start=start, stop=stop, **kw)

            def transpose_tiles(src, ready):
                pe.wait_ge(ready, 1)
                pe.sem_inc(ready, -1)
                for b in range(NB):
                    t = pe.transpose(b4(b // 4)[:, b % 4, :], src[:, b, :], ident[:, :])
                    if b % 4 == 3:
                        t.then_inc(transposed, 1)

            def project(weight, src, at):
                for half in range(2):
                    mm(bank[at + half][:, :], weight, src[:, half * 512:(half + 1) * 512])\
                        .then_inc(projected, 1)

            def project_tok(weight, src, at):
                for b in range(NB):
                    m = mm(b4(at + b // 4)[:, b % 4, :], src[:, b * P:(b + 1) * P], weight)
                    if b % 4 == 3:
                        m.then_inc(projected, 1)

            def narrow_attention(prune):
                def scores(it, n):
                    if n % 4 == 0:
                        pe.wait_ge(qk_ready, 1)
                        pe.sem_inc(qk_ready, -1)
                    pe.wait_ge(scores_free, 1)
                    pe.sem_inc(scores_free, -1)
                    p = slice(32 * (n % 4), 32 * (n % 4) + 32)
                    mm(bank[n % 2][:, :], q_b[p, n // 4, :],
                       k_mask[p, n // 4, :, :].rearrange("p a b -> p (a b)")).then_inc(scores_done, 1)

                def turn(it, n):
                    pe.wait_ge(probs_ready, 1)
                    pe.sem_inc(probs_ready, -1)
                    pe.wait_ge(turn_free, 1)
                    pe.sem_inc(turn_free, -1)
                    for i in range(4):
                        t = pe.transpose(b4(2 + n % 2)[:, i, :], prob[:, n // 4, 4 * (n % 4) + i, :],
                                         ident[:, :])
                    t.then_inc(probsT_done, 1)

                def four_heads(source, n):
                    j = n % 4
                    for i in range(4):
                        h = 4 * j + i
                        m = mm(bank[6 + n // 4][32 * j:32 * j + 32, 0:P], source[:, n // 4, h, :],
                               probT[:, n // 4, h, :], start=(i == 0), stop=(i == 3))
                    return m

                def values(it, n):
                    pe.wait_ge(probsT_ready, 1)
                    pe.sem_inc(probsT_ready, -1)
                    if n % 4 == 0:
                        pe.wait_ge(v_ready, 1)
                        pe.sem_inc(v_ready, -1)
                        pe.wait_ge(out_free, 1)
                        pe.sem_inc(out_free, -1)
                    m = four_heads(v_wide, n)
                    if n % 4 == 3:
                        m.then_inc(out_done, 1)

                def turn_sums(it, n):
                    pe.wait_ge(colsum_ready, 1)
                    pe.sem_inc(colsum_ready, -1)
                    pe.transpose(bank[5][0:H, 0:P], col_sum[:, n // 4, :], ident[:, :])\
                        .then_inc(ranked_done, 1)

                def turn_kept(it, n):
                    pe.wait_ge(kept_ready, 1)
                    pe.sem_inc(kept_ready, -1)
                    pe.transpose(bank[5][:, 256:256 + H], kept[:, :], ident[0:H, 0:H])\
                        .then_inc(keptT_done, 1)

                def values_kept(it, n):
                    pe.wait_ge(v_kept_ready, 1)
                    pe.sem_inc(v_kept_ready, -1)
                    pe.wait_ge(probsT_ready, 4)
                    pe.sem_inc(probsT_ready, -4)
                    pe.wait_ge(out_free, 1)
                    pe.sem_inc(out_free, -1)
                    for j in range(4):
                        m = four_heads(v_kept, n - 3 + j)
                    m.then_inc(out_done, 1)

                pe.sem_inc(scores_free, 2)
                pe.sem_inc(turn_free, 2)
                pe.sem_inc(out_free, 2)
                if prune:
                    pipelined(pe, [(scores, range(8), 0), (turn, range(8), 2), (turn_sums, (3, 7), 4),
                                   (turn_kept, (3, 7), 5), (values_kept, (3, 7), 6)], 8, NB // 2,
                              lambda: None)
                else:
                    pipelined(pe, [(scores, range(8), 0), (turn, range(8), 2), (values, range(8), 3)],
                              8, NB // 2, lambda: None)
                pe.wait_ge(scores_free, 2)
                pe.sem_inc(scores_free, -2)
                pe.wait_ge(turn_free, 2)
                pe.sem_inc(turn_free, -2)
                pe.wait_ge(out_free, 2)
                pe.sem_inc(out_free, -2)

            def attention_output(weight):
                pe.wait_ge(att_ready, 1)
                pe.sem_inc(att_ready, -1)
                for b in range(NB):
                    m = mm(b4(2 + b // 4)[:, b % 4, :], attT[:, b * P:(b + 1) * P], weight)
                    if b % 4 == 3:
                        m.then_inc(y_attn_done, 1)

            def wide_attention():
                def queries(it, n):
                    pe.wait_ge(q_free, 1)
                    pe.sem_inc(q_free, -1)
                    for i in range(4):
                        m = mm(b4(0)[:, i, :], wq1[:, 4 * (n % 4) + i, :],
                               xnT[:, bass.ds((2 * it + n // 4) * P, P)])
                    m.then_inc(heads_q_done, 1)

                def scores(it, n):
                    pe.wait_ge(qh_ready, 1)
                    pe.sem_inc(qh_ready, -1)
                    for i in range(4):
                        mm(b4(1 + n % 2)[:, i, :], qh[:, n % 2, i, :],
                           kT[:, bass.ds((2 * it + n // 4) * P, P)])
                    pe.wait_ge(qmk_ready, 1)
                    pe.sem_inc(qmk_ready, -1)
                    pe.wait_ge(own_free, 1)
                    pe.sem_inc(own_free, -1)
                    for i in range(4):
                        at = 4 * (n % 2) + i
                        m = mm(bank[7][:, at:at + 1], qmk[:, n % 2, i, :], ones[:, :])
                    m.then_inc(scores_done, 1)

                def turn(it, n):
                    pe.wait_ge(probs_ready, 1)
                    pe.sem_inc(probs_ready, -1)
                    for i in range(4):
                        t = pe.transpose(b4(3)[:, i, :], prob[:, 0, 4 * (n % 2) + i, :], ident[:, :])
                    t.then_inc(probsT_done, 1)

                def values(it, n):
                    pe.wait_ge(probsT_ready, 1)
                    pe.sem_inc(probsT_ready, -1)
                    for i in range(4):
                        m = mm(b4(4)[:, i, :], probT[:, 0, 4 * (n % 2) + i, :],
                               iv[:, bass.ds(2 * it + n // 4, 1), :].rearrange("p a b -> p (a b)"))
                    m.then_inc(pv_done, 1)

                def turn_heads(it, n):
                    pe.wait_ge(heads_ready, 1)
                    pe.sem_inc(heads_ready, -1)
                    for i in range(4):
                        t = pe.transpose(b4(5)[:, i, :], heads[:, n % 2, i, :], ident[:, :])
                    t.then_inc(headsT_done, 1)

                def output(it, n):
                    pe.wait_ge(headsT_ready, 1)
                    pe.sem_inc(headsT_ready, -1)
                    if n % 4 == 0:
                        pe.wait_ge(wo_free, 1)
                        pe.sem_inc(wo_free, -1)
                    for i in range(4):
                        h = 4 * (n % 4) + i
                        m = mm(bank[6][:, 0:D], headsT[:, n % 2, i, :], wo1[:, h, :],
                               start=(h == 0), stop=(h == H - 1))
                    if n % 4 == 3:
                        m.then_inc(wo_done, 1)

                pe.sem_inc(q_free, 1)
                pe.sem_inc(own_free, 1)
                pe.sem_inc(wo_free, 1)
                pipelined(pe, [(queries, range(8), 0), (scores, range(8), 1), (output, range(8), 5),
                               (turn_heads, range(8), 4), (values, range(8), 3), (turn, range(8), 2)],
                          8, NB // 2, lambda: None)
                pe.wait_ge(q_free, 1)
                pe.sem_inc(q_free, -1)
                pe.wait_ge(own_free, 1)
                pe.sem_inc(own_free, -1)
                pe.wait_ge(wo_free, 1)
                pe.sem_inc(wo_free, -1)

            def route(weight, experts, src):
                for b in range(NB):
                    m = mm(bank[7][:, b * experts:(b + 1) * experts], src[:, b * P:(b + 1) * P], weight)
                m.then_inc(router_done, 1)

            def expert_biases(b2, experts):
                pe.wait_ge(cw_ready, 1)
                pe.sem_inc(cw_ready, -1)
                for b in range(NB):
                    t = pe.transpose(b4(2 + b // 4)[0:experts, b % 4, :], cw[:, b, 0:experts], ident[:, :])
                t.then_inc(cwT_done, 1)
                pe.wait_ge(cwT_ready, 1)
                pe.sem_inc(cwT_ready, -1)
                for b in range(NB):
                    m = mm(b4(6 + b // 4)[:, b % 4, :], cwT[0:experts, b * P:(b + 1) * P], b2[0:experts, :])
                m.then_inc(bias_done, 1)
                pe.wait_ge(bias_free, 1)
                pe.sem_inc(bias_free, -1)

            def split_products(o, left, right, start, stop):
                mm(o, left(LOW), right(HIGH), start=start, stop=False)
                mm(o, left(HIGH), right(LOW), start=False, stop=False)
                return mm(o, left(HIGH), right(HIGH), start=False, stop=stop)

            def ffn(f):
                def hidden(i, n):
                    sub, half = n // 2, n % 2
                    begun = n > 0 or not isinstance(i, int)
                    if half == 0:
                        pe.wait_ge(w_in_ready[sub], 1)
                        pe.sem_inc(w_in_ready[sub], -1)
                    if f is ffn0 and half == 0:
                        pe.wait_ge(input_ready, 1)
                        pe.sem_inc(input_ready, -1)
                    at = sub if f is ffn0 else 0
                    tokens = slice(half * 512, (half + 1) * 512)
                    for fc in range(f.FC):
                        if f.FC == 4 and begun and not f.gated:
                            pe.wait_ge(h_ready, fc + 1)
                        elif f.gated and (begun or fc == 3):
                            pe.wait_ge(h_ready, f.FC + (fc == 3) if begun else 1)
                        at_bank = f.hidden_bank(n, fc)
                        m = split_products(bank[at_bank][:, :],
                                           lambda part: f.w1((w_lo, w_hi)[part], sub, fc),
                                           lambda part: (in_lo, in_hi)[part][:, at, tokens], True, True)
                        if f.gated:
                            m = split_products(bank[3 + at_bank][:, :],
                                               lambda part: f.up((w_lo, w_hi)[part], sub, fc),
                                               lambda part: (in_lo, in_hi)[part][:, at, tokens],
                                               True, True)
                        m.then_inc(h_done, 1)

                def output(i, n):
                    sub, half = n // 2, n % 2
                    if half == 0:
                        pe.wait_ge(w_out_loaded[sub], 16)
                        pe.sem_inc(w_out_loaded[sub], -16)
                    pe.wait_ge(h_ready, f.FC)
                    pe.sem_inc(h_ready, -f.FC)
                    pe.wait_ge(y_free, 1)
                    pe.sem_inc(y_free, -1)
                    for t in range(4):
                        tokens = slice(t * P, (t + 1) * P)
                        for fc in range(f.FC):
                            m = mm(b4(f.output_bank(n))[:, t, :], hT[:, half, fc, tokens], f.w2(sub, fc),
                                   start=(fc == 0), stop=(fc == f.FC - 1))
                    m.then_inc(y_done, 1)

                if f is not ffn0:
                    pe.wait_ge(input_ready, 1)
                    pe.sem_inc(input_ready, -1)
                y_banks = 2 if f.gated else 4
                for _ in range(y_banks):
                    pe.sem_inc(y_free, 1)
                halves(pe, [(hidden, range(4), 0), (output, range(4), 1)], f, lambda: None)
                pe.wait_ge(y_free, y_banks)
                pe.sem_inc(y_free, -y_banks)

            pe.wait_ge(consts_pe, 1)
            pe.sem_inc(consts_pe, -1)
            pe.wait_ge(sq_loaded, 16)
            pe.wait_ge(ctx_loaded, 16)

            project(w("wk0"), ctxT, 2)
            project_tok(w("wv0"), ctxT, 4)
            transpose_tiles(xn, norm_tok_ready)
            pe.wait_ge(feat_ready, 1)
            pe.sem_inc(feat_ready, -1)
            project(w("wq0"), xnT, 6)
            pe.wait_ge(qkv_ready, 1)
            pe.sem_inc(qkv_ready, -1)
            narrow_attention(False)
            attention_output(w("wo0"))
            transpose_tiles(xn, norm_tok_ready)
            pe.wait_ge(feat_ready, 1)
            pe.sem_inc(feat_ready, -1)
            route(w("r0"), E0, xnT)
            transpose_tiles(att, norm_tok_ready)
            pe.wait_ge(feat_ready, 1)
            pe.sem_inc(feat_ready, -1)
            ffn(ffn0)
            pe.wait_ge(b2_loaded, 32)
            expert_biases(b2_0, E0)

            project(w("wk1"), ctxT, 2)
            project_tok(w("wv1"), ctxT, 4)
            transpose_tiles(xn, norm_tok_ready)
            pe.wait_ge(feat_ready, 1)
            pe.sem_inc(feat_ready, -1)
            pe.wait_ge(qkv_ready, 1)
            pe.sem_inc(qkv_ready, -1)
            project(w("wk1"), xnT, 2)
            project_tok(w("wv1"), xnT, 4)
            pe.wait_ge(qkv_ready, 1)
            pe.sem_inc(qkv_ready, -1)
            pe.wait_ge(w1_attn_loaded, 32)
            wide_attention()
            transpose_tiles(iv, norm_tok_ready)
            pe.wait_ge(feat_ready, 1)
            pe.sem_inc(feat_ready, -1)
            ffn(mlp1)
            transpose_tiles(xn, norm_tok_ready)
            pe.wait_ge(feat_ready, 1)
            pe.sem_inc(feat_ready, -1)
            route(w("r1"), E1, xnT)
            ffn(ffn1)
            expert_biases(b2_1, E1)

            project(w("wk2"), ctxT, 2)
            project_tok(w("wv2"), ctxT, 4)
            transpose_tiles(xn, norm_tok_ready)
            pe.wait_ge(feat_ready, 1)
            pe.sem_inc(feat_ready, -1)
            project(w("wq2"), xnT, 6)
            pe.wait_ge(qkv_ready, 1)
            pe.sem_inc(qkv_ready, -1)
            narrow_attention(True)
            attention_output(w("wo2"))
            transpose_tiles(xn, norm_tok_ready)
            pe.wait_ge(feat_ready, 1)
            pe.sem_inc(feat_ready, -1)
            route(w("r2"), E2, xnT)
            ffn(ffn2)

            transpose_tiles(xn, norm_tok_ready)
            pe.wait_ge(feat_ready, 1)
            pe.sem_inc(feat_ready, -1)
            for b in range(NB):
                m = mm(bank[2][:, b:b + 1], xnT[:, b * P:(b + 1) * P], col("w1s"))
            pe.wait_ge(x3_sim, 1)
            pe.sem_inc(x3_sim, -1)
            for b in range(NB):
                m = mm(b4(b // 4)[:, b % 4, :], qT[:, b * P:(b + 1) * P], ctxT[:, b * P:(b + 1) * P])
                if b % 4 == 3:
                    m.then_inc(x3_sims, 1)
            pe.wait_ge(ctx_tok_loaded, 16)
            pe.wait_ge(x3_m, 1)
            pe.sem_inc(x3_m, -1)
            pe.transpose(bank[3][0:NB, 0:P], m_sim[:, :], ident[:, :]).then_inc(x3_mT, 1)
            for g in range(2):
                pe.wait_ge(x3_exp, 1)
                pe.sem_inc(x3_exp, -1)
                for i in range(4):
                    t = pe.transpose(b4(4 + g)[:, i, :], prob[:, 0, 4 * g + i, :], ident[:, :])
                t.then_inc(x3_t, 1)
            for g in range(2):
                pe.wait_ge(x3_te, 1)
                pe.sem_inc(x3_te, -1)
                for i in range(4):
                    m = mm(b4(6 + g)[:, i, :], probT[:, 0, 4 * g + i, :], ctx_tok[:, 4 * g + i, :])
                m.then_inc(x3_pv, 1)
            pe.wait_ge(x3_b, 1)
            pe.sem_inc(x3_b, -1)
            pe.transpose(bank[3][:, 256:256 + NB], batt[:, :], ident[0:NB, 0:NB]).then_inc(x3_bT, 1)
            for g in range(2):
                pe.wait_ge(x3_hq, 1)
                pe.sem_inc(x3_hq, -1)
                for i in range(4):
                    t = pe.transpose(b4(4 + g)[:, i, :], iv[:, 4 * g + i, :], ident[:, :])
                t.then_inc(x3_hqT, 1)
            pe.wait_ge(x3_bTe, 1)
            pe.sem_inc(x3_bTe, -1)
            for b in range(NB):
                m = mm(bank[2][:, 16 + b:17 + b], xn[:, b, :], batt_col[:, b:b + 1])
            m.then_inc(x3_hc, 1)
            pe.wait_ge(x3_feats, 1)
            pe.sem_inc(x3_feats, -1)
            for half in range(2):
                t = slice(half * 512, (half + 1) * 512)
                for i, src in enumerate((xnT[:, t], kT[:, t], normed[:, 0, t], normed[:, 1, t])):
                    m = mm(bank[half][:, :], w("wqv", i * D, D), src, start=(i == 0), stop=(i == 3))
                m.then_inc(x3_out, 1)
            pe.wait_ge(x3_oute, 1)
            pe.sem_inc(x3_oute, -1)
            for b in range(NB):
                t = pe.transpose(b4(2 + b // 4)[:, b % 4, :], attT[:, b * P:(b + 1) * P], ident[:, :])
            t.then_inc(x3_outT, 1)

            transpose_tiles(xn, norm_tok_ready)
            pe.wait_ge(feat_ready, 1)
            pe.sem_inc(feat_ready, -1)
            ffn(ffn3)

        @block.vector
        def _(dve):
            st = Steps(dve, dve_steps)

            def layer_norm(src, dst, eps, gamma=None, beta=None, give=()):
                dve.wait_ge(st.sem, st.n)
                for b in range(NB):
                    dve.bn_stats(stats[:, b, :], src[:, b, :]).then_inc(st.sem, st.one())
                dve.wait_ge(st.sem, st.n)
                for b in range(NB):
                    dve.bn_aggr(mean_var[:, b, :], stats[:, b, :]).then_inc(st.sem, st.one())
                dve.wait_ge(st.sem, st.n)
                dve.tensor_scalar(var_eps[:, :], mean_var[:, :, 1], eps, None, ALU.add)\
                    .then_inc(st.sem, st.one())
                dve.wait_ge(st.sem, st.n)
                dve.sem_inc(var_ready, 1)
                dve.wait_ge(rstd_ready, 1)
                dve.sem_inc(rstd_ready, -1)
                for b in range(NB):
                    dve.tensor_scalar(dst[:, b, :], src[:, b, :], mean_var[:, b, 0:1],
                                      rstd[:, b:b + 1], ALU.subtract, ALU.mult).then_inc(st.sem, st.one())
                if gamma:
                    dve.wait_ge(st.sem, st.n)
                    dve.tensor_tensor(dst[:, :, :], dst[:, :, :], row_b(gamma), ALU.mult)\
                        .then_inc(st.sem, st.one())
                    dve.wait_ge(st.sem, st.n)
                    dve.tensor_tensor(dst[:, :, :], dst[:, :, :], row_b(beta), ALU.add)\
                        .then_inc(st.sem, st.one())
                dve.wait_ge(st.sem, st.n)
                for token in give:
                    dve.sem_inc(token, 1)
                st.close()

            def add_to_x(what):
                dve.wait_ge(st.sem, st.n)
                dve.tensor_tensor(x[:, :, :], x[:, :, :], what, ALU.add).then_inc(st.sem, st.one())
                dve.wait_ge(st.sem, st.n)

            def copy_projected(dst, at, bias, scale):
                for half in range(2):
                    dve.wait_ge(projected, 1)
                    dve.sem_inc(projected, -1)
                    dve.tensor_scalar(dst[:, half * 512:(half + 1) * 512], bank[at + half][:, :],
                                      col(bias), scale, ALU.add, ALU.mult).then_inc(st.sem, st.one())

            def copy_values(dst, at, bias):
                for half in range(2):
                    dve.wait_ge(projected, 1)
                    dve.sem_inc(projected, -1)
                    dve.tensor_tensor(dst[:, 4 * half:4 * half + 4, :], b4(at + half),
                                      row(bias)[:, None, :].broadcast_to([P, 4, D]), ALU.add)\
                        .then_inc(st.sem, st.one())

            def narrow_attention(prune):
                def maxima(it, n):
                    dve.wait_ge(scores_done, 1)
                    dve.sem_inc(scores_done, -1)
                    if n % 4 == 3:
                        dve.sem_inc(qk_free, 1)
                    dve.tensor_reduce(neg_max[:, n, :], b4(n % 2), X_AX, ALU.max, negate=True)\
                        .then_inc(neg_max_ready, 1)

                def inverse_sums(it, n):
                    dve.wait_ge(exps_done, 4)
                    dve.sem_inc(exps_done, -4)
                    h = slice(4 * (n % 4), 4 * (n % 4) + 4)
                    dve.reciprocal(r[:, n // 4, h], z[:, n // 4, h]).then_inc(st.sem, st.one())
                    dve.wait_ge(st.sem, st.n)
                    dve.sem_inc(inverse_ready, 1)
                    dve.sem_inc(scores_free, 1)

                def copy_probsT(it, n):
                    dve.wait_ge(probsT_done, 1)
                    dve.sem_inc(probsT_done, -1)
                    h = 4 * (n % 4)
                    dve.tensor_copy(probT[:, n // 4, h:h + 4, :], b4(2 + n % 2)).then_inc(st.sem, st.one())
                    dve.wait_ge(st.sem, st.n)
                    dve.sem_inc(probsT_ready, 1)
                    dve.sem_inc(turn_free, 1)

                def copy_out(it, n):
                    dve.wait_ge(out_done, 1)
                    dve.sem_inc(out_done, -1)
                    if not prune:
                        dve.sem_inc(v_free, 1)
                    dve.tensor_copy(attT[:, bass.ds((2 * it + n // 4) * P, P)], bank[6 + n // 4][:, 0:P])\
                        .then_inc(st.sem, st.one())
                    dve.wait_ge(st.sem, st.n)
                    dve.sem_inc(out_free, 1)

                def column_sums(it, n):
                    dve.wait_ge(probsT_copied, 1)
                    dve.sem_inc(probsT_copied, -1)
                    h = slice(4 * (n % 4), 4 * (n % 4) + 4)
                    dve.tensor_reduce(col_sum[:, n // 4, h], probT[:, n // 4, h, :], X_AX, ALU.add)\
                        .then_inc(st.sem, st.one())
                    if n % 4 == 3:
                        dve.wait_ge(st.sem, st.n)
                        dve.sem_inc(colsum_ready, 1)

                def rank(it, n):
                    dve.wait_ge(ranked_done, 1)
                    dve.sem_inc(ranked_done, -1)
                    dve.tensor_scalar(ranked[:, 0:P], bank[5][0:H, P - 1::-1][:, 0:P], -1.0, None,
                                      ALU.mult).then_inc(st.sem, st.one())
                    dve.memset(ranked[:, P:P + 8], PAD).then_inc(st.sem, st.one())
                    dve.wait_ge(st.sem, st.n)
                    dve.max(top[:, 0, :], ranked[:, :]).then_inc(st.sem, st.one())
                    dve.wait_ge(st.sem, st.n)
                    dve.match_replace(ranked[:, :], top[:, 0, :], ranked[:, :], GONE)\
                        .then_inc(st.sem, st.one())
                    dve.wait_ge(st.sem, st.n)
                    dve.max(top[:, 1, :], ranked[:, :]).then_inc(st.sem, st.one())
                    dve.wait_ge(st.sem, st.n)
                    dve.memset(top[:, 1, DROP - 8:8], PAD).then_inc(st.sem, st.one())
                    dve.wait_ge(st.sem, st.n)
                    dve.match_replace(ranked[:, :], top[:, 1, :], ranked[:, :], GONE)\
                        .then_inc(st.sem, st.one())
                    dve.wait_ge(st.sem, st.n)
                    dve.tensor_scalar(kept[:, :], ranked[:, P - 1::-1][:, 0:P], PAD, None, ALU.is_gt)\
                        .then_inc(st.sem, st.one())
                    dve.wait_ge(st.sem, st.n)
                    dve.sem_inc(kept_ready, 1)

                def keep_values(it, n):
                    dve.wait_ge(keptT_done, 1)
                    dve.sem_inc(keptT_done, -1)
                    dve.wait_ge(v_ready, 1)
                    dve.sem_inc(v_ready, -1)
                    dve.tensor_tensor(v_kept[:, n // 4, :, :], v_wide[:, n // 4, :, :],
                                      bank[5][:, 256:256 + H][:, :, None].broadcast_to([P, H, 32]), ALU.mult)\
                        .then_inc(st.sem, st.one())
                    dve.wait_ge(st.sem, st.n)
                    dve.sem_inc(v_kept_ready, 1)
                    dve.sem_inc(v_free, 1)

                if prune:
                    order = [(maxima, range(8), 0), (inverse_sums, range(8), 1), (rank, (3, 7), 5),
                             (keep_values, (3, 7), 6), (copy_out, (3, 7), 7), (column_sums, range(8), 3)]
                else:
                    order = [(maxima, range(8), 0), (inverse_sums, range(8), 1), (copy_out, (3, 7), 4),
                             (copy_probsT, range(8), 2)]
                st.close()
                pipelined(dve, order, 8, NB // 2, st.close)
                dve.sem_inc(att_ready, 1)

            def attention_output(bias):
                dve.tensor_tensor(x[:, :, :], x[:, :, :], row_b(bias), ALU.add).then_inc(st.sem, st.one())
                dve.wait_ge(st.sem, st.n)
                for half in range(2):
                    dve.wait_ge(y_attn_done, 1)
                    dve.sem_inc(y_attn_done, -1)
                    part = x[:, 4 * half:4 * half + 4, :]
                    dve.tensor_tensor(part, part, b4(2 + half), ALU.add).then_inc(st.sem, st.one())
                dve.wait_ge(st.sem, st.n)

            def wide_attention():
                def queries(it, n):
                    dve.wait_ge(heads_q_done, 1)
                    dve.sem_inc(heads_q_done, -1)
                    at = COLS["bq1"][0] + 4 * (n % 4)
                    dve.tensor_tensor(qh[:, n % 2, :, :], b4(0),
                                      cols[:, at:at + 4][:, :, None].broadcast_to([P, 4, P]), ALU.add)\
                        .then_inc(st.sem, st.one())
                    dve.wait_ge(st.sem, st.n)
                    dve.sem_inc(qh_ready, 1)
                    dve.sem_inc(qh_ready_pool, 1)
                    dve.sem_inc(q_free, 1)

                def maxima(it, n):
                    dve.wait_ge(scores_done, 1)
                    dve.sem_inc(scores_done, -1)
                    own = bank[7][:, 4 * (n % 2):4 * (n % 2) + 4]
                    m = row_max[:, n % 2, :]
                    dve.tensor_reduce(m, b4(1 + n % 2), X_AX, ALU.max).then_inc(st.sem, st.one())
                    dve.wait_ge(st.sem, st.n)
                    dve.tensor_tensor(m, m, own, ALU.max).then_inc(st.sem, st.one())
                    dve.wait_ge(st.sem, st.n)
                    dve.tensor_scalar(neg_max[:, n, :], m, -SC1, None, ALU.mult).then_inc(st.sem, st.one())
                    dve.wait_ge(st.sem, st.n)
                    dve.scalar_tensor_tensor(self_arg[:, n % 2, :], own, SC1, neg_max[:, n, :],
                                             ALU.mult, ALU.add).then_inc(st.sem, st.one())
                    dve.wait_ge(st.sem, st.n)
                    dve.sem_inc(neg_max_ready, 1)
                    dve.sem_inc(own_free, 1)

                def weights(it, n):
                    dve.wait_ge(probs_ready_dve, 1)
                    dve.sem_inc(probs_ready_dve, -1)
                    four = slice(4 * (n % 2), 4 * (n % 2) + 4)
                    total, inv = z[:, 1, four], r[:, 0, 4 * (n % 4):4 * (n % 4) + 4]
                    dve.tensor_tensor(total, z[:, 0, four], self_exp[:, n % 2, :], ALU.add)\
                        .then_inc(st.sem, st.one())
                    dve.wait_ge(st.sem, st.n)
                    dve.reciprocal(inv, total).then_inc(st.sem, st.one())
                    dve.wait_ge(st.sem, st.n)
                    dve.tensor_tensor(self_w[:, n % 2, :], self_exp[:, n % 2, :], inv, ALU.mult)\
                        .then_inc(st.sem, st.one())
                    dve.wait_ge(st.sem, st.n)
                    dve.sem_inc(self_w_ready, 1)

                def heads_out(it, n):
                    dve.wait_ge(pv_done, 1)
                    dve.sem_inc(pv_done, -1)
                    dve.wait_ge(mva_ready, 1)
                    dve.sem_inc(mva_ready, -1)
                    for i in range(4):
                        dve.scalar_tensor_tensor(heads[:, n % 2, i, :], b4(4)[:, i, :],
                                                 r[:, 0, 4 * (n % 4) + i:4 * (n % 4) + i + 1],
                                                 mva[:, n % 2, i, :], ALU.mult, ALU.add)\
                            .then_inc(st.sem, st.one())
                    dve.wait_ge(st.sem, st.n)
                    dve.sem_inc(heads_ready, 1)

                def residual(it, n):
                    dve.wait_ge(wo_done, 1)
                    dve.sem_inc(wo_done, -1)
                    b = bass.ds(2 * it + n // 4, 1)
                    dve.tensor_tensor(att[:, b, :], xn[:, b, :], bank[6][:, 0:D][:, None, :], ALU.add)\
                        .then_inc(st.sem, st.one())
                    dve.wait_ge(st.sem, st.n)
                    dve.sem_inc(wo_free, 1)

                st.close()
                pipelined(dve, [(residual, (3, 7), 6), (heads_out, range(8), 4), (weights, range(8), 2),
                                (queries, range(8), 0), (maxima, range(8), 1)], 8, NB // 2, st.close)

            def route(experts, biases, give=()):
                dve.wait_ge(router_done, 1)
                dve.sem_inc(router_done, -1)
                lg = logits[:, :, 0:experts]
                dve.tensor_copy(lg, bank[7][:, 0:NB * experts].rearrange("p (b e) -> p b e", b=NB))\
                    .then_inc(st.sem, st.one())
                for bias in biases:
                    dve.wait_ge(st.sem, st.n)
                    dve.tensor_tensor(lg, lg, row(bias)[:, None, :].broadcast_to([P, NB, experts]), ALU.add)\
                        .then_inc(st.sem, st.one())
                dve.wait_ge(st.sem, st.n)
                for b in range(NB):
                    dve.max(best[:, b, :], logits[:, b, 0:experts]).then_inc(st.sem, st.one())
                dve.wait_ge(st.sem, st.n)
                dve.tensor_tensor(gap[:, :], best[:, :, 1], best[:, :, 0], ALU.subtract)\
                    .then_inc(st.sem, st.one())
                dve.wait_ge(st.sem, st.n)
                dve.sem_inc(gap_ready, 1)
                for b in range(NB):
                    dve.max_index(best_at[:, b, :], best[:, b, :], logits[:, b, 0:experts])\
                        .then_inc(st.sem, st.one())
                dve.wait_ge(st.sem, st.n)
                dve.tensor_copy(best_no[:, :, :], best_at[:, :, 0:2]).then_inc(st.sem, st.one())
                dve.wait_ge(gap_exp_ready, 1)
                dve.sem_inc(gap_exp_ready, -1)
                dve.tensor_scalar(w_a[:, :], gap_exp[:, :], 1.0, None, ALU.add).then_inc(st.sem, st.one())
                dve.wait_ge(st.sem, st.n)
                dve.reciprocal(w_a[:, :], w_a[:, :]).then_inc(st.sem, st.one())
                dve.wait_ge(st.sem, st.n)
                dve.tensor_tensor(w_b[:, :], w_a[:, :], gap_exp[:, :], ALU.mult).then_inc(st.sem, st.one())
                full = [P, NB, experts]
                number = expert_no[:, 0:experts][:, None, :].broadcast_to(full)
                for o, i, weight in ((cw, 0, w_a), (cw_b, 1, w_b)):
                    dve.wait_ge(st.sem, st.n)
                    dve.tensor_tensor(o[:, :, 0:experts], number,
                                      best_no[:, :, i:i + 1].broadcast_to(full), ALU.is_equal)\
                        .then_inc(st.sem, st.one())
                    dve.wait_ge(st.sem, st.n)
                    dve.tensor_tensor(o[:, :, 0:experts], o[:, :, 0:experts],
                                      weight[:, :, None].broadcast_to(full), ALU.mult)\
                        .then_inc(st.sem, st.one())
                dve.wait_ge(st.sem, st.n)
                dve.tensor_tensor(cw[:, :, 0:experts], cw[:, :, 0:experts], cw_b[:, :, 0:experts], ALU.add)\
                    .then_inc(st.sem, st.one())
                dve.wait_ge(st.sem, st.n)
                for token in give:
                    dve.sem_inc(token, 1)

            def expert_biases(experts):
                dve.wait_ge(cwT_done, 1)
                dve.sem_inc(cwT_done, -1)
                for half in range(2):
                    dve.tensor_copy(cwT[0:experts, half * 512:(half + 1) * 512],
                                    bank[2 + half][0:experts, :]).then_inc(st.sem, st.one())
                dve.wait_ge(st.sem, st.n)
                dve.sem_inc(cwT_ready, 1)
                dve.wait_ge(bias_done, 1)
                dve.sem_inc(bias_done, -1)
                for half in range(2):
                    part = x[:, 4 * half:4 * half + 4, :]
                    dve.tensor_tensor(part, part, b4(6 + half), ALU.add).then_inc(st.sem, st.one())
                dve.wait_ge(st.sem, st.n)
                dve.sem_inc(bias_free, 1)

            def split_input():
                dve.wait_ge(input_hi_ready, 1)
                dve.sem_inc(input_hi_ready, -1)
                dve.tensor_tensor(in_lo[:, 0, :], xnT[:, :], in_hi[:, 0, :], ALU.subtract).then_inc(input_ready, 1)

            def scaled_input(e, sub):
                for part in (in_hi, normed):
                    dve.tensor_scalar(part[:, sub, :], kT[:, :], col("gamma0", e), col("beta0", e),
                                      ALU.mult, ALU.add).then_inc(st.sem, st.one())
                dve.wait_ge(st.sem, st.n)
                dve.tensor_tensor(in_lo[:, sub, :], normed[:, sub, :], in_hi[:, sub, :], ALU.subtract)\
                    .then_inc(input_ready, 1)

            def ffn(f, finish, between=None):
                def gate(i, n):
                    half = n % 2
                    for fc in range(f.FC):
                        dve.wait_ge(g_done, 1)
                        dve.sem_inc(g_done, -1)
                        h, up = hT[:, half, fc, :], bank[3 + f.hidden_bank(n, fc)][:, :]
                        if f.up_bias:
                            dve.scalar_tensor_tensor(h, up, col(f.up_bias, fc), h, ALU.add, ALU.mult)\
                                .then_inc(h_ready, 1)
                        else:
                            dve.tensor_tensor(h, up, h, ALU.mult).then_inc(h_ready, 1)

                def next_input(i, n):
                    scaled_input(2 * i + n // 2 + 1, 1 - n // 2)

                def output(i, n):
                    dve.wait_ge(y_done, 1)
                    dve.sem_inc(y_done, -1)
                    if n % 2 == 1:
                        dve.sem_inc(w_out_free[n // 2], 1)
                    finish(2 * i + n // 2, n, b4(f.output_bank(n)))
                    dve.wait_ge(st.sem, st.n)
                    dve.sem_inc(y_free, 1)

                order = [(output, range(4), 1)]
                if f is ffn0:
                    order.insert(0, (next_input, (0, 2), 0))
                if f.gated:
                    order.insert(0, (gate, range(4), 0))
                st.close()
                halves(dve, order, f, st.close, between)

            def combine(e, n, ps):
                for t in range(4):
                    b = 4 * (n % 2) + t
                    dve.scalar_tensor_tensor(x[:, b, :], ps[:, t, :], cw[:, b, bass.ds(e, 1)],
                                             x[:, b, :], ALU.mult, ALU.add).then_inc(st.sem, st.one())

            def residual_into(dst):
                def finish(e, n, ps):
                    part = dst[:, 4 * n:4 * n + 4, :]
                    dve.tensor_tensor(part, part, ps, ALU.add).then_inc(st.sem, st.one())
                return finish

            dve.wait_ge(x_loaded, 16)
            dve.wait_ge(consts_dve, 1)
            dve.sem_inc(consts_dve, -1)
            dve.wait_ge(cols_loaded, 16)
            dve.wait_ge(rows_loaded, 16)

            copy_projected(kT, 2, "bk0", 1.0)
            copy_values(iv, 4, "bv0")
            layer_norm(x, xn, 1e-5, give=[norm_tok_ready])
            copy_projected(qT, 6, "bq0", SC0)
            dve.wait_ge(st.sem, st.n)
            dve.sem_inc(qkv_ready, 1)
            dve.sem_inc(qkv_ready_pool, 1)
            narrow_attention(False)
            attention_output("bo0")
            layer_norm(x, xn, 1e-5, give=[norm_tok_ready])
            layer_norm(xn, att, 1e-6, give=[norm_tok_ready])
            dve.wait_ge(feat_ready_dve, 1)
            dve.sem_inc(feat_ready_dve, -1)
            scaled_input(0, 0)

            def weights0():
                route(E0, [], give=[cw_ready])
                dve.tensor_tensor(cw_sum[:, :], w_a[:, :], w_b[:, :], ALU.add).then_inc(st.sem, st.one())
                dve.wait_ge(st.sem, st.n)
                for b in range(NB):
                    dve.scalar_tensor_tensor(x[:, b, :], xn[:, b, :], cw_sum[:, b:b + 1], x[:, b, :],
                                             ALU.mult, ALU.add).then_inc(st.sem, st.one())
                dve.wait_ge(st.sem, st.n)

            ffn(ffn0, combine, weights0)
            dve.wait_ge(input_ready, 1)
            dve.sem_inc(input_ready, -1)
            expert_biases(E0)

            copy_projected(kT, 2, "bk1", 1.0)
            copy_values(iv, 4, "bv1")
            layer_norm(x, xn, 1e-5, give=[norm_tok_ready, qkv_ready])
            copy_projected(qT, 2, "bk1", 1.0)
            copy_values(mv, 4, "bv1")
            dve.wait_ge(st.sem, st.n)
            dve.tensor_tensor(xn[:, :, :], xn[:, :, :], row_b("bo1"), ALU.add).then_inc(st.sem, st.one())
            dve.wait_ge(st.sem, st.n)
            dve.sem_inc(qkv_ready, 1)
            wide_attention()
            layer_norm(att, iv, 1e-6, "g1", "be1", give=[norm_tok_ready])
            split_input()
            dve.tensor_tensor(mv[:, :, :], iv[:, :, :], row_b("bm1"), ALU.add).then_inc(st.sem, st.one())
            dve.wait_ge(st.sem, st.n)
            ffn(mlp1, residual_into(mv))
            layer_norm(mv, att, 1e-6, "g2", "be2")
            add_to_x(att[:, :, :])
            layer_norm(x, xn, 1e-5, give=[norm_tok_ready])
            split_input()
            ffn(ffn1, combine, lambda: route(E1, ["rbg", "rbias"], give=[cw_ready]))
            expert_biases(E1)

            copy_projected(kT, 2, "bk2", 1.0)
            copy_values(iv, 4, "bv2")
            layer_norm(x, xn, 1e-5, give=[norm_tok_ready])
            copy_projected(qT, 6, "bq2", SC0)
            dve.wait_ge(st.sem, st.n)
            dve.sem_inc(qkv_ready, 1)
            dve.sem_inc(qkv_ready_pool, 1)
            narrow_attention(True)
            attention_output("bo2")
            layer_norm(x, xn, 1e-5, give=[norm_tok_ready])
            split_input()
            ffn(ffn2, combine, lambda: route(E2, []))

            layer_norm(x, xn, 1e-5, give=[norm_tok_ready])
            dve.wait_ge(feat_ready_dve, 1)
            dve.sem_inc(feat_ready_dve, -1)
            dve.tensor_scalar(qT[:, :], xnT[:, :], col("w3s"), col("w2s"), ALU.mult, ALU.add)\
                .then_inc(st.sem, st.one())
            dve.wait_ge(st.sem, st.n)
            dve.sem_inc(x3_sim, 1)
            for g in range(2):
                dve.wait_ge(x3_sims, 1)
                dve.sem_inc(x3_sims, -1)
                four = slice(4 * g, 4 * g + 4)
                dve.tensor_reduce(m_sim[:, four], b4(g), X_AX, ALU.max).then_inc(st.sem, st.one())
                dve.wait_ge(st.sem, st.n)
                dve.tensor_scalar(neg_max[:, g, :], m_sim[:, four], -1.0, None, ALU.mult)\
                    .then_inc(st.sem, st.one())
                dve.wait_ge(st.sem, st.n)
                dve.sem_inc(x3_neg, 1)
            dve.tensor_tensor(m_sim[:, :], m_sim[:, :], bank[2][:, 0:NB], ALU.add)\
                .then_inc(st.sem, st.one())
            dve.wait_ge(st.sem, st.n)
            dve.tensor_scalar(m_sim[:, :], m_sim[:, :], row("bsim"), None, ALU.add)\
                .then_inc(st.sem, st.one())
            dve.wait_ge(st.sem, st.n)
            dve.sem_inc(x3_m, 1)
            dve.wait_ge(x3_mT, 1)
            dve.sem_inc(x3_mT, -1)
            dve.tensor_copy(batt[:, :], bank[3][0:NB, 0:P]).then_inc(st.sem, st.one())
            dve.wait_ge(st.sem, st.n)
            dve.tensor_reduce(bstat[:, 0:1], batt[:, :], X_AX, ALU.max, negate=True)\
                .then_inc(st.sem, st.one())
            dve.wait_ge(st.sem, st.n)
            dve.sem_inc(x3_arg, 1)
            for g in range(2):
                dve.wait_ge(x3_t, 1)
                dve.sem_inc(x3_t, -1)
                dve.tensor_copy(probT[:, 0, 4 * g:4 * g + 4, :], b4(4 + g)).then_inc(st.sem, st.one())
                dve.wait_ge(st.sem, st.n)
                dve.sem_inc(x3_te, 1)
            dve.wait_ge(x3_bexp, 1)
            dve.sem_inc(x3_bexp, -1)
            dve.reciprocal(bstat[:, 2:3], bstat[:, 1:2]).then_inc(st.sem, st.one())
            dve.wait_ge(st.sem, st.n)
            dve.tensor_scalar(batt[:, :], batt2[:, :], bstat[:, 2:3], None, ALU.mult)\
                .then_inc(st.sem, st.one())
            dve.reciprocal(r[:, 0, 0:NB], z[:, 0, 0:NB]).then_inc(st.sem, st.one())
            dve.wait_ge(st.sem, st.n)
            dve.sem_inc(x3_b, 1)
            for g in range(2):
                dve.wait_ge(x3_pv, 1)
                dve.sem_inc(x3_pv, -1)
                four = slice(4 * g, 4 * g + 4)
                dve.tensor_tensor(iv[:, four, :], b4(6 + g),
                                  r[:, 0, four][:, :, None].broadcast_to([P, 4, D]), ALU.mult)\
                    .then_inc(st.sem, st.one())
                dve.wait_ge(st.sem, st.n)
                dve.sem_inc(x3_hq, 1)
            dve.wait_ge(x3_bT, 1)
            dve.sem_inc(x3_bT, -1)
            dve.tensor_copy(batt_col[:, :], bank[3][:, 256:256 + NB]).then_inc(st.sem, st.one())
            dve.wait_ge(st.sem, st.n)
            dve.sem_inc(x3_bTe, 1)
            for g in range(2):
                dve.wait_ge(x3_hqT, 1)
                dve.sem_inc(x3_hqT, -1)
                dve.tensor_copy(kT[:, g * 512:(g + 1) * 512], bank[4 + g][:, :]).then_inc(st.sem, st.one())
            dve.wait_ge(x3_hc, 1)
            dve.sem_inc(x3_hc, -1)
            dve.tensor_copy(hc_bar[:, :], bank[2][:, 16:16 + NB]).then_inc(st.sem, st.one())
            dve.wait_ge(st.sem, st.n)
            dve.tensor_tensor(normed[:, 0, :], xnT[:, :], kT[:, :], ALU.mult).then_inc(st.sem, st.one())
            dve.tensor_tensor(normed[:, 1, :].rearrange("p (b t) -> p b t", b=NB),
                              xnT[:, :].rearrange("p (b t) -> p b t", b=NB),
                              hc_bar[:, :, None].broadcast_to([D, NB, P]), ALU.mult)\
                .then_inc(st.sem, st.one())
            dve.wait_ge(st.sem, st.n)
            dve.sem_inc(x3_feats, 1)
            dve.wait_ge(x3_outT, 1)
            dve.sem_inc(x3_outT, -1)
            for half in range(2):
                part = x[:, 4 * half:4 * half + 4, :]
                dve.tensor_tensor(part, part, b4(2 + half), ALU.add).then_inc(st.sem, st.one())

            layer_norm(x, xn, 1e-5, give=[norm_tok_ready])
            split_input()
            dve.tensor_tensor(mv[:, :, :], xn[:, :, :], row_b("b2_3"), ALU.add).then_inc(st.sem, st.one())
            dve.wait_ge(st.sem, st.n)
            ffn(ffn3, residual_into(mv))
            layer_norm(mv, att, 1e-5, "g3", "be3")
            add_to_x(att[:, :, :])
            dve.sem_inc(store_done, 1)


def kernel(**inputs):
    import numpy as np
    import concourse.bacc as _bacc
    from concourse import mybir as _mybir
    from concourse.bass_utils import run_bass_kernel_spmd as _run

    g = {k: np.asarray(v) for k, v in inputs.items()}
    lay = np.ascontiguousarray

    def chunks(a):
        return a.reshape(-1, P).T

    def weights(a):
        e, k, m = a.shape
        return a.reshape(e, k // P, P, m).transpose(0, 2, 1, 3).reshape(e, P, -1)

    ws = g["L3_xattn_w_sim"]
    beta0 = g["L0_ffn_beta"]
    cols = np.concatenate([
        chunks(g["L0_xattn_wq_b"]), chunks(g["L0_xattn_wk_b"]), chunks(g["L0_ffn_gamma"]),
        chunks(beta0), chunks(beta0[0]), chunks(g["L0_ffn_b1"]), chunks(g["L1_xattn_bk"]),
        chunks(g["L1_xattn_bq"]), chunks(g["L1_xattn_bg"]), chunks(g["L1_xattn_bl"]), chunks(g["L1_ffn_b1"]),
        chunks(g["L2_xattn_bq"]), chunks(g["L2_xattn_bk"]), chunks(ws[:D]), chunks(ws[D:2 * D]),
        chunks(ws[2 * D:]), chunks(g["L3_xattn_b_qv"]), chunks(g["L3_ffn_b1"][0])], axis=1)
    rows = np.concatenate([g[n].reshape(-1) for n in (
        "L0_xattn_wv_b", "L0_xattn_wo_b", "L1_xattn_bv", "L1_xattn_bo", "L1_xattn_bm", "L1_xattn_g1",
        "L1_xattn_b1", "L1_xattn_g2", "L1_xattn_b2", "L2_xattn_bv", "L2_xattn_bo")] + [
        g["L3_ffn_b2"][0], g["L3_ffn_gamma"], g["L3_ffn_beta"], g["L1_ffn_bg"], g["L1_ffn_bias"],
        g["L3_xattn_b_sim"]]).reshape(1, -1)
    sq = np.concatenate([
        g["L0_xattn_wq_w"].T, g["L0_xattn_wk_w"].T, g["L0_xattn_wv_w"].T, g["L0_xattn_wo_w"].T,
        g["L0_ffn_Wg"], g["L1_xattn_Wk"], g["L1_xattn_Wv"], g["L1_ffn_Wg"], g["L2_xattn_Wq"].T,
        g["L2_xattn_Wk"].T, g["L2_xattn_Wv"].T, g["L2_xattn_Wo"].T, g["L2_ffn_router_w"].T,
        weights(g["L3_xattn_W_qv"][None])[0]], axis=1)
    arrays = {
        "x_in": g["x"].transpose(1, 0, 2),
        "ctx_in": g["ctx_1024"].transpose(1, 0, 2),
        "ctxT_in": g["ctx_1024"].reshape(T, D).T,
        "cols_in": cols, "rows_in": rows, "sq_in": sq,
        "w0_in": np.concatenate([g["L0_ffn_W1"], weights(g["L0_ffn_W2"])], axis=2),
        "w1q_in": g["L1_xattn_Wq"].transpose(1, 0, 2),
        "w1o_in": g["L1_xattn_Wo"].reshape(H, D, D).transpose(1, 0, 2),
        "w1m_in": np.concatenate([g["L1_xattn_Wg"], g["L1_xattn_Wl"], weights(g["L1_xattn_Wm"][None])[0]], axis=1),
        "w1_in": np.concatenate([g["L1_ffn_W1"], weights(g["L1_ffn_W2"])], axis=2),
        "w2_in": np.concatenate([g["L2_ffn_w_gate"], g["L2_ffn_w_up"], weights(g["L2_ffn_w_down"])], axis=2),
        "w3_in": np.concatenate([g["L3_ffn_w1"][0], weights(g["L3_ffn_w2"][0:1])[0]], axis=1),
        "b2_0_in": g["L0_ffn_b2"], "b2_1_in": g["L1_ffn_b2"],
    }
    arrays = {k: lay(v) for k, v in arrays.items()}
    nc = _bacc.Bacc("TRN2", target_bir_lowering=False, num_devices=1)
    args = [nc.dram_tensor(k, v.shape, _mybir.dt.from_np(v.dtype), kind="ExternalInput").ap()
            for k, v in arrays.items()]
    out = nc.dram_tensor("out_dram", (P, NB, D), _mybir.dt.float32, kind="ExternalOutput").ap()
    build(nc, *args, out)
    result = _run(nc, [arrays], core_ids=[0])
    return result.results[0]["out_dram"].transpose(1, 0, 2)
```

```python
import concourse.bass as bass
from concourse import mybir
from contextlib import ExitStack

NB, P, D = 8, 128, 128
T = NB * P
H = 16
DH = D // H
E0, F0 = 8, 512
E1, F1 = 16, 256
E2, F2 = 8, 512
F3 = 512
FM = 512
KEEP = int(P * 0.9)
DROP = P - KEEP
assert 8 < DROP <= 16

COLS, ROWS, SQS = {}, {}, {}


def _place(table, names):
    at = 0
    for name, n in names:
        table[name] = (at, n)
        at += n
    table["end"] = at


_place(COLS, [("bq0", 1), ("bk0", 1), ("gamma0", E0), ("beta0", E0 + 1), ("b1_0", E0 * F0 // P),
              ("bk1", 1), ("bq1", H), ("bg1", FM // P), ("bl1", FM // P), ("b1_1", E1 * F1 // P),
              ("bq2", 1), ("bk2", 1), ("w1s", 1), ("w2s", 1), ("w3s", 1), ("b1_3", F3 // P)])
_place(ROWS, [("bv0", D), ("bo0", D), ("bv1", D), ("bo1", D), ("bm1", D), ("g1", D), ("be1", D),
              ("g2", D), ("be2", D), ("bv2", D), ("bo2", D), ("b2_3", D), ("g3", D), ("be3", D),
              ("bqv", D), ("rbg", E1), ("rbias", E1), ("bsim", 1)])
_place(SQS, [("wq0", D), ("wk0", D), ("wv0", D), ("wo0", D), ("r0", E0), ("wk1", D), ("wv1", D),
             ("r1", E1), ("wq2", D), ("wk2", D), ("wv2", D), ("wo2", D), ("r2", E2), ("wqv", 4 * D)])


def stages(order, groups, current, previous):
    for step in range(groups):
        for stage, positions, lag in order:
            for back, on in ((0, current), (1, previous)):
                n = step - lag + back * groups
                if on and n in positions and 0 <= n < groups:
                    yield stage, n, back


def pipelined(eng, order, groups, iterations, close):
    for stage, n, back in stages(order, groups, True, False):
        stage(0, n)
    close()
    with eng.Fori(1, iterations) as it:
        for stage, n, back in stages(order, groups, True, True):
            stage(it - back, n)
        close()
    for stage, n, back in stages(order, groups, False, True):
        stage(iterations - 1, n)
    close()


class Steps:

    def __init__(self, eng, sem):
        self.eng, self.sem, self.n = eng, sem, 0

    def one(self):
        self.n += 1
        return 1

    def close(self):
        if self.n:
            self.eng.wait_ge(self.sem, self.n)
            self.eng.sem_inc(self.sem, -self.n)
            self.n = 0


def build(nc, x_in, ctx_in, ctxT_in, cols_in, rows_in, sq_in, w0_in, w1q_in, w1o_in, w1m_in, w1_in,
          w2_in, w3_in, b2_0_in, b2_1_in, out):
    F32 = mybir.dt.float32
    F32R = mybir.dt.float32r
    U32 = mybir.dt.uint32
    ALU = mybir.AluOpType
    ACT = mybir.ActivationFunctionType
    X_AX = mybir.AxisListType.X

    ctx = ExitStack()
    with ctx:
        def sb(name, shape, dt=F32):
            return ctx.enter_context(nc.sbuf_tensor(name, shape, dt))

        def sem(name):
            return ctx.enter_context(nc.semaphore(name))

        x = sb("x_tok", [P, NB, D])
        xn = sb("xn_tok", [P, NB, D])
        xnT = sb("xn_feat", [D, T])
        ctxT = sb("ctx_feat", [D, T])
        kT = sb("keys_feat", [D, T])
        qT = sb("queries_feat", [D, T])
        iv = sb("values_ctx", [P, NB, D])
        mv = sb("values_state", [P, NB, D])
        xm = iv
        ctx_tok = mv
        att = sb("att_tok", [P, NB, D])
        attT = sb("att_feat", [D, T])
        prob = sb("probabilities", [P, 2, H, P])
        probT = sb("probabilities_keys", [P, 2, H, P])
        scratch = sb("scratch", [P, 10, 512])

        def part(at, **sizes):
            return scratch[:, at:at + 2, :].rearrange("p a (h t) -> p a h t", **sizes)

        q_b_hi = sb("queries_batch_hi", [D, 2, P], F32R)
        q_b_lo = sb("queries_batch_lo", [D, 2, P], F32R)
        k_mask_hi = sb("keys_masked_hi", [D, 2, 4, P], F32R)
        k_mask_lo = sb("keys_masked_lo", [D, 2, 4, P], F32R)
        head_mask = sb("head_mask", [P, 4])
        slot_mask = sb("slot_mask", [P, 4, 32])
        v_wide = part(2, t=32)
        v_kept = part(4, t=32)
        qh = part(0, t=P)
        qmk = part(2, t=P)
        mva = part(4, t=D)
        heads = part(6, t=D)
        headsT = part(8, t=P)
        hT = sb("hidden", [P, 2, 4, 512])
        normed = sb("expert_input", [D, 2, T])
        w_in = sb("weights_in", [P, 1024])
        w_hi = sb("weights_in_hi", [P, 2, 1024], F32R)
        w_lo = sb("weights_in_lo", [P, 2, 1024], F32R)
        w_out = sb("weights_out", [P, 2, 512])
        in_hi = sb("input_hi", [D, 2, T], F32R)
        in_lo = sb("input_lo", [D, 2, T], F32R)
        cols = sb("cols", [P, COLS["end"]])
        rows = sb("rows", [P, ROWS["end"]])
        sq = sb("square_weights", [D, SQS["end"]])
        wq1 = sb("wq1", [D, H, D])
        wo1 = sb("wo1", [D, H, D])
        b2_0 = sb("b2_0", [E0, D])
        b2_1 = sb("b2_1", [E1, D])
        ident = sb("identity", [P, P])
        ones = sb("ones", [P, 1])
        neg_half = sb("neg_half", [P, NB])
        expert_no = sb("expert_number", [P, E1])
        stats = sb("stats", [P, NB, 6])
        mean_var = sb("mean_var", [P, NB, 2])
        var_eps = sb("var_eps", [P, NB])
        rstd = sb("rstd", [P, NB])
        neg_max = sb("neg_max", [P, 8, 4])
        row_max = sb("row_max", [P, 2, 4])
        z = sb("exp_sums", [P, 2, H])
        r = sb("inverse_sums", [P, 2, H])
        self_arg = sb("self_arg", [P, 2, 4])
        self_exp = sb("self_exp", [P, 2, 4])
        self_w = sb("self_weight", [P, 2, 4])
        col_sum = sb("column_sums", [P, 2, H])
        ranked = sb("ranked", [H, P + 8])
        top = sb("top", [H, 2, 8])
        kept = sb("kept", [H, P])
        logits = sb("logits", [P, NB, E1])
        best = sb("best", [P, NB, 8])
        best_at = sb("best_at", [P, NB, 8], U32)
        best_no = sb("best_number", [P, NB, 2])
        gap = sb("gap", [P, NB])
        gap_exp = sb("gap_exp", [P, NB])
        w_a = sb("weight_first", [P, NB])
        w_b = sb("weight_second", [P, NB])
        cw = sb("combine_weights", [P, NB, E1])
        cw_b = sb("combine_weights_second", [P, NB, E1])
        cw_sum = sb("combine_sum", [P, NB])
        cwT = attT[0:E1, :]
        m_sim = sb("row_maxima", [P, NB])
        batt = probT[0:NB, 1, 8, :]
        batt2 = probT[0:NB, 1, 9, :]
        bstat = sb("row_weights_stats", [NB, 4])
        batt_col = sb("row_weights", [P, NB])
        hc_bar = sb("hc_bar", [D, NB])

        def col(name, i=0, n=1):
            at = COLS[name][0] + i
            return cols[:, bass.ds(at, n)] if not isinstance(at, int) else cols[:, at:at + n]

        def row(name):
            at, n = ROWS[name]
            return rows[:, at:at + n]

        def row_b(name):
            return row(name)[:, None, :].broadcast_to([P, NB, D])

        def w(name, i=0, n=None):
            at, size = SQS[name]
            return sq[:, at + i:at + i + (n or size)]

        bank = [ctx.enter_context(nc.psum_tensor(f"bank{i}", [P, 512], F32)) for i in range(8)]

        def b4(i):
            return bank[i][:, :].rearrange("p (a b) -> p a b", a=4)

        x_loaded = sem("x_loaded")
        ctx_loaded = sem("ctx_loaded")
        cols_loaded = sem("cols_loaded")
        rows_loaded = sem("rows_loaded")
        sq_loaded = sem("sq_loaded")
        sq_rest_loaded = sem("sq_rest_loaded")
        w1_attn_loaded = sem("w1_attn_loaded")
        ctx_tok_loaded = sem("ctx_tok_loaded")
        b2_loaded = sem("b2_loaded")
        w_in_loaded = sem("w_in_loaded")
        w_loaded_free = sem("w_loaded_free")
        w_out_loaded = [sem("w_out_loaded0"), sem("w_out_loaded1")]
        consts_dve = sem("consts_dve")
        consts_pe = sem("consts_pe")
        dve_steps = sem("dve_steps")
        act_steps = sem("act_steps")
        pool_steps = sem("pool_steps")
        var_ready = sem("var_ready")
        rstd_ready = sem("rstd_ready")
        norm_tok_ready = sem("norm_tok_ready")
        transposed = sem("transposed")
        feat_ready = sem("feat_ready")
        feat_ready_dve = sem("feat_ready_dve")
        projected = sem("projected")
        qkv_ready = sem("qkv_ready")
        qkv_ready_pool = sem("qkv_ready_pool")
        qk_ready = sem("qk_ready")
        qk_free = sem("qk_free")
        scores_done = sem("scores_done")
        neg_max_ready = sem("neg_max_ready")
        probs_ready = sem("probs_ready")
        probsT_done = sem("probsT_done")
        probsT_ready = sem("probsT_ready")
        out_done = sem("out_done")
        out_free = sem("out_free")
        colsum_ready = sem("colsum_ready")
        ranked_done = sem("ranked_done")
        kept_ready = sem("kept_ready")
        keptT_done = sem("keptT_done")
        v_kept_ready = sem("v_kept_ready")
        att_ready = sem("att_ready")
        exps_done = sem("exps_done")
        scores_free = sem("scores_free")
        inverse_ready = sem("inverse_ready")
        turn_free = sem("turn_free")
        v_free = sem("v_free")
        v_ready = sem("v_ready")
        probsT_copied = sem("probsT_copied")
        y_attn_done = sem("y_attn_done")
        heads_q_done = sem("heads_q_done")
        q_free = sem("q_free")
        qh_ready = sem("qh_ready")
        qh_ready_pool = sem("qh_ready_pool")
        qmk_ready = sem("qmk_ready")
        probs_ready_dve = sem("probs_ready_dve")
        self_w_ready = sem("self_w_ready")
        mva_ready = sem("mva_ready")
        pv_done = sem("pv_done")
        own_free = sem("own_free")
        heads_ready = sem("heads_ready")
        headsT_done = sem("headsT_done")
        headsT_ready = sem("headsT_ready")
        wo_done = sem("wo_done")
        wo_free = sem("wo_free")
        router_done = sem("router_done")
        gap_ready = sem("gap_ready")
        gap_exp_ready = sem("gap_exp_ready")
        cw_ready = sem("cw_ready")
        cwT_done = sem("cwT_done")
        cwT_ready = sem("cwT_ready")
        bias_done = sem("bias_done")
        bias_free = sem("bias_free")
        input_ready = sem("input_ready")
        h_done = sem("h_done")
        g_done = sem("g_done")
        h_ready = sem("h_ready")
        input_hi_ready = sem("input_hi_ready")
        w_in_ready = [sem("w_in_ready0"), sem("w_in_ready1")]
        w_in_free = [sem("w_in_free0"), sem("w_in_free1")]
        w_out_free = [sem("w_out_free0"), sem("w_out_free1")]
        y_done = sem("y_done")
        y_free = sem("y_free")
        result_ready = sem("result_ready")
        store_done = sem("store_done")
        x3_sim = sem("x3_sim")
        x3_sims = sem("x3_sims")
        x3_neg = sem("x3_neg")
        x3_exp = sem("x3_exp")
        x3_own = sem("x3_own")
        x3_prob = sem("x3_prob")
        x3_t = sem("x3_t")
        x3_te = sem("x3_te")
        x3_pv = sem("x3_pv")
        x3_m = sem("x3_m")
        x3_mT = sem("x3_mT")
        x3_arg = sem("x3_arg")
        x3_bexp = sem("x3_bexp")
        x3_b = sem("x3_b")
        x3_bT = sem("x3_bT")
        x3_bTe = sem("x3_bTe")
        x3_hc = sem("x3_hc")
        x3_feats = sem("x3_feats")
        x3_out = sem("x3_out")

        block = ctx.enter_context(nc.Block())

        SC0 = float(DH) ** -0.5
        SC1 = float(D) ** -0.5
        PAD, GONE = -1.0e30, -3.0e38

        LOW, HIGH = 0, 1

        class FFN:
            def __init__(self, experts, width, gated, first, bias, up_bias):
                self.E, self.FC, self.gated = experts, width // P, gated
                self.first, self.bias, self.up_bias = first, bias, up_bias

            def w1(self, part, sub, fc):
                return part[:, sub, fc * P:(fc + 1) * P]

            def up(self, part, sub, fc):
                at = self.FC * P + fc * P
                return part[:, sub, at:at + P]

            def w2(self, sub, fc):
                return w_out[:, sub, fc * D:(fc + 1) * D]

            def in_columns(self):
                return (2 if self.gated else 1) * self.FC * P

            def columns(self):
                return self.in_columns() + self.FC * D

            def hidden_bank(self, n, k):
                return k % 3 if self.gated else (self.FC * n + k) % 4

            def output_bank(self, n):
                return 6 + n % 2 if self.gated else 4 + n

        ffn0 = FFN(E0, F0, False, ACT.Relu, "b1_0", None)
        mlp1 = FFN(1, FM, True, ACT.Relu, "bg1", "bl1")
        ffn1 = FFN(E1, F1, False, ACT.Relu, "b1_1", None)
        ffn2 = FFN(E2, F2, True, ACT.Silu, None, None)
        ffn3 = FFN(1, F3, False, ACT.Relu, "b1_3", None)

        def halves(eng, order, f, close, between={}, before_last=None):
            groups, iterations = (2, 1) if f.E == 1 else (4, f.E // 2)
            last = order[-1][0]
            for stage, n, back in stages(order, groups, True, False):
                if stage is last and n in between:
                    between[n]()
                stage(0, n)
            close()
            if iterations > 1:
                with eng.Fori(1, iterations) as i:
                    for stage, n, back in stages(order, groups, True, True):
                        stage(i - back, n)
                    close()
            for stage, n, back in stages(order, groups, False, True):
                if before_last and stage is last and n == groups - 1:
                    before_last()
                stage(iterations - 1, n)
            close()

        @block.sync
        def _(sp):
            sp.dma_start(x[:, :, :], x_in).then_inc(x_loaded, 16)
            sp.dma_start(ctxT[:, :], ctxT_in).then_inc(ctx_loaded, 16)
            first = SQS["wk1"][0]
            sp.dma_start(sq[:, 0:first], sq_in[:, 0:first]).then_inc(sq_loaded, 16)
            sp.dma_start(cols[:, :], cols_in).then_inc(cols_loaded, 16)
            sp.dma_start(rows[:, :], rows_in.broadcast_to([P, ROWS["end"]])).then_inc(rows_loaded, 16)
            sp.dma_start(sq[:, first:SQS["end"]], sq_in[:, first:SQS["end"]]).then_inc(sq_rest_loaded, 16)
            sp.dma_start(b2_0[:, :], b2_0_in).then_inc(b2_loaded, 16)
            sp.dma_start(b2_1[:, :], b2_1_in).then_inc(b2_loaded, 16)
            sp.sem_inc(w_loaded_free, 1)
            for sub in range(2):
                sp.sem_inc(w_out_free[sub], 1)

            def load_weights(source, f, sub):
                cut, end = f.in_columns(), f.columns()
                sp.wait_ge(w_loaded_free, 1)
                sp.sem_inc(w_loaded_free, -1)
                sp.dma_start(w_in[:, 0:cut], source[:, 0:cut]).then_inc(w_in_loaded, 16)
                sp.wait_ge(w_out_free[sub], 1)
                sp.sem_inc(w_out_free[sub], -1)
                sp.dma_start(w_out[:, sub, 0:end - cut], source[:, cut:end]).then_inc(w_out_loaded[sub], 16)

            def load_experts(source, f):
                with sp.Fori(0, f.E // 2) as i:
                    for sub in range(2):
                        load_weights(source[bass.ds(2 * i + sub, 1), :, :]
                                     .rearrange("e p n -> p (e n)"), f, sub)

            load_experts(w0_in, ffn0)
            sp.dma_start(wq1[:, :, :], w1q_in).then_inc(w1_attn_loaded, 16)
            sp.dma_start(wo1[:, :, :], w1o_in).then_inc(w1_attn_loaded, 16)
            load_weights(w1m_in, mlp1, 0)
            load_experts(w1_in, ffn1)
            sp.dma_start(ctx_tok[:, :, :], ctx_in).then_inc(ctx_tok_loaded, 16)
            load_experts(w2_in, ffn2)
            load_weights(w3_in, ffn3, 0)
            for half in range(2):
                sp.wait_ge(result_ready, 1)
                sp.sem_inc(result_ready, -1)
                four = slice(4 * half, 4 * half + 4)
                sp.dma_start(out[:, four, :], x[:, four, :]).then_inc(store_done, 16)
            sp.wait_ge(store_done, 32)

        @block.gpsimd
        def _(pool):
            st = Steps(pool, pool_steps)
            pool.memset(ident[:, :], 0.0).then_inc(st.sem, st.one())
            pool.memset(head_mask[:, :], 1.0).then_inc(st.sem, st.one())
            pool.memset(neg_half[:, :], -0.5).then_inc(st.sem, st.one())
            pool.memset(ones[:, :], 1.0).then_inc(st.sem, st.one())
            pool.memset(slot_mask[:, :, :], 1.0).then_inc(st.sem, st.one())
            pool.iota(expert_no[:, :], [[1, E1]], base=0, channel_multiplier=0,
                      allow_small_or_imprecise_dtypes=True).then_inc(st.sem, st.one())
            pool.wait_ge(st.sem, st.n)
            pool.affine_select(out=ident[:, :], in_=ident[:, :], compare_op=ALU.not_equal,
                               fill=1.0, base=0, pattern=[[-1, P]], channel_multiplier=1)\
                .then_inc(st.sem, st.one())
            pool.affine_select(out=slot_mask[:, :, :], in_=slot_mask[:, :, :], compare_op=ALU.is_ge, fill=0.0,
                               base=0, pattern=[[-DH, 4], [1, 32]], channel_multiplier=0)\
                .then_inc(st.sem, st.one())
            pool.wait_ge(st.sem, st.n)
            pool.affine_select(out=slot_mask[:, :, :], in_=slot_mask[:, :, :], compare_op=ALU.is_ge, fill=0.0,
                               base=DH - 1, pattern=[[DH, 4], [-1, 32]], channel_multiplier=0)\
                .then_inc(st.sem, st.one())
            for g in range(4):
                m = head_mask[32 * g:32 * g + 32, :]
                pool.wait_ge(st.sem, st.n)
                pool.affine_select(out=m, in_=m, compare_op=ALU.is_ge, fill=0.0, base=0,
                                   pattern=[[-DH, 4]], channel_multiplier=1).then_inc(st.sem, st.one())
                pool.wait_ge(st.sem, st.n)
                pool.affine_select(out=m, in_=m, compare_op=ALU.is_ge, fill=0.0, base=DH - 1,
                                   pattern=[[DH, 4]], channel_multiplier=-1).then_inc(st.sem, st.one())
            pool.wait_ge(st.sem, st.n)
            pool.sem_inc(consts_pe, 1)
            pool.sem_inc(consts_dve, 1)
            st.close()

            def inverse_roots(halves=(0, 1)):
                for half in halves:
                    four = slice(4 * half, 4 * half + 4)
                    pool.wait_ge(var_ready, 1)
                    pool.sem_inc(var_ready, -1)
                    pool.tensor_tensor(rstd[:, four], var_eps[:, four], neg_half[:, four], ALU.pow)\
                        .then_inc(rstd_ready, 1)

            def narrow_attention():
                pool.wait_ge(qkv_ready_pool, 1)
                pool.sem_inc(qkv_ready_pool, -1)

                def spread_queries_keys(it, n):
                    pool.wait_ge(qk_free, 1)
                    pool.sem_inc(qk_free, -1)
                    tok = bass.ds((2 * it + n // 4) * P, P)
                    for masked, keys in ((k_mask_hi, in_hi), (k_mask_lo, in_lo)):
                        pool.tensor_tensor(masked[:, n // 4, :, :],
                                           keys[:, 0, tok][:, None, :].broadcast_to([D, 4, P]),
                                           head_mask[:, :, None].broadcast_to([D, 4, P]), ALU.mult)\
                            .then_inc(st.sem, st.one())
                    if n == 0 and isinstance(it, int):
                        pool.wait_ge(qkv_ready_pool, 1)
                        pool.sem_inc(qkv_ready_pool, -1)
                    pool.tensor_copy(q_b_hi[:, n // 4, :], qT[:, tok]).then_inc(st.sem, st.one())
                    pool.wait_ge(st.sem, st.n)
                    pool.tensor_tensor(q_b_lo[:, n // 4, :], qT[:, tok], q_b_hi[:, n // 4, :],
                                       ALU.subtract).then_inc(st.sem, st.one())
                    pool.wait_ge(st.sem, st.n)
                    pool.sem_inc(qk_ready, 1)

                def spread_values(it, n):
                    pool.wait_ge(v_free, 1)
                    pool.sem_inc(v_free, -1)
                    four = [P, 4, 4, 32]
                    v_b = iv[:, bass.ds(2 * it + n // 4, 1), :].rearrange("p b (j c) -> p (b j) c", j=4)
                    pool.tensor_tensor(v_wide[:, n // 4, :, :].rearrange("p (j i) c -> p j i c", j=4),
                                       v_b[:, :, None, :].broadcast_to(four),
                                       slot_mask[:, None, :, :].broadcast_to(four), ALU.mult)\
                        .then_inc(v_ready, 1)

                def normalise(it, n):
                    pool.wait_ge(inverse_ready, 1)
                    pool.sem_inc(inverse_ready, -1)
                    h = slice(4 * (n % 4), 4 * (n % 4) + 4)
                    pool.tensor_tensor(prob[:, n // 4, h, :], prob[:, n // 4, h, :],
                                       r[:, n // 4, h][:, :, None].broadcast_to([P, 4, P]), ALU.mult)\
                        .then_inc(probs_ready, 1)

                for sub in range(2):
                    pool.sem_inc(qk_free, 1)
                    pool.sem_inc(v_free, 1)
                pipelined(pool, [(spread_queries_keys, (0, 4), 0), (spread_values, (0, 4), 5),
                                 (normalise, range(8), 5)], 8, NB // 2, st.close)
                pool.wait_ge(qk_free, 2)
                pool.sem_inc(qk_free, -2)
                pool.wait_ge(v_free, 2)
                pool.sem_inc(v_free, -2)

            def split_weights(f, sub):
                n = slice(0, f.in_columns())
                pool.wait_ge(w_in_loaded, 16)
                pool.sem_inc(w_in_loaded, -16)
                pool.wait_ge(w_in_free[sub], 1)
                pool.sem_inc(w_in_free[sub], -1)
                pool.tensor_scalar(w_hi[:, sub, n], w_in[:, n], 1.0, None, ALU.mult)\
                    .then_inc(st.sem, st.one())
                pool.wait_ge(st.sem, st.n)
                pool.tensor_tensor(w_lo[:, sub, n], w_in[:, n], w_hi[:, sub, n], ALU.subtract)\
                    .then_inc(st.sem, st.one())
                pool.wait_ge(st.sem, st.n)
                pool.sem_inc(w_in_ready[sub], 1)
                pool.sem_inc(w_loaded_free, 1)
                st.close()

            def split_other_experts(f):
                split_weights(f, 1)
                with pool.Fori(1, f.E // 2):
                    for sub in range(2):
                        split_weights(f, sub)

            def wide_attention():
                def self_products(it, n):
                    pool.wait_ge(qh_ready_pool, 1)
                    pool.sem_inc(qh_ready_pool, -1)
                    tok = bass.ds((2 * it + n // 4) * P, P)
                    pool.tensor_tensor(qmk[:, n % 2, :, :], qh[:, n % 2, :, :],
                                       qT[:, tok][:, None, :].broadcast_to([P, 4, P]), ALU.mult)\
                        .then_inc(qmk_ready, 1)

                def self_values(it, n):
                    pool.wait_ge(self_w_ready, 1)
                    pool.sem_inc(self_w_ready, -1)
                    pool.tensor_tensor(mva[:, n % 2, :, :],
                                       mv[:, bass.ds(2 * it + n // 4, 1), :].broadcast_to([P, 4, D]),
                                       self_w[:, n % 2, :, None].broadcast_to([P, 4, D]), ALU.mult)\
                        .then_inc(mva_ready, 1)

                pipelined(pool, [(self_values, range(8), 2), (self_products, range(8), 0)],
                          8, NB // 2, lambda: None)

            for sub in range(2):
                pool.sem_inc(w_in_free[sub], 1)
            inverse_roots()
            narrow_attention()
            split_weights(ffn0, 0)
            inverse_roots()
            inverse_roots()
            split_other_experts(ffn0)
            inverse_roots()
            split_weights(mlp1, 0)
            wide_attention()
            inverse_roots()
            inverse_roots((0, 0, 1, 1))
            split_weights(ffn1, 0)
            split_other_experts(ffn1)
            inverse_roots()
            narrow_attention()
            split_weights(ffn2, 0)
            inverse_roots()
            split_other_experts(ffn2)
            inverse_roots()
            split_weights(ffn3, 0)
            inverse_roots()
            inverse_roots()

        @block.scalar
        def _(act):
            st = Steps(act, act_steps)

            def evacuate_transposed(dst, also=(), split=False):
                for half in range(2):
                    act.wait_ge(transposed, 1)
                    act.sem_inc(transposed, -1)
                    tokens = slice(half * 512, (half + 1) * 512)
                    act.activation(dst[:, tokens], bank[half][:, :], ACT.Copy).then_inc(st.sem, st.one())
                    if split:
                        act.activation(in_hi[:, 0, tokens], bank[half][:, :], ACT.Copy)\
                            .then_inc(st.sem, st.one())
                        act.wait_ge(st.sem, st.n)
                        act.sem_inc(input_hi_ready, 1)
                act.wait_ge(st.sem, st.n)
                act.sem_inc(feat_ready, 1)
                for token in also:
                    act.sem_inc(token, 1)
                st.close()

            def narrow_attention(prune):
                def exps(it, n):
                    act.wait_ge(neg_max_ready, 1)
                    act.sem_inc(neg_max_ready, -1)
                    for i in range(4):
                        h = 4 * (n % 4) + i
                        act.activation(prob[:, n // 4, h, :], b4(n % 2)[:, i, :], ACT.Exp,
                                       bias=neg_max[:, n, i:i + 1], accum_out=z[:, n // 4, h:h + 1])\
                            .then_inc(st.sem, st.one())
                    act.wait_ge(st.sem, st.n)
                    act.sem_inc(scores_free, 1)
                    act.sem_inc(exps_done, 1)

                def copy_probsT(it, n):
                    act.wait_ge(probsT_done, 1)
                    act.sem_inc(probsT_done, -1)
                    h = 4 * (n % 4)
                    act.activation(probT[:, n // 4, h:h + 4, :], b4(2 + n % 2), ACT.Copy)\
                        .then_inc(st.sem, st.one())
                    act.wait_ge(st.sem, st.n)
                    act.sem_inc(probsT_ready, 1)
                    act.sem_inc(turn_free, 1)
                    act.sem_inc(probsT_copied, 1)

                if prune:
                    pipelined(act, [(exps, range(8), 0), (copy_probsT, range(8), 2)], 8, NB // 2, st.close)
                else:
                    pipelined(act, [(exps, range(8), 0)], 8, NB // 2, st.close)

            def wide_attention():
                def copy_probsT(it, n):
                    act.wait_ge(probsT_done, 1)
                    act.sem_inc(probsT_done, -1)
                    act.activation(probT[:, 0, 4 * (n % 2):4 * (n % 2) + 4, :], b4(3), ACT.Copy)\
                        .then_inc(probsT_ready, 1)

                def copy_headsT(it, n):
                    act.wait_ge(headsT_done, 1)
                    act.sem_inc(headsT_done, -1)
                    act.activation(headsT[:, n % 2, :, :], b4(5), ACT.Copy).then_inc(headsT_ready, 1)

                def exps(it, n):
                    act.wait_ge(neg_max_ready, 1)
                    act.sem_inc(neg_max_ready, -1)
                    for i in range(4):
                        act.activation(prob[:, 0, 4 * (n % 2) + i, :], b4(1 + n % 2)[:, i, :],
                                       ACT.Exp, bias=neg_max[:, n, i:i + 1], scale=SC1,
                                       accum_out=z[:, 0, 4 * (n % 2) + i:4 * (n % 2) + i + 1])\
                            .then_inc(st.sem, st.one())
                    act.activation(self_exp[:, n % 2, :], self_arg[:, n % 2, :], ACT.Exp)\
                        .then_inc(st.sem, st.one())
                    act.wait_ge(st.sem, st.n)
                    act.sem_inc(probs_ready, 1)
                    act.sem_inc(probs_ready_dve, 1)

                pipelined(act, [(copy_headsT, range(8), 5), (copy_probsT, range(8), 3), (exps, range(8), 1)],
                          8, NB // 2, st.close)

            def router_exp():
                act.wait_ge(gap_ready, 1)
                act.sem_inc(gap_ready, -1)
                act.activation(gap_exp[:, :], gap[:, :], ACT.Exp).then_inc(gap_exp_ready, 1)

            def ffn(f):
                def hidden(i, n):
                    half, e = n % 2, 2 * i + n // 2
                    for fc in range(f.FC):
                        act.wait_ge(h_done, 1)
                        act.sem_inc(h_done, -1)
                        kw = {"bias": col(f.bias, e * f.FC + fc)} if f.bias else {}
                        act.activation(hT[:, half, fc, :], bank[f.hidden_bank(n, fc)][:, :], f.first, **kw)\
                            .then_inc(g_done if f.gated else h_ready, 1)
                    if half == 1:
                        act.sem_inc(w_in_free[n // 2], 1)

                order = [(hidden, range(4), 0)]
                halves(act, order, f, st.close, {2: router_exp} if f.E > 1 else {})

            act.wait_ge(cols_loaded, 16)
            evacuate_transposed(xnT)
            narrow_attention(False)
            evacuate_transposed(xnT)
            evacuate_transposed(kT, also=[feat_ready_dve])
            ffn(ffn0)
            evacuate_transposed(xnT)
            wide_attention()
            evacuate_transposed(xnT, split=True)
            ffn(mlp1)
            evacuate_transposed(xnT, split=True)
            ffn(ffn1)
            evacuate_transposed(xnT)
            narrow_attention(True)
            evacuate_transposed(xnT, split=True)
            ffn(ffn2)
            evacuate_transposed(xnT, also=[feat_ready_dve])
            for g in range(2):
                act.wait_ge(x3_neg, 1)
                act.sem_inc(x3_neg, -1)
                for i in range(4):
                    b = 4 * g + i
                    act.activation(prob[:, 0, b, :], b4(g)[:, i, :], ACT.Exp,
                                   bias=neg_max[:, g, i:i + 1], accum_out=z[:, 0, b:b + 1])\
                        .then_inc(st.sem, st.one())
                act.wait_ge(st.sem, st.n)
                act.sem_inc(x3_exp, 1)
            act.wait_ge(x3_arg, 1)
            act.sem_inc(x3_arg, -1)
            act.activation(batt2[:, :], batt[:, :], ACT.Exp, bias=bstat[:, 0:1],
                           accum_out=bstat[:, 1:2]).then_inc(st.sem, st.one())
            act.wait_ge(st.sem, st.n)
            act.sem_inc(x3_bexp, 1)
            evacuate_transposed(xnT, split=True)
            ffn(ffn3)

        @block.tensor
        def _(pe):
            def mm(o, l, rh, start=True, stop=True, **kw):
                return pe.matmul(o, l, rh, start=start, stop=stop, **kw)

            def transpose_tiles(src, ready):
                for b in range(NB):
                    if b % 4 == 0:
                        pe.wait_ge(ready, 1)
                        pe.sem_inc(ready, -1)
                    t = pe.transpose(b4(b // 4)[:, b % 4, :], src[:, b, :], ident[:, :])
                    if b % 4 == 3:
                        t.then_inc(transposed, 1)

            def project(weight, src, at):
                for half in range(2):
                    mm(bank[at + half][:, :], weight, src[:, half * 512:(half + 1) * 512])\
                        .then_inc(projected, 1)

            def project_tok(weight, src, at):
                for b in range(NB):
                    m = mm(b4(at + b // 4)[:, b % 4, :], src[:, b * P:(b + 1) * P], weight)
                    if b % 4 == 3:
                        m.then_inc(projected, 1)

            def split_products(o, left, right, start, stop):
                mm(o, left(LOW), right(HIGH), start=start, stop=False)
                mm(o, left(HIGH), right(LOW), start=False, stop=False)
                return mm(o, left(HIGH), right(HIGH), start=False, stop=stop)

            def narrow_attention(prune):
                def scores(it, n):
                    if n % 4 == 0:
                        pe.wait_ge(qk_ready, 1)
                        pe.sem_inc(qk_ready, -1)
                    pe.wait_ge(scores_free, 1)
                    pe.sem_inc(scores_free, -1)
                    p = slice(32 * (n % 4), 32 * (n % 4) + 32)
                    split_products(bank[n % 2][:, :],
                                   lambda part: (q_b_lo, q_b_hi)[part][p, n // 4, :],
                                   lambda part: (k_mask_lo, k_mask_hi)[part][p, n // 4, :, :]
                                   .rearrange("p a b -> p (a b)"), True, True).then_inc(scores_done, 1)

                def turn(it, n):
                    pe.wait_ge(probs_ready, 1)
                    pe.sem_inc(probs_ready, -1)
                    pe.wait_ge(turn_free, 1)
                    pe.sem_inc(turn_free, -1)
                    for i in range(4):
                        t = pe.transpose(b4(2 + n % 2)[:, i, :], prob[:, n // 4, 4 * (n % 4) + i, :],
                                         ident[:, :])
                    t.then_inc(probsT_done, 1)

                def head_outputs(source, parity, groups):
                    for i in range(4):
                        for j in groups:
                            h = 4 * j + i
                            m = mm(bank[6 + parity][32 * j:32 * j + 32, 0:P], source[:, parity, h, :],
                                   probT[:, parity, h, :], start=(i == 0), stop=(i == 3))
                    return m

                def values(it, n):
                    pe.wait_ge(probsT_ready, 1)
                    pe.sem_inc(probsT_ready, -1)
                    if n % 4 == 0:
                        pe.wait_ge(v_ready, 1)
                        pe.sem_inc(v_ready, -1)
                        pe.wait_ge(out_free, 1)
                        pe.sem_inc(out_free, -1)
                    m = head_outputs(v_wide, n // 4, [n % 4])
                    if n % 4 == 3:
                        m.then_inc(out_done, 1)

                def turn_sums(it, n):
                    pe.wait_ge(colsum_ready, 1)
                    pe.sem_inc(colsum_ready, -1)
                    pe.transpose(bank[5][0:H, 0:P], col_sum[:, n // 4, :], ident[:, :])\
                        .then_inc(ranked_done, 1)

                def turn_kept(it, n):
                    pe.wait_ge(kept_ready, 1)
                    pe.sem_inc(kept_ready, -1)
                    pe.transpose(bank[5][:, 256:256 + H], kept[:, :], ident[0:H, 0:H])\
                        .then_inc(keptT_done, 1)

                def values_kept(it, n):
                    pe.wait_ge(v_kept_ready, 1)
                    pe.sem_inc(v_kept_ready, -1)
                    pe.wait_ge(probsT_ready, 4)
                    pe.sem_inc(probsT_ready, -4)
                    pe.wait_ge(out_free, 1)
                    pe.sem_inc(out_free, -1)
                    head_outputs(v_kept, n // 4, range(4)).then_inc(out_done, 1)

                pe.sem_inc(scores_free, 2)
                pe.sem_inc(turn_free, 2)
                pe.sem_inc(out_free, 2)
                if prune:
                    pipelined(pe, [(scores, range(8), 0), (turn, range(8), 3), (turn_sums, (3, 7), 5),
                                   (turn_kept, (3, 7), 6), (values_kept, (3, 7), 7)], 8, NB // 2,
                              lambda: None)
                else:
                    pipelined(pe, [(scores, range(8), 0), (turn, range(8), 3), (values, range(8), 4)],
                              8, NB // 2, lambda: None)
                pe.wait_ge(scores_free, 2)
                pe.sem_inc(scores_free, -2)
                pe.wait_ge(turn_free, 2)
                pe.sem_inc(turn_free, -2)
                pe.wait_ge(out_free, 2)
                pe.sem_inc(out_free, -2)

            def attention_output(weight):
                pe.wait_ge(att_ready, 1)
                pe.sem_inc(att_ready, -1)
                for b in range(NB):
                    m = mm(b4(2 + b // 4)[:, b % 4, :], attT[:, b * P:(b + 1) * P], weight)
                    if b % 4 == 3:
                        m.then_inc(y_attn_done, 1)

            def wide_attention():
                def queries(it, n):
                    pe.wait_ge(q_free, 1)
                    pe.sem_inc(q_free, -1)
                    for i in range(4):
                        m = mm(b4(0)[:, i, :], wq1[:, 4 * (n % 4) + i, :],
                               xnT[:, bass.ds((2 * it + n // 4) * P, P)])
                    m.then_inc(heads_q_done, 1)

                def scores(it, n):
                    pe.wait_ge(qh_ready, 1)
                    pe.sem_inc(qh_ready, -1)
                    for i in range(4):
                        mm(b4(1 + n % 2)[:, i, :], qh[:, n % 2, i, :],
                           kT[:, bass.ds((2 * it + n // 4) * P, P)])
                    pe.wait_ge(qmk_ready, 1)
                    pe.sem_inc(qmk_ready, -1)
                    pe.wait_ge(own_free, 1)
                    pe.sem_inc(own_free, -1)
                    for i in range(4):
                        at = 4 * (n % 2) + i
                        m = mm(bank[7][:, at:at + 1], qmk[:, n % 2, i, :], ones[:, :])
                    m.then_inc(scores_done, 1)

                def turn(it, n):
                    pe.wait_ge(probs_ready, 1)
                    pe.sem_inc(probs_ready, -1)
                    for i in range(4):
                        t = pe.transpose(b4(3)[:, i, :], prob[:, 0, 4 * (n % 2) + i, :], ident[:, :])
                    t.then_inc(probsT_done, 1)

                def values(it, n):
                    pe.wait_ge(probsT_ready, 1)
                    pe.sem_inc(probsT_ready, -1)
                    for i in range(4):
                        m = mm(b4(4)[:, i, :], probT[:, 0, 4 * (n % 2) + i, :],
                               iv[:, bass.ds(2 * it + n // 4, 1), :].rearrange("p a b -> p (a b)"))
                    m.then_inc(pv_done, 1)

                def turn_heads(it, n):
                    pe.wait_ge(heads_ready, 1)
                    pe.sem_inc(heads_ready, -1)
                    for i in range(4):
                        t = pe.transpose(b4(5)[:, i, :], heads[:, n % 2, i, :], ident[:, :])
                    t.then_inc(headsT_done, 1)

                def output(it, n):
                    pe.wait_ge(headsT_ready, 1)
                    pe.sem_inc(headsT_ready, -1)
                    if n % 4 == 0:
                        pe.wait_ge(wo_free, 1)
                        pe.sem_inc(wo_free, -1)
                    for i in range(4):
                        h = 4 * (n % 4) + i
                        m = mm(bank[6][:, 0:D], headsT[:, n % 2, i, :], wo1[:, h, :],
                               start=(h == 0), stop=(h == H - 1))
                    if n % 4 == 3:
                        m.then_inc(wo_done, 1)

                pe.sem_inc(q_free, 1)
                pe.sem_inc(own_free, 1)
                pe.sem_inc(wo_free, 1)
                pipelined(pe, [(queries, range(8), 0), (scores, range(8), 1), (output, range(8), 5),
                               (turn_heads, range(8), 4), (values, range(8), 3), (turn, range(8), 2)],
                          8, NB // 2, lambda: None)
                pe.wait_ge(q_free, 1)
                pe.sem_inc(q_free, -1)
                pe.wait_ge(own_free, 1)
                pe.sem_inc(own_free, -1)
                pe.wait_ge(wo_free, 1)
                pe.sem_inc(wo_free, -1)

            def route(weight, experts, src):
                for b in range(NB):
                    m = mm(bank[7][:, b * experts:(b + 1) * experts], src[:, b * P:(b + 1) * P], weight)
                m.then_inc(router_done, 1)

            def turn_weights(experts):
                pe.wait_ge(cw_ready, 1)
                pe.sem_inc(cw_ready, -1)
                for b in range(NB):
                    t = pe.transpose(b4(6 + b // 4)[0:experts, b % 4, :], cw[:, b, 0:experts], ident[:, :])
                t.then_inc(cwT_done, 1)

            def bias_products(b2, experts):
                pe.wait_ge(b2_loaded, 32)
                pe.wait_ge(cwT_ready, 1)
                pe.sem_inc(cwT_ready, -1)
                for b in range(NB):
                    m = mm(b4(6 + b // 4)[:, b % 4, :], cwT[0:experts, b * P:(b + 1) * P], b2[0:experts, :])
                m.then_inc(bias_done, 1)
                pe.wait_ge(bias_free, 1)
                pe.sem_inc(bias_free, -1)

            def ffn(f, b2=None):
                def hidden(i, n):
                    sub, half = n // 2, n % 2
                    begun = n > 0 or not isinstance(i, int)
                    if half == 0:
                        pe.wait_ge(w_in_ready[sub], 1)
                        pe.sem_inc(w_in_ready[sub], -1)
                    if f is ffn0 or (isinstance(i, int) and n < 2):
                        pe.wait_ge(input_ready, 1)
                        pe.sem_inc(input_ready, -1)
                    at = sub if f is ffn0 else 0
                    tokens = slice(half * 512, (half + 1) * 512)
                    for fc in range(f.FC):
                        if f.FC == 4 and begun and not f.gated:
                            pe.wait_ge(h_ready, fc + 1)
                        elif f.gated and (begun or fc == 3):
                            pe.wait_ge(h_ready, f.FC + (fc == 3) if begun else 1)
                        at_bank = f.hidden_bank(n, fc)
                        m = split_products(bank[at_bank][:, :],
                                           lambda part: f.w1((w_lo, w_hi)[part], sub, fc),
                                           lambda part: (in_lo, in_hi)[part][:, at, tokens], True, True)
                        if f.gated:
                            m = split_products(bank[3 + at_bank][:, :],
                                               lambda part: f.up((w_lo, w_hi)[part], sub, fc),
                                               lambda part: (in_lo, in_hi)[part][:, at, tokens],
                                               True, True)
                        m.then_inc(h_done, 1)

                def output(i, n):
                    sub, half = n // 2, n % 2
                    if half == 0:
                        pe.wait_ge(w_out_loaded[sub], 16)
                        pe.sem_inc(w_out_loaded[sub], -16)
                    pe.wait_ge(h_ready, f.FC)
                    pe.sem_inc(h_ready, -f.FC)
                    pe.wait_ge(y_free, 1)
                    pe.sem_inc(y_free, -1)
                    for t in range(4):
                        tokens = slice(t * P, (t + 1) * P)
                        for fc in range(f.FC):
                            m = mm(b4(f.output_bank(n))[:, t, :], hT[:, half, fc, tokens], f.w2(sub, fc),
                                   start=(fc == 0), stop=(fc == f.FC - 1))
                    m.then_inc(y_done, 1)

                y_banks = 2 if f.gated else 4
                for _ in range(y_banks):
                    pe.sem_inc(y_free, 1)
                between = {1: lambda: turn_weights(f.E), 2: lambda: bias_products(b2, f.E)} if b2 else {}
                halves(pe, [(hidden, range(4), 0), (output, range(4), 1)], f, lambda: None, between)
                pe.wait_ge(y_free, y_banks)
                pe.sem_inc(y_free, -y_banks)

            pe.wait_ge(consts_pe, 1)
            pe.sem_inc(consts_pe, -1)
            pe.wait_ge(sq_loaded, 16)
            pe.wait_ge(ctx_loaded, 16)

            project(w("wk0"), ctxT, 2)
            project_tok(w("wv0"), ctxT, 4)
            transpose_tiles(xn, norm_tok_ready)
            pe.wait_ge(feat_ready, 1)
            pe.sem_inc(feat_ready, -1)
            project(w("wq0"), xnT, 6)
            pe.wait_ge(qkv_ready, 1)
            pe.sem_inc(qkv_ready, -1)
            narrow_attention(False)
            attention_output(w("wo0"))
            transpose_tiles(xn, norm_tok_ready)
            pe.wait_ge(feat_ready, 1)
            pe.sem_inc(feat_ready, -1)
            route(w("r0"), E0, xnT)
            transpose_tiles(att, norm_tok_ready)
            pe.wait_ge(feat_ready, 1)
            pe.sem_inc(feat_ready, -1)
            ffn(ffn0, b2_0)

            pe.wait_ge(sq_rest_loaded, 16)
            project(w("wk1"), ctxT, 2)
            project_tok(w("wv1"), ctxT, 4)
            transpose_tiles(xn, norm_tok_ready)
            pe.wait_ge(feat_ready, 1)
            pe.sem_inc(feat_ready, -1)
            pe.wait_ge(qkv_ready, 1)
            pe.sem_inc(qkv_ready, -1)
            project(w("wk1"), xnT, 2)
            project_tok(w("wv1"), xnT, 4)
            pe.wait_ge(qkv_ready, 1)
            pe.sem_inc(qkv_ready, -1)
            pe.wait_ge(w1_attn_loaded, 32)
            wide_attention()
            transpose_tiles(iv, norm_tok_ready)
            pe.wait_ge(feat_ready, 1)
            pe.sem_inc(feat_ready, -1)
            ffn(mlp1)
            transpose_tiles(xn, norm_tok_ready)
            pe.wait_ge(feat_ready, 1)
            pe.sem_inc(feat_ready, -1)
            route(w("r1"), E1, xnT)
            ffn(ffn1, b2_1)

            project(w("wk2"), ctxT, 2)
            project_tok(w("wv2"), ctxT, 4)
            transpose_tiles(xn, norm_tok_ready)
            pe.wait_ge(feat_ready, 1)
            pe.sem_inc(feat_ready, -1)
            project(w("wq2"), xnT, 6)
            pe.wait_ge(qkv_ready, 1)
            pe.sem_inc(qkv_ready, -1)
            narrow_attention(True)
            attention_output(w("wo2"))
            transpose_tiles(xn, norm_tok_ready)
            pe.wait_ge(feat_ready, 1)
            pe.sem_inc(feat_ready, -1)
            route(w("r2"), E2, xnT)
            ffn(ffn2)

            transpose_tiles(xn, norm_tok_ready)
            pe.wait_ge(feat_ready, 1)
            pe.sem_inc(feat_ready, -1)
            pe.wait_ge(x3_sim, 1)
            pe.sem_inc(x3_sim, -1)
            for b in range(NB):
                m = mm(b4(b // 4)[:, b % 4, :], qT[:, b * P:(b + 1) * P], ctxT[:, b * P:(b + 1) * P])
                if b % 4 == 3:
                    m.then_inc(x3_sims, 1)
            for b in range(NB):
                m = mm(bank[2][:, b:b + 1], xnT[:, b * P:(b + 1) * P], col("w1s"))
            m.then_inc(x3_own, 1)
            pe.wait_ge(ctx_tok_loaded, 16)
            for g in range(2):
                pe.wait_ge(x3_prob, 1)
                pe.sem_inc(x3_prob, -1)
                for i in range(4):
                    t = pe.transpose(b4(4 + g)[:, i, :], prob[:, 0, 4 * g + i, :], ident[:, :])
                t.then_inc(x3_t, 1)
            pe.wait_ge(x3_m, 1)
            pe.sem_inc(x3_m, -1)
            pe.transpose(bank[3][0:NB, 0:P], m_sim[:, :], ident[:, :]).then_inc(x3_mT, 1)

            def project_features(banks, features):
                for b in range(NB):
                    t = slice(b * P, (b + 1) * P)
                    for i in features:
                        m = mm(b4(banks + b // 4)[:, b % 4, :], feats[i][:, t], w("wqv", i * D, D),
                               start=(i == features[0]), stop=(i == features[-1]))
                    if b % 4 == 3:
                        m.then_inc(x3_out, 1)

            feats = (xnT, kT, normed[:, 0, :], normed[:, 1, :])
            project_features(0, [0])
            for g in range(2):
                pe.wait_ge(x3_te, 1)
                pe.sem_inc(x3_te, -1)
                for i in range(4):
                    m = mm(b4(6 + g)[:, i, :], ctx_tok[:, 4 * g + i, :], probT[:, 0, 4 * g + i, :])
                m.then_inc(x3_pv, 1)
            pe.wait_ge(x3_b, 1)
            pe.sem_inc(x3_b, -1)
            pe.transpose(bank[3][:, 256:256 + NB], batt[:, :], ident[0:NB, 0:NB]).then_inc(x3_bT, 1)
            pe.wait_ge(x3_bTe, 1)
            pe.sem_inc(x3_bTe, -1)
            for b in range(NB):
                m = mm(bank[2][:, 16 + b:17 + b], xn[:, b, :], batt_col[:, b:b + 1])
            m.then_inc(x3_hc, 1)
            pe.wait_ge(x3_feats, 1)
            pe.sem_inc(x3_feats, -1)
            project_features(4, [1, 2, 3])

            transpose_tiles(xn, norm_tok_ready)
            pe.wait_ge(feat_ready, 1)
            pe.sem_inc(feat_ready, -1)
            ffn(ffn3)

        @block.vector
        def _(dve):
            st = Steps(dve, dve_steps)

            def norm_stats(half, src, eps):
                batches = range(4 * half, 4 * half + 4)
                four = slice(4 * half, 4 * half + 4)
                dve.wait_ge(st.sem, st.n)
                for b in batches:
                    dve.bn_stats(stats[:, b, :], src[:, b, :]).then_inc(st.sem, st.one())
                dve.wait_ge(st.sem, st.n)
                for b in batches:
                    dve.bn_aggr(mean_var[:, b, :], stats[:, b, :]).then_inc(st.sem, st.one())
                dve.wait_ge(st.sem, st.n)
                dve.tensor_scalar(var_eps[:, four], mean_var[:, four, 1], eps, None, ALU.add)\
                    .then_inc(st.sem, st.one())
                dve.wait_ge(st.sem, st.n)
                dve.sem_inc(var_ready, 1)

            def norm_apply(half, src, dst, give=None, gamma=None, shift=None):
                batches = range(4 * half, 4 * half + 4)
                if gamma:
                    for b in batches:
                        dve.scalar_tensor_tensor(src[:, b, :], src[:, b, :], mean_var[:, b, 0:1],
                                                 row(gamma), ALU.subtract, ALU.mult)\
                            .then_inc(st.sem, st.one())
                    dve.wait_ge(st.sem, st.n)
                dve.wait_ge(rstd_ready, 1)
                dve.sem_inc(rstd_ready, -1)
                for b in batches:
                    if gamma:
                        dve.scalar_tensor_tensor(dst[:, b, :], src[:, b, :], rstd[:, b:b + 1], shift(b),
                                                 ALU.mult, ALU.add).then_inc(st.sem, st.one())
                    else:
                        dve.tensor_scalar(dst[:, b, :], src[:, b, :], mean_var[:, b, 0:1], rstd[:, b:b + 1],
                                          ALU.subtract, ALU.mult).then_inc(st.sem, st.one())
                dve.wait_ge(st.sem, st.n)
                if give:
                    dve.sem_inc(give, 1)

            def norm_half(half, src, dst, eps, *args):
                norm_stats(half, src, eps)
                norm_apply(half, src, dst, *args)

            def norm_x():
                for half in range(2):
                    norm_stats(half, x, 1e-5)
                for half in range(2):
                    norm_apply(half, x, xn, norm_tok_ready)

            def next_norm():
                norm_half(0, x, xn, 1e-5, norm_tok_ready)

            def add_row_to_x(name):
                dve.tensor_tensor(x[:, :, :], x[:, :, :], row_b(name), ALU.add).then_inc(st.sem, st.one())
                dve.wait_ge(st.sem, st.n)

            def x_of(b):
                return x[:, b, :]

            def copy_projected(dst, at, bias, scale):
                for half in range(2):
                    dve.wait_ge(projected, 1)
                    dve.sem_inc(projected, -1)
                    dve.tensor_scalar(dst[:, half * 512:(half + 1) * 512], bank[at + half][:, :],
                                      col(bias), scale, ALU.add, ALU.mult).then_inc(st.sem, st.one())

            def split_keys():
                dve.wait_ge(st.sem, st.n)
                dve.tensor_copy(in_hi[:, 0, :], kT[:, :]).then_inc(st.sem, st.one())
                dve.wait_ge(st.sem, st.n)
                dve.tensor_tensor(in_lo[:, 0, :], kT[:, :], in_hi[:, 0, :], ALU.subtract)\
                    .then_inc(st.sem, st.one())

            def copy_values(dst, at, bias):
                for half in range(2):
                    dve.wait_ge(projected, 1)
                    dve.sem_inc(projected, -1)
                    dve.tensor_tensor(dst[:, 4 * half:4 * half + 4, :], b4(at + half),
                                      row(bias)[:, None, :].broadcast_to([P, 4, D]), ALU.add)\
                        .then_inc(st.sem, st.one())

            def narrow_attention(prune):
                def maxima(it, n):
                    dve.wait_ge(scores_done, 1)
                    dve.sem_inc(scores_done, -1)
                    if n % 4 == 3:
                        dve.sem_inc(qk_free, 1)
                    dve.tensor_reduce(neg_max[:, n, :], b4(n % 2), X_AX, ALU.max, negate=True)\
                        .then_inc(neg_max_ready, 1)

                def inverse_sums(it, n):
                    dve.wait_ge(exps_done, 1)
                    dve.sem_inc(exps_done, -1)
                    h = slice(4 * (n % 4), 4 * (n % 4) + 4)
                    dve.reciprocal(r[:, n // 4, h], z[:, n // 4, h]).then_inc(st.sem, st.one())
                    dve.wait_ge(st.sem, st.n)
                    dve.sem_inc(inverse_ready, 1)

                def copy_probsT(it, n):
                    dve.wait_ge(probsT_done, 1)
                    dve.sem_inc(probsT_done, -1)
                    h = 4 * (n % 4)
                    dve.tensor_copy(probT[:, n // 4, h:h + 4, :], b4(2 + n % 2)).then_inc(st.sem, st.one())
                    dve.wait_ge(st.sem, st.n)
                    dve.sem_inc(probsT_ready, 1)
                    dve.sem_inc(turn_free, 1)

                def copy_out(it, n):
                    dve.wait_ge(out_done, 1)
                    dve.sem_inc(out_done, -1)
                    if not prune:
                        dve.sem_inc(v_free, 1)
                    dve.tensor_copy(attT[:, bass.ds((2 * it + n // 4) * P, P)], bank[6 + n // 4][:, 0:P])\
                        .then_inc(st.sem, st.one())
                    dve.wait_ge(st.sem, st.n)
                    dve.sem_inc(out_free, 1)

                def column_sums(it, n):
                    dve.wait_ge(probsT_copied, 1)
                    dve.sem_inc(probsT_copied, -1)
                    h = slice(4 * (n % 4), 4 * (n % 4) + 4)
                    dve.tensor_reduce(col_sum[:, n // 4, h], probT[:, n // 4, h, :], X_AX, ALU.add)\
                        .then_inc(st.sem, st.one())
                    if n % 4 == 3:
                        dve.wait_ge(st.sem, st.n)
                        dve.sem_inc(colsum_ready, 1)

                def rank(it, n):
                    dve.wait_ge(ranked_done, 1)
                    dve.sem_inc(ranked_done, -1)
                    dve.tensor_scalar(ranked[:, 0:P], bank[5][0:H, P - 1::-1][:, 0:P], -1.0, None,
                                      ALU.mult).then_inc(st.sem, st.one())
                    dve.memset(ranked[:, P:P + 8], PAD).then_inc(st.sem, st.one())
                    dve.wait_ge(st.sem, st.n)
                    dve.max(top[:, 0, :], ranked[:, :]).then_inc(st.sem, st.one())
                    dve.wait_ge(st.sem, st.n)
                    dve.match_replace(ranked[:, :], top[:, 0, :], ranked[:, :], GONE)\
                        .then_inc(st.sem, st.one())
                    dve.wait_ge(st.sem, st.n)
                    dve.max(top[:, 1, :], ranked[:, :]).then_inc(st.sem, st.one())
                    dve.wait_ge(st.sem, st.n)
                    dve.memset(top[:, 1, DROP - 8:8], PAD).then_inc(st.sem, st.one())
                    dve.wait_ge(st.sem, st.n)
                    dve.match_replace(ranked[:, :], top[:, 1, :], ranked[:, :], GONE)\
                        .then_inc(st.sem, st.one())
                    dve.wait_ge(st.sem, st.n)
                    dve.tensor_scalar(kept[:, :], ranked[:, P - 1::-1][:, 0:P], PAD, None, ALU.is_gt)\
                        .then_inc(st.sem, st.one())
                    dve.wait_ge(st.sem, st.n)
                    dve.sem_inc(kept_ready, 1)

                def keep_values(it, n):
                    dve.wait_ge(keptT_done, 1)
                    dve.sem_inc(keptT_done, -1)
                    dve.wait_ge(v_ready, 1)
                    dve.sem_inc(v_ready, -1)
                    dve.tensor_tensor(v_kept[:, n // 4, :, :], v_wide[:, n // 4, :, :],
                                      bank[5][:, 256:256 + H][:, :, None].broadcast_to([P, H, 32]), ALU.mult)\
                        .then_inc(st.sem, st.one())
                    dve.wait_ge(st.sem, st.n)
                    dve.sem_inc(v_kept_ready, 1)
                    dve.sem_inc(v_free, 1)

                if prune:
                    order = [(maxima, range(8), 0), (inverse_sums, range(8), 1), (rank, (3, 7), 5),
                             (keep_values, (3, 7), 6), (column_sums, range(8), 4), (copy_out, (3, 7), 8)]
                else:
                    order = [(maxima, range(8), 0), (inverse_sums, range(8), 1), (copy_out, (3, 7), 5),
                             (copy_probsT, range(8), 3)]
                st.close()
                pipelined(dve, order, 8, NB // 2, st.close)
                dve.sem_inc(att_ready, 1)

            def attention_output(bias):
                dve.tensor_tensor(x[:, :, :], x[:, :, :], row_b(bias), ALU.add).then_inc(st.sem, st.one())
                dve.wait_ge(st.sem, st.n)
                for half in range(2):
                    dve.wait_ge(y_attn_done, 1)
                    dve.sem_inc(y_attn_done, -1)
                    part = x[:, 4 * half:4 * half + 4, :]
                    dve.tensor_tensor(part, part, b4(2 + half), ALU.add).then_inc(st.sem, st.one())
                    norm_stats(half, x, 1e-5)

            def mlp_norm(half):
                norm_half(half, att, xm, 1e-6, norm_tok_ready, "g1", lambda b: row("be1"))

            def wide_attention():
                def queries(it, n):
                    dve.wait_ge(heads_q_done, 1)
                    dve.sem_inc(heads_q_done, -1)
                    at = COLS["bq1"][0] + 4 * (n % 4)
                    dve.tensor_tensor(qh[:, n % 2, :, :], b4(0),
                                      cols[:, at:at + 4][:, :, None].broadcast_to([P, 4, P]), ALU.add)\
                        .then_inc(st.sem, st.one())
                    dve.wait_ge(st.sem, st.n)
                    dve.sem_inc(qh_ready, 1)
                    dve.sem_inc(qh_ready_pool, 1)
                    dve.sem_inc(q_free, 1)

                def maxima(it, n):
                    dve.wait_ge(scores_done, 1)
                    dve.sem_inc(scores_done, -1)
                    own = bank[7][:, 4 * (n % 2):4 * (n % 2) + 4]
                    m = row_max[:, n % 2, :]
                    dve.tensor_reduce(m, b4(1 + n % 2), X_AX, ALU.max).then_inc(st.sem, st.one())
                    dve.wait_ge(st.sem, st.n)
                    dve.tensor_tensor(m, m, own, ALU.max).then_inc(st.sem, st.one())
                    dve.wait_ge(st.sem, st.n)
                    dve.tensor_scalar(neg_max[:, n, :], m, -SC1, None, ALU.mult).then_inc(st.sem, st.one())
                    dve.wait_ge(st.sem, st.n)
                    dve.scalar_tensor_tensor(self_arg[:, n % 2, :], own, SC1, neg_max[:, n, :],
                                             ALU.mult, ALU.add).then_inc(st.sem, st.one())
                    dve.wait_ge(st.sem, st.n)
                    dve.sem_inc(neg_max_ready, 1)
                    dve.sem_inc(own_free, 1)

                def weights(it, n):
                    dve.wait_ge(probs_ready_dve, 1)
                    dve.sem_inc(probs_ready_dve, -1)
                    four = slice(4 * (n % 2), 4 * (n % 2) + 4)
                    total, inv = z[:, 1, four], r[:, 0, 4 * (n % 4):4 * (n % 4) + 4]
                    dve.tensor_tensor(total, z[:, 0, four], self_exp[:, n % 2, :], ALU.add)\
                        .then_inc(st.sem, st.one())
                    dve.wait_ge(st.sem, st.n)
                    dve.reciprocal(inv, total).then_inc(st.sem, st.one())
                    dve.wait_ge(st.sem, st.n)
                    dve.tensor_tensor(self_w[:, n % 2, :], self_exp[:, n % 2, :], inv, ALU.mult)\
                        .then_inc(st.sem, st.one())
                    dve.wait_ge(st.sem, st.n)
                    dve.sem_inc(self_w_ready, 1)

                def heads_out(it, n):
                    dve.wait_ge(pv_done, 1)
                    dve.sem_inc(pv_done, -1)
                    dve.wait_ge(mva_ready, 1)
                    dve.sem_inc(mva_ready, -1)
                    for i in range(4):
                        dve.scalar_tensor_tensor(heads[:, n % 2, i, :], b4(4)[:, i, :],
                                                 r[:, 0, 4 * (n % 4) + i:4 * (n % 4) + i + 1],
                                                 mva[:, n % 2, i, :], ALU.mult, ALU.add)\
                            .then_inc(st.sem, st.one())
                    dve.wait_ge(st.sem, st.n)
                    dve.sem_inc(heads_ready, 1)

                def residual(it, n):
                    if isinstance(it, int) and (it, n) == (NB // 2 - 1, 7):
                        mlp_norm(0)
                    dve.wait_ge(wo_done, 1)
                    dve.sem_inc(wo_done, -1)
                    b = bass.ds(2 * it + n // 4, 1)
                    dve.tensor_tensor(att[:, b, :], xn[:, b, :], bank[6][:, 0:D][:, None, :], ALU.add)\
                        .then_inc(st.sem, st.one())
                    dve.wait_ge(st.sem, st.n)
                    dve.sem_inc(wo_free, 1)

                st.close()
                pipelined(dve, [(residual, (3, 7), 6), (heads_out, range(8), 4), (queries, range(8), 0),
                                (weights, range(8), 2), (maxima, range(8), 1)], 8, NB // 2, st.close)

            def route(experts, biases, give=()):
                dve.wait_ge(router_done, 1)
                dve.sem_inc(router_done, -1)
                lg = logits[:, :, 0:experts]
                dve.tensor_copy(lg, bank[7][:, 0:NB * experts].rearrange("p (b e) -> p b e", b=NB))\
                    .then_inc(st.sem, st.one())
                for bias in biases:
                    dve.wait_ge(st.sem, st.n)
                    dve.tensor_tensor(lg, lg, row(bias)[:, None, :].broadcast_to([P, NB, experts]), ALU.add)\
                        .then_inc(st.sem, st.one())
                dve.wait_ge(st.sem, st.n)
                for b in range(NB):
                    dve.max(best[:, b, :], logits[:, b, 0:experts]).then_inc(st.sem, st.one())
                dve.wait_ge(st.sem, st.n)
                dve.tensor_tensor(gap[:, :], best[:, :, 1], best[:, :, 0], ALU.subtract)\
                    .then_inc(st.sem, st.one())
                dve.wait_ge(st.sem, st.n)
                dve.sem_inc(gap_ready, 1)
                for b in range(NB):
                    dve.max_index(best_at[:, b, :], best[:, b, :], logits[:, b, 0:experts])\
                        .then_inc(st.sem, st.one())
                dve.wait_ge(st.sem, st.n)
                dve.tensor_copy(best_no[:, :, :], best_at[:, :, 0:2]).then_inc(st.sem, st.one())
                dve.wait_ge(gap_exp_ready, 1)
                dve.sem_inc(gap_exp_ready, -1)
                dve.tensor_scalar(w_a[:, :], gap_exp[:, :], 1.0, None, ALU.add).then_inc(st.sem, st.one())
                dve.wait_ge(st.sem, st.n)
                dve.reciprocal(w_a[:, :], w_a[:, :]).then_inc(st.sem, st.one())
                dve.wait_ge(st.sem, st.n)
                dve.tensor_tensor(w_b[:, :], w_a[:, :], gap_exp[:, :], ALU.mult).then_inc(st.sem, st.one())
                full = [P, NB, experts]
                number = expert_no[:, 0:experts][:, None, :].broadcast_to(full)
                for o, i, weight in ((cw, 0, w_a), (cw_b, 1, w_b)):
                    dve.wait_ge(st.sem, st.n)
                    dve.tensor_tensor(o[:, :, 0:experts], number,
                                      best_no[:, :, i:i + 1].broadcast_to(full), ALU.is_equal)\
                        .then_inc(st.sem, st.one())
                    dve.wait_ge(st.sem, st.n)
                    dve.tensor_tensor(o[:, :, 0:experts], o[:, :, 0:experts],
                                      weight[:, :, None].broadcast_to(full), ALU.mult)\
                        .then_inc(st.sem, st.one())
                dve.wait_ge(st.sem, st.n)
                dve.tensor_tensor(cw[:, :, 0:experts], cw[:, :, 0:experts], cw_b[:, :, 0:experts], ALU.add)\
                    .then_inc(st.sem, st.one())
                dve.wait_ge(st.sem, st.n)
                for token in give:
                    dve.sem_inc(token, 1)

            def copy_weights(experts):
                dve.wait_ge(cwT_done, 1)
                dve.sem_inc(cwT_done, -1)
                for half in range(2):
                    dve.tensor_copy(cwT[0:experts, half * 512:(half + 1) * 512],
                                    bank[6 + half][0:experts, :]).then_inc(st.sem, st.one())
                dve.wait_ge(st.sem, st.n)
                dve.sem_inc(cwT_ready, 1)

            def add_biases():
                dve.wait_ge(bias_done, 1)
                dve.sem_inc(bias_done, -1)
                for half in range(2):
                    part = x[:, 4 * half:4 * half + 4, :]
                    dve.tensor_tensor(part, part, b4(6 + half), ALU.add).then_inc(st.sem, st.one())
                dve.wait_ge(st.sem, st.n)
                dve.sem_inc(bias_free, 1)

            def split_input():
                for half in range(2):
                    tokens = slice(half * 512, (half + 1) * 512)
                    dve.wait_ge(input_hi_ready, 1)
                    dve.sem_inc(input_hi_ready, -1)
                    dve.tensor_tensor(in_lo[:, 0, tokens], xnT[:, tokens], in_hi[:, 0, tokens],
                                      ALU.subtract).then_inc(input_ready, 1)

            def scaled_input(e, sub):
                for half in range(2):
                    tokens = slice(half * 512, (half + 1) * 512)
                    for part in (in_hi, normed):
                        dve.tensor_scalar(part[:, sub, tokens], kT[:, tokens], col("gamma0", e),
                                          col("beta0", e), ALU.mult, ALU.add).then_inc(st.sem, st.one())
                    dve.wait_ge(st.sem, st.n)
                    dve.tensor_tensor(in_lo[:, sub, tokens], normed[:, sub, tokens],
                                      in_hi[:, sub, tokens], ALU.subtract).then_inc(input_ready, 1)

            def ffn(f, finish, between={}, before_last=None):
                def gate(i, n):
                    half = n % 2
                    for fc in range(f.FC):
                        dve.wait_ge(g_done, 1)
                        dve.sem_inc(g_done, -1)
                        h, up = hT[:, half, fc, :], bank[3 + f.hidden_bank(n, fc)][:, :]
                        if f.up_bias:
                            dve.scalar_tensor_tensor(h, up, col(f.up_bias, fc), h, ALU.add, ALU.mult)\
                                .then_inc(h_ready, 1)
                        else:
                            dve.tensor_tensor(h, up, h, ALU.mult).then_inc(h_ready, 1)

                def next_input(i, n):
                    scaled_input(2 * i + n // 2 + 1, 1 - n // 2)

                def output(i, n):
                    dve.wait_ge(y_done, 1)
                    dve.sem_inc(y_done, -1)
                    if n % 2 == 1:
                        dve.sem_inc(w_out_free[n // 2], 1)
                    finish(2 * i + n // 2, n, b4(f.output_bank(n)))
                    dve.wait_ge(st.sem, st.n)
                    dve.sem_inc(y_free, 1)

                order = [(output, range(4), 1)]
                if f is ffn0:
                    order.insert(0, (next_input, (0, 2), 0))
                if f.gated:
                    order.insert(0, (gate, range(4), 0))
                st.close()
                halves(dve, order, f, st.close, between, before_last)

            def combine(e, n, ps):
                for t in range(4):
                    b = 4 * (n % 2) + t
                    dve.scalar_tensor_tensor(x[:, b, :], ps[:, t, :], cw[:, b, bass.ds(e, 1)],
                                             x[:, b, :], ALU.mult, ALU.add).then_inc(st.sem, st.one())

            def residual_into(dst):
                def finish(e, n, ps):
                    part = dst[:, 4 * n:4 * n + 4, :]
                    dve.tensor_tensor(part, part, ps, ALU.add).then_inc(st.sem, st.one())
                return finish

            dve.wait_ge(x_loaded, 16)
            dve.wait_ge(consts_dve, 1)
            dve.sem_inc(consts_dve, -1)

            norm_x()
            dve.wait_ge(cols_loaded, 16)
            dve.wait_ge(rows_loaded, 16)
            copy_projected(kT, 2, "bk0", 1.0)
            copy_values(iv, 4, "bv0")
            split_keys()
            dve.wait_ge(st.sem, st.n)
            dve.sem_inc(qkv_ready_pool, 1)
            copy_projected(qT, 6, "bq0", SC0)
            dve.wait_ge(st.sem, st.n)
            dve.sem_inc(qkv_ready, 1)
            dve.sem_inc(qkv_ready_pool, 1)
            narrow_attention(False)
            attention_output("bo0")
            for half in range(2):
                norm_apply(half, x, xn, norm_tok_ready)
                norm_stats(half, xn, 1e-6)
            for half in range(2):
                norm_apply(half, xn, att, norm_tok_ready)
            dve.wait_ge(feat_ready_dve, 1)
            dve.sem_inc(feat_ready_dve, -1)
            scaled_input(0, 0)

            def weights0():
                route(E0, [], give=[cw_ready])
                dve.tensor_tensor(cw_sum[:, :], w_a[:, :], w_b[:, :], ALU.add).then_inc(st.sem, st.one())
                dve.wait_ge(st.sem, st.n)
                for b in range(NB):
                    dve.scalar_tensor_tensor(x[:, b, :], xn[:, b, :], cw_sum[:, b:b + 1], x[:, b, :],
                                             ALU.mult, ALU.add).then_inc(st.sem, st.one())
                dve.wait_ge(st.sem, st.n)

            ffn(ffn0, combine, {0: weights0, 1: lambda: copy_weights(E0), 2: add_biases}, next_norm)
            dve.wait_ge(input_ready, 2)
            dve.sem_inc(input_ready, -2)

            norm_half(1, x, xn, 1e-5, norm_tok_ready)
            copy_projected(kT, 2, "bk1", 1.0)
            copy_values(iv, 4, "bv1")
            dve.wait_ge(st.sem, st.n)
            dve.sem_inc(qkv_ready, 1)
            copy_projected(qT, 2, "bk1", 1.0)
            copy_values(mv, 4, "bv1")
            dve.wait_ge(st.sem, st.n)
            dve.sem_inc(qkv_ready, 1)
            dve.tensor_tensor(xn[:, :, :], xn[:, :, :], row_b("bo1"), ALU.add).then_inc(st.sem, st.one())
            wide_attention()
            mlp_norm(1)
            split_input()
            add_row_to_x("be2")
            dve.tensor_tensor(mv[:, :, :], xm[:, :, :], row_b("bm1"), ALU.add).then_inc(st.sem, st.one())
            dve.wait_ge(st.sem, st.n)

            def block_norm(half):
                norm_half(half, mv, x, 1e-6, None, "g2", x_of)
                norm_half(half, x, xn, 1e-5, norm_tok_ready)

            ffn(mlp1, residual_into(mv), {}, lambda: block_norm(0))
            block_norm(1)
            split_input()
            ffn(ffn1, combine, {0: lambda: route(E1, ["rbg", "rbias"], give=[cw_ready]),
                                1: lambda: copy_weights(E1), 2: add_biases}, next_norm)

            norm_half(1, x, xn, 1e-5, norm_tok_ready)
            copy_projected(kT, 2, "bk2", 1.0)
            copy_values(iv, 4, "bv2")
            split_keys()
            dve.wait_ge(st.sem, st.n)
            dve.sem_inc(qkv_ready_pool, 1)
            copy_projected(qT, 6, "bq2", SC0)
            dve.wait_ge(st.sem, st.n)
            dve.sem_inc(qkv_ready, 1)
            dve.sem_inc(qkv_ready_pool, 1)
            narrow_attention(True)
            attention_output("bo2")
            for half in range(2):
                norm_apply(half, x, xn, norm_tok_ready)
            split_input()
            ffn(ffn2, combine, {0: lambda: route(E2, [])}, next_norm)

            def add_features(banks):
                dve.wait_ge(st.sem, st.n)
                for half in range(2):
                    dve.wait_ge(x3_out, 1)
                    dve.sem_inc(x3_out, -1)
                    part = x[:, 4 * half:4 * half + 4, :]
                    dve.tensor_tensor(part, part, b4(banks + half), ALU.add).then_inc(st.sem, st.one())
                    if banks == 4:
                        norm_stats(half, x, 1e-5)

            norm_half(1, x, xn, 1e-5, norm_tok_ready)
            dve.wait_ge(feat_ready_dve, 1)
            dve.sem_inc(feat_ready_dve, -1)
            dve.tensor_scalar(qT[:, :], xnT[:, :], col("w3s"), col("w2s"), ALU.mult, ALU.add)\
                .then_inc(st.sem, st.one())
            dve.wait_ge(st.sem, st.n)
            dve.sem_inc(x3_sim, 1)
            add_row_to_x("bqv")
            for g in range(2):
                dve.wait_ge(x3_sims, 1)
                dve.sem_inc(x3_sims, -1)
                four = slice(4 * g, 4 * g + 4)
                dve.tensor_reduce(m_sim[:, four], b4(g), X_AX, ALU.max).then_inc(st.sem, st.one())
                dve.wait_ge(st.sem, st.n)
                dve.tensor_scalar(neg_max[:, g, :], m_sim[:, four], -1.0, None, ALU.mult)\
                    .then_inc(st.sem, st.one())
                dve.wait_ge(st.sem, st.n)
                dve.sem_inc(x3_neg, 1)
            for g in range(2):
                dve.wait_ge(x3_exp, 1)
                dve.sem_inc(x3_exp, -1)
                four = slice(4 * g, 4 * g + 4)
                dve.reciprocal(r[:, 0, four], z[:, 0, four]).then_inc(st.sem, st.one())
                dve.wait_ge(st.sem, st.n)
                dve.tensor_tensor(prob[:, 0, four, :], prob[:, 0, four, :],
                                  r[:, 0, four][:, :, None].broadcast_to([P, 4, P]), ALU.mult)\
                    .then_inc(x3_prob, 1)
            dve.wait_ge(x3_own, 1)
            dve.sem_inc(x3_own, -1)
            dve.tensor_tensor(m_sim[:, :], m_sim[:, :], bank[2][:, 0:NB], ALU.add)\
                .then_inc(st.sem, st.one())
            dve.wait_ge(st.sem, st.n)
            dve.tensor_scalar(m_sim[:, :], m_sim[:, :], row("bsim"), None, ALU.add)\
                .then_inc(st.sem, st.one())
            dve.wait_ge(st.sem, st.n)
            dve.sem_inc(x3_m, 1)
            dve.wait_ge(x3_mT, 1)
            dve.sem_inc(x3_mT, -1)
            dve.tensor_copy(batt[:, :], bank[3][0:NB, 0:P]).then_inc(st.sem, st.one())
            dve.wait_ge(st.sem, st.n)
            dve.tensor_reduce(bstat[:, 0:1], batt[:, :], X_AX, ALU.max, negate=True)\
                .then_inc(st.sem, st.one())
            dve.wait_ge(st.sem, st.n)
            dve.sem_inc(x3_arg, 1)
            for g in range(2):
                dve.wait_ge(x3_t, 1)
                dve.sem_inc(x3_t, -1)
                dve.tensor_copy(probT[:, 0, 4 * g:4 * g + 4, :], b4(4 + g)).then_inc(st.sem, st.one())
                dve.wait_ge(st.sem, st.n)
                dve.sem_inc(x3_te, 1)
            dve.wait_ge(x3_bexp, 1)
            dve.sem_inc(x3_bexp, -1)
            dve.reciprocal(bstat[:, 2:3], bstat[:, 1:2]).then_inc(st.sem, st.one())
            dve.wait_ge(st.sem, st.n)
            dve.tensor_scalar(batt[:, :], batt2[:, :], bstat[:, 2:3], None, ALU.mult)\
                .then_inc(st.sem, st.one())
            dve.wait_ge(st.sem, st.n)
            dve.sem_inc(x3_b, 1)
            dve.wait_ge(x3_bT, 1)
            dve.sem_inc(x3_bT, -1)
            dve.tensor_copy(batt_col[:, :], bank[3][:, 256:256 + NB]).then_inc(st.sem, st.one())
            dve.wait_ge(st.sem, st.n)
            dve.sem_inc(x3_bTe, 1)
            for g in range(2):
                dve.wait_ge(x3_pv, 1)
                dve.sem_inc(x3_pv, -1)
                dve.tensor_copy(kT[:, g * 512:(g + 1) * 512], bank[6 + g][:, :]).then_inc(st.sem, st.one())
            dve.wait_ge(x3_hc, 1)
            dve.sem_inc(x3_hc, -1)
            dve.tensor_copy(hc_bar[:, :], bank[2][:, 16:16 + NB]).then_inc(st.sem, st.one())
            dve.wait_ge(st.sem, st.n)
            dve.tensor_tensor(normed[:, 0, :], xnT[:, :], kT[:, :], ALU.mult).then_inc(st.sem, st.one())
            dve.tensor_tensor(normed[:, 1, :].rearrange("p (b t) -> p b t", b=NB),
                              xnT[:, :].rearrange("p (b t) -> p b t", b=NB),
                              hc_bar[:, :, None].broadcast_to([D, NB, P]), ALU.mult)\
                .then_inc(st.sem, st.one())
            dve.wait_ge(st.sem, st.n)
            dve.sem_inc(x3_feats, 1)
            add_features(0)
            add_features(4)

            for half in range(2):
                norm_apply(half, x, xn, norm_tok_ready)
            split_input()
            dve.tensor_tensor(mv[:, :, :], xn[:, :, :], row_b("b2_3"), ALU.add).then_inc(st.sem, st.one())
            dve.wait_ge(st.sem, st.n)
            add_row_to_x("be3")

            def last_norm(half):
                norm_half(half, mv, x, 1e-5, result_ready, "g3", x_of)

            ffn(ffn3, residual_into(mv), {}, lambda: last_norm(0))
            last_norm(1)


def kernel(**inputs):
    import numpy as np
    import concourse.bacc as _bacc
    from concourse import mybir as _mybir
    from concourse.bass_utils import run_bass_kernel_spmd as _run

    g = {k: np.asarray(v) for k, v in inputs.items()}
    lay = np.ascontiguousarray

    def chunks(a):
        return a.reshape(-1, P).T

    def weights(a):
        e, k, m = a.shape
        return a.reshape(e, k // P, P, m).transpose(0, 2, 1, 3).reshape(e, P, -1)

    ws = g["L3_xattn_w_sim"]
    beta0 = g["L0_ffn_beta"]
    cols = np.concatenate([
        chunks(g["L0_xattn_wq_b"]), chunks(g["L0_xattn_wk_b"]), chunks(g["L0_ffn_gamma"]),
        chunks(beta0), chunks(beta0[0]), chunks(g["L0_ffn_b1"]), chunks(g["L1_xattn_bk"]),
        chunks(g["L1_xattn_bq"]), chunks(g["L1_xattn_bg"]), chunks(g["L1_xattn_bl"]), chunks(g["L1_ffn_b1"]),
        chunks(g["L2_xattn_bq"]), chunks(g["L2_xattn_bk"]), chunks(ws[:D]), chunks(ws[D:2 * D]),
        chunks(ws[2 * D:]), chunks(g["L3_ffn_b1"][0])], axis=1)
    rows = np.concatenate([g[n].reshape(-1) for n in (
        "L0_xattn_wv_b", "L0_xattn_wo_b", "L1_xattn_bv", "L1_xattn_bo", "L1_xattn_bm", "L1_xattn_g1",
        "L1_xattn_b1", "L1_xattn_g2", "L1_xattn_b2", "L2_xattn_bv", "L2_xattn_bo")] + [
        g["L3_ffn_b2"][0], g["L3_ffn_gamma"], g["L3_ffn_beta"], g["L3_xattn_b_qv"], g["L1_ffn_bg"],
        g["L1_ffn_bias"], g["L3_xattn_b_sim"]]).reshape(1, -1)
    sq = np.concatenate([
        g["L0_xattn_wq_w"].T, g["L0_xattn_wk_w"].T, g["L0_xattn_wv_w"].T, g["L0_xattn_wo_w"].T,
        g["L0_ffn_Wg"], g["L1_xattn_Wk"], g["L1_xattn_Wv"], g["L1_ffn_Wg"], g["L2_xattn_Wq"].T,
        g["L2_xattn_Wk"].T, g["L2_xattn_Wv"].T, g["L2_xattn_Wo"].T, g["L2_ffn_router_w"].T,
        weights(g["L3_xattn_W_qv"][None])[0]], axis=1)
    arrays = {
        "x_in": g["x"].transpose(1, 0, 2),
        "ctx_in": g["ctx_1024"].transpose(1, 0, 2),
        "ctxT_in": g["ctx_1024"].reshape(T, D).T,
        "cols_in": cols, "rows_in": rows, "sq_in": sq,
        "w0_in": np.concatenate([g["L0_ffn_W1"], weights(g["L0_ffn_W2"])], axis=2),
        "w1q_in": g["L1_xattn_Wq"].transpose(1, 0, 2),
        "w1o_in": g["L1_xattn_Wo"].reshape(H, D, D).transpose(1, 0, 2),
        "w1m_in": np.concatenate([g["L1_xattn_Wg"], g["L1_xattn_Wl"], weights(g["L1_xattn_Wm"][None])[0]], axis=1),
        "w1_in": np.concatenate([g["L1_ffn_W1"], weights(g["L1_ffn_W2"])], axis=2),
        "w2_in": np.concatenate([g["L2_ffn_w_gate"], g["L2_ffn_w_up"], weights(g["L2_ffn_w_down"])], axis=2),
        "w3_in": np.concatenate([g["L3_ffn_w1"][0], weights(g["L3_ffn_w2"][0:1])[0]], axis=1),
        "b2_0_in": g["L0_ffn_b2"], "b2_1_in": g["L1_ffn_b2"],
    }
    arrays = {k: lay(v) for k, v in arrays.items()}
    nc = _bacc.Bacc("TRN2", target_bir_lowering=False, num_devices=1)
    args = [nc.dram_tensor(k, v.shape, _mybir.dt.from_np(v.dtype), kind="ExternalInput").ap()
            for k, v in arrays.items()]
    out = nc.dram_tensor("out_dram", (P, NB, D), _mybir.dt.float32, kind="ExternalOutput").ap()
    build(nc, *args, out)
    result = _run(nc, [arrays], core_ids=[0])
    return result.results[0]["out_dram"].transpose(1, 0, 2)
```
